# Optimizing a Trainium2 kernel written in Bass

```python
import numpy as np
import jax
import jax.numpy as jnp

def _softmax(x, axis=-1):
    return jax.nn.softmax(x, axis=axis)

def _gelu(x):
    return jax.nn.gelu(x, approximate=True)

def _silu(x):
    return jax.nn.silu(x)

def _sigmoid(x):
    return jax.nn.sigmoid(x)

def _layernorm(x, axis=-1, eps=1e-05):
    m = jnp.mean(x, axis=axis, keepdims=True)
    v = jnp.var(x, axis=axis, keepdims=True)
    return (x - m) / jnp.sqrt(v + eps)

def _scatter_add(tgt, idx, src, axis=0):
    return tgt.at[idx].add(src)

def _segment_sum(src, seg, n):
    return jax.ops.segment_sum(src, seg, n)
kernel_name = 'mk_gps_d1_gnn_r8_adf645'

def setup_inputs(seed: int=0):
    np.random.seed(seed)
    _w = jnp.asarray

    def _rec_inputs():
        import jax
        import jax.numpy as jnp
        _gk = jax.random.key(seed)
        x = -0.0003713 + 1 * jax.random.normal(jax.random.fold_in(_gk, 1), (6250, 256), jnp.float32)
        _s = jax.random.randint(jax.random.fold_in(_gk, 2), (100000,), 0, 6250, jnp.int32)
        _d = jax.random.randint(jax.random.fold_in(_gk, 3), (100000,), 0, 6250, jnp.int32)
        _loop = jnp.arange(6250, dtype=jnp.int32)
        src = jnp.concatenate([_s, _d, _loop])
        dst = jnp.concatenate([_d, _s, _loop])
        _o = jnp.argsort(dst, stable=True)
        src = src[_o]
        dst = dst[_o]
        return (x, src, dst)
    x, src, dst = _rec_inputs()

    def _L0_gnn_setup():
        import jax, jax.numpy as jnp
        import numpy as np
        N, IN_DIM, OUT_DIM, HEADS, E = (6250, 256, 256, 4, 100000)
        HEAD_DIM = OUT_DIM // HEADS
        NEG_SLOPE = 0.2
        key = jax.random.key(seed)
        k = jax.random.split(key, 6)
        h = jax.random.normal(k[0], (N, IN_DIM), dtype=jnp.float32)
        edge_index = jax.random.randint(k[1], (2, E), 0, N, dtype=jnp.int32)
        W = jax.random.normal(k[2], (OUT_DIM, IN_DIM), dtype=jnp.float32) * (1.0 / np.sqrt(IN_DIM))
        b = jnp.zeros((OUT_DIM,), dtype=jnp.float32)
        a_src = jax.random.normal(k[3], (HEADS, HEAD_DIM), dtype=jnp.float32) * (1.0 / np.sqrt(HEAD_DIM))
        a_dst = jax.random.normal(k[4], (HEADS, HEAD_DIM), dtype=jnp.float32) * (1.0 / np.sqrt(HEAD_DIM))
        return {'h': h, 'edge_index': edge_index, 'W': W, 'b': b, 'a_src': a_src, 'a_dst': a_dst}
    _L0_gnn_all = _L0_gnn_setup()
    _L0_gnn_in = {k: v for k, v in _L0_gnn_all.items() if k in ('W', 'b', 'a_src', 'a_dst')}
    del _L0_gnn_all

    def _L0_mix_setup():
        import jax, jax.numpy as jnp
        import numpy as np
        D_MODEL = 256
        NUM_HEADS = 8
        DEPTH = D_MODEL // NUM_HEADS
        B, L = (32, 512)

        def _feature_map(x):
            return jax.nn.elu(x) + 1.0
        key = jax.random.key(seed)
        ks = jax.random.split(key, 9)
        sc = 1.0 / np.sqrt(D_MODEL)
        return {'x': jax.random.normal(ks[0], (B, L, D_MODEL), dtype=jnp.float32), 'wq': jax.random.normal(ks[1], (D_MODEL, D_MODEL), dtype=jnp.float32) * sc, 'bq': jnp.zeros((D_MODEL,), dtype=jnp.float32), 'wk': jax.random.normal(ks[2], (D_MODEL, D_MODEL), dtype=jnp.float32) * sc, 'bk': jnp.zeros((D_MODEL,), dtype=jnp.float32), 'wv': jax.random.normal(ks[3], (D_MODEL, D_MODEL), dtype=jnp.float32) * sc, 'bv': jnp.zeros((D_MODEL,), dtype=jnp.float32), 'wo': jax.random.normal(ks[4], (D_MODEL, D_MODEL), dtype=jnp.float32) * sc, 'bo': jnp.zeros((D_MODEL,), dtype=jnp.float32)}
    _L0_mix_all = _L0_mix_setup()
    _L0_mix_in = {k: v for k, v in _L0_mix_all.items() if k in ('wq', 'bq', 'wk', 'bk', 'wv', 'bv', 'wo', 'bo')}
    del _L0_mix_all

    def _L0_ffn_setup():
        import jax, jax.numpy as jnp
        import numpy as np
        B, N, D = (16, 512, 256)
        NUM_EXPERTS, TOP_K, HEADS = (4, 2, 4)
        N_EDGES = 131072
        LN_EPS = 1e-05

        def _layernorm(x, g, b):
            mu = x.mean(-1, keepdims=True)
            var = ((x - mu) ** 2).mean(-1, keepdims=True)
            return (x - mu) * jax.lax.rsqrt(var + LN_EPS) * g + b

        def _forward(x, edge_index, W_gat, att_src, att_dst, b_gat, ln_gamma, ln_beta, W1, b1, W2, b2):
            Bc, Nc, Dc = x.shape
            M = Bc * Nc
            x_flat = x.reshape(M, Dc)
            h = (x_flat @ W_gat).reshape(M, HEADS, NUM_EXPERTS)
            loops = jnp.arange(M, dtype=edge_index.dtype)
            src = jnp.concatenate([edge_index[0], loops])
            dst = jnp.concatenate([edge_index[1], loops])
            a_src = (h * att_src).sum(-1)
            a_dst = (h * att_dst).sum(-1)
            e = jax.nn.leaky_relu(a_src[src] + a_dst[dst], negative_slope=0.2)
            e_max = jax.ops.segment_max(e, dst, num_segments=M)
            ee = jnp.exp(e - e_max[dst])
            denom = jax.ops.segment_sum(ee, dst, num_segments=M)
            alpha = ee / (denom[dst] + 1e-16)
            msg = h[src] * alpha[:, :, None]
            agg = jax.ops.segment_sum(msg, dst, num_segments=M).reshape(M, HEADS * NUM_EXPERTS) + b_gat
            scores = _layernorm(agg, ln_gamma, ln_beta).reshape(M, HEADS, NUM_EXPERTS).mean(1)
            scores = scores.reshape(Bc, Nc, NUM_EXPERTS)
            topk_s, topk_i = jax.lax.top_k(scores, TOP_K)
            w = jax.nn.softmax(topk_s, axis=-1)
            out = jnp.zeros_like(x)
            for ei in range(NUM_EXPERTS):
                g = jnp.where(topk_i == ei, w, 0.0).sum(-1)
                hh = jax.nn.gelu(x @ W1[ei] + b1[ei], approximate=False)
                out = out + g[..., None] * (hh @ W2[ei] + b2[ei])
            return out
        key = jax.random.key(seed)
        ks = jax.random.split(key, 8)
        s = 0.05
        return {'x': jax.random.normal(ks[0], (B, N, D), jnp.float32), 'W_gat': jax.random.normal(ks[1], (D, HEADS * NUM_EXPERTS), jnp.float32) * s, 'att_src': jax.random.normal(ks[2], (HEADS, NUM_EXPERTS), jnp.float32) * s, 'att_dst': jax.random.normal(ks[3], (HEADS, NUM_EXPERTS), jnp.float32) * s, 'b_gat': jnp.zeros((HEADS * NUM_EXPERTS,), jnp.float32), 'ln_gamma': jnp.ones((HEADS * NUM_EXPERTS,), jnp.float32), 'ln_beta': jnp.zeros((HEADS * NUM_EXPERTS,), jnp.float32), 'W1': jax.random.normal(ks[4], (NUM_EXPERTS, D, 2 * D), jnp.float32) * s, 'b1': jnp.zeros((NUM_EXPERTS, 2 * D), jnp.float32), 'W2': jax.random.normal(ks[5], (NUM_EXPERTS, 2 * D, D), jnp.float32) * s, 'b2': jnp.zeros((NUM_EXPERTS, D), jnp.float32), 'edge_index': jax.random.randint(ks[6], (2, N_EDGES), 0, B * N, jnp.int32)}
    _L0_ffn_all = _L0_ffn_setup()
    _L0_ffn_in = {k: v for k, v in _L0_ffn_all.items() if k in ('W_gat', 'att_src', 'att_dst', 'b_gat', 'ln_gamma', 'ln_beta', 'W1', 'b1', 'W2', 'b2', 'edge_index')}
    del _L0_ffn_all
    return {'x': x, 'src': src, 'dst': dst, 'L0_gnn_W': _L0_gnn_in['W'], 'L0_gnn_b': _L0_gnn_in['b'], 'L0_gnn_a_src': _L0_gnn_in['a_src'], 'L0_gnn_a_dst': _L0_gnn_in['a_dst'], 'L0_mix_wq': _L0_mix_in['wq'], 'L0_mix_bq': _L0_mix_in['bq'], 'L0_mix_wk': _L0_mix_in['wk'], 'L0_mix_bk': _L0_mix_in['bk'], 'L0_mix_wv': _L0_mix_in['wv'], 'L0_mix_bv': _L0_mix_in['bv'], 'L0_mix_wo': _L0_mix_in['wo'], 'L0_mix_bo': _L0_mix_in['bo'], 'L0_ffn_W_gat': _L0_ffn_in['W_gat'], 'L0_ffn_att_src': _L0_ffn_in['att_src'], 'L0_ffn_att_dst': _L0_ffn_in['att_dst'], 'L0_ffn_b_gat': _L0_ffn_in['b_gat'], 'L0_ffn_ln_gamma': _L0_ffn_in['ln_gamma'], 'L0_ffn_ln_beta': _L0_ffn_in['ln_beta'], 'L0_ffn_W1': _L0_ffn_in['W1'], 'L0_ffn_b1': _L0_ffn_in['b1'], 'L0_ffn_W2': _L0_ffn_in['W2'], 'L0_ffn_b2': _L0_ffn_in['b2'], 'L0_ffn_edge_index': _L0_ffn_in['edge_index']}

def reference(x, src, dst, L0_gnn_W, L0_gnn_b, L0_gnn_a_src, L0_gnn_a_dst, L0_mix_wq, L0_mix_bq, L0_mix_wk, L0_mix_bk, L0_mix_wv, L0_mix_bv, L0_mix_wo, L0_mix_bo, L0_ffn_W_gat, L0_ffn_att_src, L0_ffn_att_dst, L0_ffn_b_gat, L0_ffn_ln_gamma, L0_ffn_ln_beta, L0_ffn_W1, L0_ffn_b1, L0_ffn_W2, L0_ffn_b2, L0_ffn_edge_index):
    import jax
    import jax.numpy as jnp

    def _L0_gnn_ref(h, edge_index, W, b, a_src, a_dst):
        import jax, jax.numpy as jnp
        import numpy as np
        N, IN_DIM, OUT_DIM, HEADS, E = (6250, 256, 256, 4, 100000)
        HEAD_DIM = OUT_DIM // HEADS
        NEG_SLOPE = 0.2
        idx_i, idx_j = (edge_index[0], edge_index[1])
        Wh = (h @ W.T + b).reshape(N, HEADS, HEAD_DIM)
        alpha_src = jnp.einsum('nhd,hd->nh', Wh, a_src)
        alpha_dst = jnp.einsum('nhd,hd->nh', Wh, a_dst)
        e = jax.nn.leaky_relu(alpha_src[idx_i] + alpha_dst[idx_j], NEG_SLOPE)
        m = jax.ops.segment_max(e, idx_i, num_segments=N)
        ex = jnp.exp(e - m[idx_i])
        denom = jax.ops.segment_sum(ex, idx_i, num_segments=N)
        att = ex / denom[idx_i]
        out = jax.ops.segment_sum(att[:, :, None] * Wh[idx_j], idx_i, num_segments=N)
        return out.reshape(N, OUT_DIM)

    def _L0_mix_ref(x, wq, bq, wk, bk, wv, bv, wo, bo):
        import jax, jax.numpy as jnp
        import numpy as np
        D_MODEL = 256
        NUM_HEADS = 8
        DEPTH = D_MODEL // NUM_HEADS
        B, L = (32, 512)

        def _feature_map(x):
            return jax.nn.elu(x) + 1.0
        b, l, _ = x.shape
        q = (x @ wq + bq).reshape(b, l, NUM_HEADS, DEPTH)
        k = (x @ wk + bk).reshape(b, l, NUM_HEADS, DEPTH)
        v = (x @ wv + bv).reshape(b, l, NUM_HEADS, DEPTH)
        q = _feature_map(q)
        k = _feature_map(k)
        kv = jnp.einsum('blhd,blhe->bhde', k, v)
        k_sum = jnp.sum(k, axis=1)
        qkv = jnp.einsum('blhd,bhde->blhe', q, kv)
        normalizer = jnp.einsum('blhd,bhd->blh', q, k_sum) + 1e-06
        out = qkv / normalizer[..., None]
        out = out.reshape(b, l, D_MODEL)
        return out @ wo + bo

    def _L0_ffn_ref(x, W_gat, att_src, att_dst, b_gat, ln_gamma, ln_beta, W1, b1, W2, b2, edge_index):
        import jax, jax.numpy as jnp
        import numpy as np
        B, N, D = (16, 512, 256)
        NUM_EXPERTS, TOP_K, HEADS = (4, 2, 4)
        N_EDGES = 131072
        LN_EPS = 1e-05

        def _layernorm(x, g, b):
            mu = x.mean(-1, keepdims=True)
            var = ((x - mu) ** 2).mean(-1, keepdims=True)
            return (x - mu) * jax.lax.rsqrt(var + LN_EPS) * g + b

        def _forward(x, edge_index, W_gat, att_src, att_dst, b_gat, ln_gamma, ln_beta, W1, b1, W2, b2):
            Bc, Nc, Dc = x.shape
            M = Bc * Nc
            x_flat = x.reshape(M, Dc)
            h = (x_flat @ W_gat).reshape(M, HEADS, NUM_EXPERTS)
            loops = jnp.arange(M, dtype=edge_index.dtype)
            src = jnp.concatenate([edge_index[0], loops])
            dst = jnp.concatenate([edge_index[1], loops])
            a_src = (h * att_src).sum(-1)
            a_dst = (h * att_dst).sum(-1)
            e = jax.nn.leaky_relu(a_src[src] + a_dst[dst], negative_slope=0.2)
            e_max = jax.ops.segment_max(e, dst, num_segments=M)
            ee = jnp.exp(e - e_max[dst])
            denom = jax.ops.segment_sum(ee, dst, num_segments=M)
            alpha = ee / (denom[dst] + 1e-16)
            msg = h[src] * alpha[:, :, None]
            agg = jax.ops.segment_sum(msg, dst, num_segments=M).reshape(M, HEADS * NUM_EXPERTS) + b_gat
            scores = _layernorm(agg, ln_gamma, ln_beta).reshape(M, HEADS, NUM_EXPERTS).mean(1)
            scores = scores.reshape(Bc, Nc, NUM_EXPERTS)
            topk_s, topk_i = jax.lax.top_k(scores, TOP_K)
            w = jax.nn.softmax(topk_s, axis=-1)
            out = jnp.zeros_like(x)
            for ei in range(NUM_EXPERTS):
                g = jnp.where(topk_i == ei, w, 0.0).sum(-1)
                hh = jax.nn.gelu(x @ W1[ei] + b1[ei], approximate=False)
                out = out + g[..., None] * (hh @ W2[ei] + b2[ei])
            return out
        return _forward(x, edge_index, W_gat, att_src, att_dst, b_gat, ln_gamma, ln_beta, W1, b1, W2, b2)
    edge_index = jnp.stack([src, dst])
    xn = _layernorm(x, axis=-1)
    x = x + _L0_gnn_ref(xn, edge_index, L0_gnn_W, L0_gnn_b, L0_gnn_a_src, L0_gnn_a_dst) + _L0_mix_ref(xn[None], L0_mix_wq, L0_mix_bq, L0_mix_wk, L0_mix_bk, L0_mix_wv, L0_mix_bv, L0_mix_wo, L0_mix_bo)[0]
    x = x + _L0_ffn_ref(_layernorm(x, axis=-1)[None], L0_ffn_W_gat, L0_ffn_att_src, L0_ffn_att_dst, L0_ffn_b_gat, L0_ffn_ln_gamma, L0_ffn_ln_beta, L0_ffn_W1, L0_ffn_b1, L0_ffn_W2, L0_ffn_b2, L0_ffn_edge_index)[0]
    return x

_drawn_inputs = setup_inputs


def setup_inputs(seed=0):
    import zlib

    import numpy as np

    out = dict(_drawn_inputs(seed))
    spreads = {'L0_gnn_b': (0.0, 0.1),
     'L0_mix_bq': (0.0, 2.0),
     'L0_mix_bk': (0.0, 2.0),
     'L0_mix_bv': (0.0, 0.1),
     'L0_mix_bo': (0.0, 0.1),
     'L0_ffn_b_gat': (0.0, 0.1),
     'L0_ffn_ln_gamma': (1.0, 0.2),
     'L0_ffn_ln_beta': (0.0, 0.1),
     'L0_ffn_b1': (0.0, 0.1),
     'L0_ffn_b2': (0.0, 0.1)}
    factors = {'L0_mix_wq': 11.391}
    for name, (base, spread) in spreads.items():
        noise = np.random.default_rng([zlib.crc32(name.encode()), seed]).standard_normal(out[name].shape)
        drawn = base * np.exp(spread * noise) if base else spread * noise
        out[name] = jnp.asarray(drawn.astype(out[name].dtype))
    for name, factor in factors.items():
        out[name] = (out[name] * factor).astype(out[name].dtype)
    return out
```

```python
import concourse.bass as bass
from concourse import mybir
from contextlib import ExitStack

F32 = mybir.dt.float32
BF16 = mybir.dt.bfloat16
I32 = mybir.dt.int32
U16 = mybir.dt.uint16
ALU = mybir.AluOpType
ACT = mybir.ActivationFunctionType
AX = mybir.AxisListType

P = 128
N, D, H = 6250, 256, 4
DH = D // H
NB = -(-N // P)
NP = NB * P
LAST = N - (NB - 1) * P
E1, E2 = 206250, 131072
TG = 4
GE = TG * P
MH, MD = 8, 32
HALF = P + 1
NE, F = 4, 512
EPS = 1e-5
NOWHERE = float(1 << 22)
NO_LANE = 255
U = 4
RUN = 13


class Graph:

    def __init__(self, name, edges, wh):
        self.name, self.edges, self.wh = name, edges, wh
        self.c = -(-edges // P)
        self.cp = -(-self.c // (2 * RUN)) * 2 * RUN
        self.s = -(-(edges // GE + NB) // U) * U
        self.acc = H * (wh + 1)
        self.row = self.acc + H


GNN = Graph("gnn", E1, DH)
FFN = Graph("ffn", E2, 4)


class Steps:

    def __init__(self, eng, sem):
        self.eng, self.sem, self.base, self.n = eng, sem, 0, 0

    def __call__(self, ins):
        self.n += 1
        ins.then_inc(self.sem, 1)
        self.eng.wait_ge(self.sem, self.base + self.n)

    def enter(self, i, k):
        self.before, self.k = self.base + self.n, k
        self.base, self.n = self.before + i * k, 0

    def leave(self, trips):
        assert self.n == self.k, (self.n, self.k)
        self.base, self.n = self.before + trips * self.k, 0


def alone(eng):
    eng.nop(nofuse=True)


def mean_var(dve, step, halves, mean, var, room):
    step(dve.tensor_tensor(mean, halves[:, :, 1], halves[:, :, 4], ALU.add))
    step(dve.tensor_scalar(mean, mean, 0.5, None, ALU.mult))
    step(dve.tensor_tensor(room, halves[:, :, 1], mean, ALU.subtract))
    step(dve.tensor_tensor(room, room, room, ALU.mult))
    step(dve.tensor_tensor(var, halves[:, :, 2], halves[:, :, 5], ALU.add))
    step(dve.scalar_tensor_tensor(var, var, 1.0 / D, room, ALU.mult, ALU.add))


def bcast(ap, n):
    return ap.unsqueeze(0).broadcast_to([n, ap.shape[0]])


def build(nc, io, out, debug=None):
    ctx = ExitStack()
    with ctx:
        def sb(name, shape, dt=F32):
            return ctx.enter_context(nc.sbuf_tensor(name, shape, dt))

        def sem(name):
            return ctx.enter_context(nc.semaphore(name))

        def dram(name, shape, dt=F32):
            return nc.dram_tensor(name, shape, dt, kind="Internal").ap()

        m = type("Memory", (), {})()
        m.table = {GNN: dram("gnn_table", (NP, GNN.row)), FFN: dram("ffn_table", (NP, FFN.row))}
        m.sorted = {g: dram(g.name + "_sorted", (g.s * GE, 1), I32) for g in (GNN, FFN)}
        m.phi_q = dram("phi_q", (NB * P, 2 * P))

        m.wide = sb("wide", [P, NP * 2])
        m.acc = sb("acc", [P, (NB + 1) * GNN.acc])
        m.acc_f = sb("acc_f", [P, NB + 1, FFN.acc])
        m.weights = sb("weights", [P, 9232])
        m.slots = sb("slots", [P, 9400])
        m.sinit = sb("sinit", [P, 2, NB])
        m.ends = sb("ends", [P, 2, NB])
        m.block_of = {g: sb(g.name + "_block_of", [1, g.s], I32) for g in (GNN, FFN)}
        m.att = sb("att", [P, NB, 2 * H])
        m.v = sb("v", [P, NB, H])
        m.low = sb("low", [P, H])
        m.mtab = sb("mtab", [P, NB + 1, H])
        m.ttab = sb("ttab", [P, NB + 1, 2 * H])
        m.kv = sb("kv", [P, 2, HALF])
        m.kvm = sb("kvm", [P, 2, P + H])
        m.stats = sb("stats", [P, NB, 2])
        m.rstd = sb("rstd", [P, NB])
        m.bn = sb("bn", [P, 6])
        m.small = sb("small", [P, 256])
        m.node_of = sb("node_of", [P, NB])
        m.h2 = sb("h2", [P, NB, H * FFN.wh])
        m.gates = sb("gates", [P, NB, NE])
        m.ident = sb("ident", [P, P])
        m.ident_b = sb("ident_b", [P, P], BF16)
        m.before = sb("before", [P, P])
        m.ones = sb("ones", [P, P])
        m.iota_n = sb("iota_n", [P, P])
        m.head_mask = sb("head_mask", [P, P])
        m.head_of = sb("head_of", [P, H])
        m.four = ctx.enter_context(nc.psum_tensor("four_banks", [P, 2048], F32))
        m.ps = [ctx.enter_context(nc.psum_tensor(f"bank{i}", [P, 512], F32)) for i in range(4)]

        sort_and_project(nc, m, io, sem)
        if debug == "sort":
            return
        graph_groups(nc, m, GNN, sem)
        if debug == "gnn":
            return
        combine(nc, m, io, sem)
        if debug == "combine":
            return
        graph_groups(nc, m, FFN, sem)
        if debug == "ffn":
            return
        score(nc, m, io, sem)
        experts(nc, m, io, out, sem)


def region(tensor, layout):
    at, views = 0, {}
    for name, words in layout:
        views[name] = tensor[:, at:at + words]
        at += words
    assert at <= tensor.shape[1], (at, tensor.shape)
    return views


def sort_and_project(nc, m, io, sem):
    C, CF = GNN.cp, FFN.cp
    r = region(m.acc, [("pos1", C), ("pack1", C), ("pos2", CF), ("pack2", CF),
                       ("key", C), ("scan", C), ("blk", C // 2), ("mask", C // 2), ("one", C // 2),
                       ("fill", 512)])
    pos = {GNN: r["pos1"], FFN: r["pos2"]}
    pack = {GNN: r["pack1"].bitcast(I32), FFN: r["pack2"].bitcast(I32)}
    key, scan, scani = r["key"].bitcast(I32), r["scan"], r["scan"].bitcast(I32)
    blk, mask, one = (r[n].bitcast(BF16) for n in ("blk", "mask", "one"))
    fill = r["fill"].bitcast(I32)
    x = m.wide[:, :].rearrange("p (b d) -> p b d", d=D)
    w = region(m.weights, [("wt", 2 * D), ("wk", 2 * D), ("wv", 2 * D), ("wq", 2 * D), ("bias", 3 * D),
                           ("a", 2 * D), ("bq", 2)])
    wt, wk, wv, wq = (w[n].rearrange("p (k n) -> p k n", k=2) for n in ("wt", "wk", "wv", "wq"))
    s = region(m.slots, [("xn", D), ("xnt", D), ("row", GNN.row), ("k", D), ("v", 2 * HALF),
                         ("neg", 2 * D), ("prod", 2 * D), ("phi", D), ("qpos", D),
                         ("stage_pos", 2 * RUN), ("stage_pack", 2 * RUN), ("iota_s", GNN.s), ("count", GNN.s),
                         ("lane_in", 1), ("iota_p", 1)])
    row = s["row"][:, 0:GNN.acc].rearrange("p (h w) -> p h w", h=H)
    vrow = s["v"].rearrange("p (j w) -> p j w", j=2)
    tot, totall, pad, starts, iota_f = (m.small[:, i * NB:(i + 1) * NB] for i in range(5))
    padi = pad.bitcast(I32)
    stage_pos, stage_pack = s["stage_pos"].bitcast(I32), s["stage_pack"].bitcast(I32)
    trips = [g.cp // (2 * RUN) for g in (GNN, FFN)]
    fills = [len(range(0, g.s * GE // P, 512)) for g in (GNN, FFN)]

    edges_in = [sem("gnn_edges_in"), sem("ffn_edges_in")]
    x_in, weights_in = sem("x_in"), sem("weights_in")
    const_ready, pads_ready, iota_ready = sem("const_ready"), sem("pads_ready"), sem("iota_ready")
    fill_ready, filled = sem("fill_ready"), [sem("gnn_filled"), sem("ffn_filled")]
    totals_ready, sums_ready, key_free, places_ready = (sem(n) for n in ("totals_ready", "sums_ready", "key_free", "places_ready"))
    staged = [sem("staged0"), sem("staged1")]
    scattered = [sem("scattered0"), sem("scattered1")]
    dve_step, var_ready, std_ready = sem("project_step"), sem("var_ready"), sem("std_ready")
    xn_ready, turned, xnt_ready, products_ready, products_read = (
        sem(n) for n in ("xn_ready", "turned", "xnt_ready", "products_ready", "products_read"))
    neg_ready, exp_ready, kv_in_ready, kv_made = (sem(n) for n in ("neg_ready", "exp_ready", "kv_in_ready", "kv_made"))
    row_ready, row_saved, phi_saved, slots_free = (sem(n) for n in ("row_ready", "row_saved", "phi_saved", "slots_free"))
    least = [sem(f"gnn_least{i}") for i in range(4)]
    prod_ready, v_ready, v_saved = sem("prod_ready"), sem("gnn_v_ready"), sem("gnn_v_saved")
    ps_w, ps_v, ps_q, ps_t = m.four[:, 0:512], m.four[:, 512:768], m.four[:, 1024:1280], m.four[:, 1536:1792]
    ps_kv = m.ps[0][:, 0:2 * HALF].rearrange("p (j w) -> p j w", j=2)
    ps_s = m.ps[1]

    with nc.Block() as block:
        @block.sync
        def _(sp):
            sp.wait_ge(pads_ready, 1)
            last = E1 - (P - 1) * GNN.c
            for t, n in ((key, "src"), (pack[GNN], "dst")):
                sp.dma_start(t[0:P - 1, 0:GNN.c], io[n][0:(P - 1) * GNN.c].rearrange("(p c) -> p c", c=GNN.c)).then_inc(edges_in[0], 16)
                sp.dma_start(t[P - 1:P, 0:last], io[n][(P - 1) * GNN.c:E1].unsqueeze(0)).then_inc(edges_in[0], 16)
            for i, g in enumerate((GNN, FFN)):
                flat = m.sorted[g].rearrange("(p c) o -> p (c o)", p=P)
                cols = g.s * GE // P
                for c0 in range(0, cols, 512):
                    c1 = min(cols, c0 + 512)
                    sp.dma_start(flat[:, c0:c1], fill[:, 0:c1 - c0]).then_inc(filled[i], 16)
            sp.wait_ge(key_free, 1)
            sp.dma_start(key[:, 0:FFN.c], io["edge_index"][1, :].rearrange("(p c) -> p c", p=P)).then_inc(edges_in[1], 16)
            sp.dma_start(pack[FFN][:, 0:FFN.c], io["edge_index"][0, :].rearrange("(p c) -> p c", p=P)).then_inc(edges_in[1], 16)
            done = 0
            for gi, g in enumerate((GNN, FFN)):
                sp.wait_ge(places_ready, gi + 1)

                def stage(i, half, free=None):
                    if free is not None:
                        sp.wait_ge(scattered[half], free)
                    at = slice(half * RUN, (half + 1) * RUN)
                    src = bass.ds(i * (2 * RUN) + half * RUN, RUN)
                    sp.dma_start(stage_pos[:, at], pos[g].bitcast(I32)[:, src]).then_inc(staged[half], 16)
                    sp.dma_start(stage_pack[:, at], pack[g][:, src]).then_inc(staged[half], 16)

                for half in range(2):
                    stage(0, half, 16 * RUN * done if done else None)
                with sp.Fori(1, trips[gi]) as i:
                    for half in range(2):
                        stage(i, half, i * (16 * RUN) + 16 * RUN * done)
                done += trips[gi]

        @block.gpsimd
        def _(pool):
            pool.iota(m.iota_n[:, :].bitcast(I32), [[1, P]], base=0, channel_multiplier=0).then_inc(iota_ready, 1)
            pool.iota(m.before[:, :].bitcast(I32), [[1, P]], base=0, channel_multiplier=-1).then_inc(iota_ready, 1)
            pool.iota(s["iota_p"].bitcast(I32), [[0, 1]], base=0, channel_multiplier=1).then_inc(iota_ready, 1)
            pool.iota(s["iota_s"].bitcast(I32), [[GE, GNN.s]], base=0, channel_multiplier=0).then_inc(iota_ready, 1)
            done = 0
            for gi, g in enumerate((GNN, FFN)):
                pool.wait_ge(filled[gi], 16 * fills[gi])
                with pool.Fori(0, trips[gi]) as i:
                    for half in range(2):
                        pool.wait_ge(staged[half], i * 32 + 32 * (done + 1))
                        alone(pool)
                        for c in range(half * RUN, (half + 1) * RUN):
                            pool.indirect_dma_start(
                                out=m.sorted[g], out_offset=bass.IndirectOffsetOnAxis(ap=stage_pos[:, c:c + 1], axis=0),
                                in_=stage_pack[:, c:c + 1], in_offset=None, bounds_check=g.s * GE - 1,
                                oob_is_err=False).then_inc(scattered[half], 16)
                done += trips[gi]
            for half in range(2):
                pool.wait_ge(scattered[half], 16 * RUN * done)

        @block.scalar
        def _(act):
            act.dma_start(x[:, 0:NB - 1, :], io["x"][0:(NB - 1) * P, :].rearrange("(b p) d -> p b d", p=P)).then_inc(x_in, 16)
            act.wait_ge(pads_ready, 1)
            act.dma_start(x[0:LAST, NB - 1, :], io["x"][(NB - 1) * P:N, :]).then_inc(x_in, 16)
            for t, n in ((wt, "W_t"), (wk, "wk"), (wv, "wv"), (wq, "wq")):
                act.dma_start(t, io[n].rearrange("(k p) n -> p k n", p=P)).then_inc(weights_in, 16)
            for i, n in enumerate(("b", "bk", "bv")):
                act.dma_start(w["bias"][:, i * D:(i + 1) * D], bcast(io[n], P)).then_inc(weights_in, 16)
            for i, n in enumerate(("a_src", "a_dst")):
                act.dma_start(w["a"][:, i * D:(i + 1) * D], bcast(io[n].rearrange("h d -> (h d)"), P)).then_inc(weights_in, 16)
            act.dma_start(w["bq"], io["bq"].rearrange("(p k) -> p k", k=2)).then_inc(weights_in, 16)
            act.wait_ge(var_ready, 1)
            act.activation(m.rstd[:, :], m.rstd[:, :], ACT.Sqrt).then_inc(std_ready, 1)
            act.sem_inc(slots_free, 1)
            with act.Fori(0, NB) as i:
                act.wait_ge(turned, i + 1)
                act.copy(s["xnt"], ps_t).then_inc(xnt_ready, 1)
                act.wait_ge(neg_ready, i + 1)
                act.activation(s["neg"], s["neg"], ACT.Exp).then_inc(exp_ready, 1)
                act.wait_ge(row_ready, i + 1)
                act.dma_start(m.table[GNN][bass.ds(i * P, P), 0:GNN.acc], s["row"][:, 0:GNN.acc]).then_inc(row_saved, 16)
                act.wait_ge(kv_in_ready, i + 1)
                act.dma_start(m.phi_q[bass.ds(i * P, P), :], s["phi"]).then_inc(phi_saved, 16)
                act.wait_ge(row_saved, i * 16 + 16)
                act.wait_ge(phi_saved, i * 16 + 16)
                act.sem_inc(slots_free, 1)
            act.wait_ge(v_ready, 1)
            act.dma_start(m.table[GNN].rearrange("(b p) w -> p b w", p=P)[:, :, GNN.acc:], m.v[:, :, :]).then_inc(v_saved, 16)
            act.wait_ge(v_saved, 16)

        @block.vector
        def _(dve):
            step = Steps(dve, dve_step)
            step(dve.memset(key, 8191))
            step(dve.memset(pack[GNN], 0))
            step(dve.memset(pack[FFN], 0))
            step(dve.memset(fill, NO_LANE))
            step(dve.memset(x[96:P, NB - 1, :], 0.0))
            step(dve.memset(one, 1.0))
            step(dve.memset(m.ones[:, :], 1.0))
            step(dve.memset(m.kv[:, :, :], 0.0))
            step(dve.memset(s["v"], 1.0))
            step(dve.memset(s["row"], 1.0))
            dve.memset(pos[GNN], NOWHERE).then_inc(pads_ready, 1)
            step(dve.memset(pos[FFN], NOWHERE))
            dve.wait_ge(iota_ready, 4)
            step(dve.tensor_copy(m.iota_n[:, :], m.iota_n[:, :].bitcast(I32)))
            step(dve.tensor_copy(m.before[:, :], m.before[:, :].bitcast(I32)))
            step(dve.tensor_copy(iota_f, m.iota_n[:, 0:NB]))
            step(dve.tensor_copy(s["iota_s"], s["iota_s"].bitcast(I32)))
            step(dve.tensor_scalar(m.ident[:, :], m.before[:, :], 0.0, None, ALU.is_equal))
            step(dve.tensor_copy(m.ident_b[:, :], m.ident[:, :]))
            step(dve.tensor_scalar(m.before[:, :], m.before[:, :], 0.0, None, ALU.is_gt))
            step(dve.memset(m.node_of[:, :], 1.0))
            step(dve.tensor_copy(s["lane_in"], s["iota_p"].bitcast(I32)))
            step(dve.tensor_scalar(m.node_of[:, NB - 1:NB], s["lane_in"], float(LAST), None, ALU.is_lt))
            step(dve.tensor_scalar(s["iota_p"].bitcast(I32), s["iota_p"].bitcast(I32), 5, None, ALU.arith_shift_right))
            step(dve.tensor_copy(s["lane_in"], s["iota_p"].bitcast(I32)))
            step(dve.tensor_copy(m.head_mask[:, :].bitcast(I32), m.iota_n[:, :]))
            step(dve.tensor_scalar(m.head_mask[:, :].bitcast(I32), m.head_mask[:, :].bitcast(I32), 5, None, ALU.arith_shift_right))
            step(dve.tensor_copy(m.head_mask[:, :], m.head_mask[:, :].bitcast(I32)))
            step(dve.tensor_scalar(m.head_mask[:, :], m.head_mask[:, :], s["lane_in"], None, ALU.is_equal))
            step(dve.tensor_scalar(m.head_of[:, :], m.iota_n[:, 0:H], s["lane_in"], None, ALU.is_equal))
            dve.wait_ge(pads_ready, 1)
            for gi, g in enumerate((GNN, FFN)):
                c = g.cp
                dve.wait_ge(edges_in[gi], (64, 32)[gi])
                step(dve.tensor_scalar(scani[:, 0:c], key[:, 0:c], 7, None, ALU.arith_shift_right))
                step(dve.tensor_copy(blk[:, 0:c], scani[:, 0:c]))
                step(dve.tensor_scalar(pack[g], pack[g], float(N - 1), 256.0, ALU.min, ALU.mult))
                step(dve.tensor_scalar(scani[:, 0:c], key[:, 0:c], P - 1, None, ALU.bitwise_and))
                step(dve.tensor_tensor(pack[g], pack[g], scani[:, 0:c], ALU.add))
                if gi == 0:
                    dve.memset(key[:, FFN.c:FFN.cp], 8191).then_inc(key_free, 1)
                with dve.Fori(0, NB) as b:
                    step.enter(b, 1)
                    step(dve.tensor_scalar(mask[:, 0:c], blk[:, 0:c], iota_f[:, bass.ds(b, 1)], 0.0, ALU.is_equal,
                                           ALU.add, accum_out=tot[:, bass.ds(b, 1)]))
                    step.leave(NB)
                dve.sem_inc(totals_ready, 1)
                dve.wait_ge(sums_ready, gi + 1)
                step(dve.tensor_scalar(padi, ps_s[:, 64:64 + NB], float(GE - 1), None, ALU.add))
                step(dve.tensor_scalar(padi, padi, GE.bit_length() - 1, GE.bit_length() - 1, ALU.arith_shift_right,
                                       ALU.logical_shift_left))
                step(dve.tensor_copy(totall, padi))
                step(dve.tensor_tensor_scan(m.ends[:, gi, :], m.ones[:, 0:NB], totall, 0.0, ALU.mult, ALU.add))
                step(dve.tensor_tensor(starts, m.ends[:, gi, :], totall, ALU.subtract))
                step(dve.scalar_tensor_tensor(m.sinit[:, gi, :], starts, -1.0, ps_s[:, 0:NB], ALU.add, ALU.add))
                with dve.Fori(0, NB) as b:
                    step.enter(b, 3)
                    step(dve.tensor_scalar(mask[:, 0:c], blk[:, 0:c], iota_f[:, bass.ds(b, 1)], None, ALU.is_equal))
                    step(dve.tensor_tensor_scan(scan[:, 0:c], one[:, 0:c], mask[:, 0:c],
                                                m.sinit[:, gi, bass.ds(b, 1)], ALU.mult, ALU.add))
                    alone(dve)
                    step(dve.copy_predicated(pos[g], mask[:, 0:c].bitcast(U16), scan[:, 0:c]))
                    step.leave(NB)
                dve.tensor_copy(pos[g].bitcast(I32), pos[g]).then_inc(places_ready, 1)
                count = s["count"][0:1, 0:g.s]
                step(dve.memset(count, 0.0))
                with dve.Fori(0, NB) as b:
                    step.enter(b, 1)
                    step(dve.scalar_tensor_tensor(count, s["iota_s"][0:1, 0:g.s], m.ends[0:1, gi, bass.ds(b, 1)],
                                                  count, ALU.is_ge, ALU.add))
                    step.leave(NB)
                step(dve.tensor_copy(m.block_of[g][:, :], count))

            dve.wait_ge(x_in, 32)
            halves = m.att[:, :, 0:6]
            with dve.Fori(0, NB) as b:
                step.enter(b, 1)
                step(dve.bn_stats(m.att[:, bass.ds(b, 1), 0:6].rearrange("p o d -> p (o d)"),
                                  x[:, bass.ds(b, 1), :].rearrange("p o d -> p (o d)")))
                step.leave(NB)
            mean_var(dve, step, halves, m.stats[:, :, 0], m.rstd[:, :], m.stats[:, :, 1])
            dve.tensor_scalar(m.rstd[:, :], m.rstd[:, :], EPS, None, ALU.add).then_inc(var_ready, 1)
            dve.wait_ge(std_ready, 1)
            step(dve.reciprocal(m.rstd[:, :], m.rstd[:, :]))
            dve.wait_ge(weights_in, 16 * 10)
            with dve.Fori(0, NB) as i:
                step.enter(i, 8)
                one_of = bass.ds(i, 1)
                dve.tensor_scalar(s["xn"], x[:, one_of, :].rearrange("p o d -> p (o d)"), m.stats[:, one_of, 0],
                                  m.rstd[:, one_of], ALU.subtract, ALU.mult).then_inc(xn_ready, 1)
                dve.wait_ge(products_ready, i + 1)
                dve.wait_ge(slots_free, i + 1)
                step(dve.tensor_tensor(row[:, :, 0:DH], ps_w[:, 0:D].rearrange("p (h d) -> p h d", h=H),
                                       w["bias"][:, 0:D].rearrange("p (h d) -> p h d", h=H), ALU.add))
                step(dve.tensor_tensor(s["k"], ps_w[:, D:2 * D], w["bias"][:, D:2 * D], ALU.add))
                step(dve.tensor_tensor(vrow[:, :, 0:P], ps_v.rearrange("p (j w) -> p j w", j=2),
                                       w["bias"][:, 2 * D:].rearrange("p (j w) -> p j w", j=2), ALU.add))
                step(dve.tensor_scalar(s["v"], s["v"], m.node_of[:, one_of], None, ALU.mult))
                step(dve.tensor_scalar(s["neg"][:, 0:D], s["k"], 0.0, None, ALU.min))
                for j in range(2):
                    c = slice(j * P, (j + 1) * P)
                    step(dve.tensor_scalar(s["qpos"][:, c], ps_q[:, c], w["bq"][:, j:j + 1], 0.0, ALU.add, ALU.max))
                dve.tensor_scalar(s["neg"][:, D:D + P], ps_q[:, 0:P], w["bq"][:, 0:1], 0.0, ALU.add, ALU.min)
                dve.tensor_scalar(s["neg"][:, D + P:], ps_q[:, P:], w["bq"][:, 1:2], 0.0, ALU.add, ALU.min).then_inc(neg_ready, 1)
                for j, signals in ((0, row_ready), (1, prod_ready)):
                    c = slice(j * D, (j + 1) * D)
                    dve.tensor_tensor(s["prod"][:, c].rearrange("p (h d) -> p h d", h=H), row[:, :, 0:DH],
                                      w["a"][:, c].rearrange("p (h d) -> p h d", h=H), ALU.mult).then_inc(signals, 1)
                dve.wait_ge(row_ready, i + 1)
                dve.wait_ge(prod_ready, i + 1)
                dve.tensor_reduce(m.att[:, one_of, :], s["prod"].rearrange("p (g d) -> p g d", d=DH), AX.X, ALU.add)
                dve.wait_ge(exp_ready, i + 1)
                step(dve.scalar_tensor_tensor(s["k"], s["k"], 0.0, s["neg"][:, 0:D], ALU.max, ALU.add))
                dve.tensor_tensor(s["phi"], s["qpos"], s["neg"][:, D:], ALU.add).then_inc(kv_in_ready, 1)
                dve.wait_ge(kv_made, i + 1)
                dve.tensor_tensor(m.kv[:, :, :], m.kv[:, :, :], ps_kv, ALU.add).then_inc(products_read, 1)
                dve.wait_ge(products_read, i + 1)
                step.leave(NB)
            least_v(dve, m, ps_s, least, v_ready, step)

        @block.tensor
        def _(pe):
            for gi in range(2):
                pe.wait_ge(totals_ready, gi + 1)
                nc.tensor.matmul(ps_s[:, 0:NB], m.before[:, :], tot, start=True, stop=True)
                nc.tensor.matmul(ps_s[:, 64:64 + NB], m.ones[:, :], tot, start=True, stop=True).then_inc(sums_ready, 1)
            pe.wait_ge(weights_in, 16 * 10)
            with pe.Fori(0, NB) as i:
                pe.wait_ge(xn_ready, i + 1)
                for k in range(2):
                    c = slice(k * P, (k + 1) * P)
                    last = nc.tensor.transpose(ps_t[:, c], s["xn"][:, c], m.ident[:, :])
                last.then_inc(turned, 1)
                pe.wait_ge(xnt_ready, i + 1)
                for k in range(2):
                    c, st = slice(k * P, (k + 1) * P), dict(start=k == 0, stop=k == 1)
                    nc.tensor.matmul(ps_w[:, 0:D], s["xnt"][:, c], wt[:, k, :], **st)
                for k in range(2):
                    c, st = slice(k * P, (k + 1) * P), dict(start=k == 0, stop=k == 1)
                    nc.tensor.matmul(ps_w[:, D:], s["xnt"][:, c], wk[:, k, :], **st)
                for k in range(2):
                    c, st = slice(k * P, (k + 1) * P), dict(start=k == 0, stop=k == 1)
                    nc.tensor.matmul(ps_v, s["xnt"][:, c], wv[:, k, :], **st)
                for j in range(2):
                    for k in range(2):
                        c, st = slice(k * P, (k + 1) * P), dict(start=k == 0, stop=k == 1)
                        last = nc.tensor.matmul(ps_q[:, j * P:(j + 1) * P], wq[:, k, j * P:(j + 1) * P], s["xnt"][:, c], **st)
                last.then_inc(products_ready, 1)
                pe.wait_ge(kv_in_ready, i + 1)
                for j in range(2):
                    last = nc.tensor.matmul(ps_kv[:, j, :], s["k"][:, j * P:(j + 1) * P], vrow[:, j, :], start=True, stop=True)
                last.then_inc(kv_made, 1)
            least_v_products(nc, pe, m, ps_s, least)


def graph_groups(nc, m, g, sem):
    groups, W = g.s, g.wh + 1
    lists = region(m.weights, [("raw", (groups + 1) * TG), ("lane", (groups + 1) * TG), ("index", (groups + 1) * TG)])
    raw, index = lists["raw"].bitcast(I32), lists["index"].bitcast(I32)
    lane = lists["lane"]
    s = region(m.slots, [(f"rows{u}", TG * g.row) for u in range(U)] + [(f"one_hot{o}", TG * P) for o in range(2)]
               + [(f"one_hot_t{o}", TG * P) for o in range(2)] + [(f"one_hot_b{o}", TG * P // 2) for o in range(2)]
               + [("spread", TG * H * P // 2)] + [(f"index{u}", TG) for u in range(U)]
               + [("term", 2 * H), ("scale", H), ("gmax", H), ("z", TG * H), ("weight", TG * H)])
    rows = [s[f"rows{u}"].rearrange("p (t w) -> p t w", t=TG) for u in range(U)]
    one_hot = [s[f"one_hot{o}"].rearrange("p (t n) -> p t n", t=TG) for o in range(2)]
    one_hot_t = [s[f"one_hot_t{o}"].rearrange("p (t n) -> p t n", t=TG) for o in range(2)]
    one_hot_b = [s[f"one_hot_b{o}"].bitcast(BF16).rearrange("p (t n) -> p t n", t=TG) for o in range(2)]
    spread = s["spread"].bitcast(BF16).rearrange("p (t h e) -> p t h e", t=TG, h=H)
    slot_index = [s[f"index{u}"].bitcast(I32) for u in range(U)]
    term, scale, gmax, z, weight = (s[n] for n in ("term", "scale", "gmax", "z", "weight"))
    z3, weight3 = z.rearrange("p (t h) -> p t h", h=H), weight.rearrange("p (t h) -> p t h", h=H)
    acc = m.acc[:, :].rearrange("p (b w) -> p b w", w=GNN.acc) if g is GNN else m.acc_f[:, :, :]
    ps_max = m.four[:, :].rearrange("p (t h e) -> p h t e", t=TG, h=H)
    ps_t, ps_e, ps_sum = m.ps[0], m.ps[1][:, 0:TG * 2 * H].rearrange("p (t c) -> p t c", t=TG), m.ps[2][:, 0:g.acc]

    def n(name):
        return sem(f"{g.name}_{name}")

    list_in, lists_ready = n("list_in"), n("lists_ready")
    indexed, gathered = n("indexed"), [n(f"gathered{u}") for u in range(U)]
    one_hot_ready, one_hot_b_ready, turned, one_hot_t_ready = (n(x) for x in (
        "one_hot_ready", "one_hot_b_ready", "turned", "one_hot_t_ready"))
    spread_ready, max_ready, term_ready, scale_ready, terms_at_edges = (n(x) for x in (
        "spread_ready", "max_ready", "term_ready", "scale_ready", "terms_at_edges"))
    e_ready, weight_ready, messages_ready, summed, dve_step = (n(x) for x in (
        "e_ready", "weight_ready", "messages_ready", "summed", "dve_step"))
    trips = groups // U

    with nc.Block() as block:
        @block.sync
        def _(sp):
            sp.dma_start(raw[:, 0:groups * TG].rearrange("p (s t) -> p s t", t=TG),
                         m.sorted[g].rearrange("(s p t) o -> p s (t o)", p=P, t=TG)).then_inc(list_in, 16)

        @block.gpsimd
        def _(pool):
            def gather(i, u, free):
                pool.wait_ge(indexed, i * U + u + 1)
                alone(pool)
                if free:
                    pool.wait_ge(summed, i * U + u - U + 1)
                    alone(pool)
                for t in range(TG):
                    pool.indirect_dma_start(out=rows[u][:, t, :], out_offset=None, in_=m.table[g],
                                            in_offset=bass.IndirectOffsetOnAxis(ap=slot_index[u][:, t:t + 1], axis=0)
                                            ).then_inc(gathered[u], 16)

            for u in range(U):
                gather(0, u, False)
            with pool.Fori(1, trips) as i:
                for u in range(U):
                    gather(i, u, True)

        @block.scalar
        def _(act):
            def one_hots(k, o):
                act.wait_ge(one_hot_ready, k + 1)
                act.copy(one_hot_b[o], one_hot[o]).then_inc(one_hot_b_ready, 1)

            def turned_out(k, o):
                act.wait_ge(turned, k + 1)
                act.copy(one_hot_t[o], ps_t[:, :].rearrange("p (t n) -> p t n", t=TG)).then_inc(one_hot_t_ready, 1)

            def group(i, u, last=False):
                k, o = i * U + u, (u + 1) % 2
                act.wait_ge(term_ready, k + 1)
                act.activation(scale, scale, ACT.Exp).then_inc(scale_ready, 1)
                if not last:
                    one_hots(k + 1, o)
                act.wait_ge(e_ready, k + 1)
                act.activation(weight, z, ACT.Exp).then_inc(weight_ready, 1)
                if not last:
                    turned_out(k + 1, o)

            def indices(i, u):
                act.copy(slot_index[u], index[:, bass.ds((i * U + u) * TG, TG)]).then_inc(indexed, 1)

            act.wait_ge(lists_ready, 1)
            for u in range(U):
                indices(0, u)
            one_hots(0, 0)
            turned_out(0, 0)
            with act.Fori(0, trips - 1) as i:
                for u in range(U):
                    group(i, u)
                    act.wait_ge(gathered[u], i * (16 * TG) + 16 * TG)
                    alone(act)
                    indices(i + 1, u)
            for u in range(U):
                group(trips - 1, u, last=u == U - 1)

        @block.vector
        def _(dve):
            step = Steps(dve, dve_step)
            dve.wait_ge(list_in, 16)
            lane_i = lane.bitcast(I32)
            step(dve.memset(raw[:, groups * TG:], NO_LANE))
            step(dve.tensor_scalar(index, raw, 8, None, ALU.arith_shift_right))
            step(dve.tensor_scalar(lane_i, raw, 255, None, ALU.bitwise_and))
            dve.tensor_copy(lane, lane_i).then_inc(lists_ready, 1)
            if g is GNN:
                step(dve.memset(m.acc[:, :], 0.0))
                step(dve.memset(m.mtab[:, :, :], 0.0))
            else:
                own = m.acc_f[:, 0:NB, :].rearrange("p b (h w) -> p b h w", h=H)
                step(dve.memset(m.acc_f[:, :, :], 1.0))
                for h in range(H):
                    step(dve.tensor_copy(own[:, :, h, 0:g.wh], m.h2[:, :, h * g.wh:(h + 1) * g.wh]))
                step(dve.memset(m.mtab[:, NB, :], 0.0))
                step(dve.tensor_copy(m.mtab[:, 0:NB, :], m.v[:, :, :]))
            top = m.ttab[:, :, H:]
            step(dve.tensor_tensor(top, m.ttab[:, :, 0:H], m.mtab[:, :, :], ALU.add))
            step(dve.scalar_tensor_tensor(top, top, 0.2, top, ALU.mult, ALU.max))
            dve.wait_ge(lists_ready, 1)

            def one_hots(k, o):
                lanes = lane[:, bass.ds(k * TG, TG)].unsqueeze(2).broadcast_to([P, TG, P])
                dve.tensor_tensor(one_hot[o], m.iota_n[:, :].unsqueeze(1).broadcast_to([P, TG, P]), lanes,
                                  ALU.is_equal).then_inc(one_hot_ready, 1)

            def spreads(u, tiles, last):
                for t in tiles:
                    for h in range(H):
                        ins = dve.tensor_scalar(spread[:, t, h, :], m.ident_b[:, :], rows[u][:, t, g.acc + h:g.acc + h + 1],
                                                None, ALU.mult)
                if last:
                    ins.then_inc(spread_ready, 1)

            def group(i, u, last=False):
                k, o = i * U + u, (u + 1) % 2
                b = bass.ds(dve.value_load(m.block_of[g][0:1, bass.ds(k, 1)], min_val=0, max_val=NB), 1)
                old = m.ttab[:, b, H:].rearrange("p o h -> p (o h)")
                own = m.ttab[:, b, 0:H].rearrange("p o h -> p (o h)")
                best = m.mtab[:, b, :].rearrange("p o h -> p (o h)")
                dve.wait_ge(max_ready, k + 1)
                step(dve.tensor_reduce(gmax, ps_max, AX.XY, ALU.max))
                step(dve.tensor_tensor(best, best, gmax, ALU.max))
                step(dve.tensor_tensor(gmax, own, best, ALU.add))
                step(dve.scalar_tensor_tensor(term[:, H:], gmax, 0.2, gmax, ALU.mult, ALU.max))
                step(dve.tensor_tensor(scale, old, term[:, H:], ALU.subtract))
                alone(dve)
                step(dve.tensor_copy(old, term[:, H:]))
                alone(dve)
                dve.tensor_copy(term[:, 0:H], own).then_inc(term_ready, 1)
                if not last:
                    one_hots(k + 1, o)
                dve.wait_ge(terms_at_edges, k + 1)
                step(dve.tensor_tensor(z3, rows[u][:, :, g.acc:], ps_e[:, :, 0:H], ALU.add))
                step(dve.scalar_tensor_tensor(z, z, 0.2, z, ALU.mult, ALU.max))
                dve.tensor_tensor(z3, z3, ps_e[:, :, H:], ALU.subtract).then_inc(e_ready, 1)
                if not last:
                    v = (u + 1) % U
                    dve.wait_ge(gathered[v], i * (16 * TG) + 16 * TG * (1 + (u + 1) // U))
                    spreads(v, (0,), False)
                dve.wait_ge(weight_ready, k + 1)
                msg = rows[u][:, :, 0:g.acc].rearrange("p t (h w) -> p t h w", h=H)
                for t in range(TG):
                    ins = dve.tensor_tensor(msg[:, t], msg[:, t], weight3[:, t, :].unsqueeze(2).broadcast_to([P, H, W]), ALU.mult)
                ins.then_inc(messages_ready, 1)
                if not last:
                    spreads(v, range(1, TG), True)
                dve.wait_ge(scale_ready, k + 1)
                sums = acc[:, b, :].rearrange("p o (h w) -> p (o h) w", h=H)
                step(dve.tensor_tensor(sums, sums, scale.unsqueeze(2).broadcast_to([P, H, W]), ALU.mult))
                dve.wait_ge(summed, k + 1)
                step(dve.tensor_tensor(sums, sums, ps_sum.rearrange("p (h w) -> p h w", h=H), ALU.add))

            one_hots(0, 0)
            dve.wait_ge(gathered[0], 16 * TG)
            spreads(0, range(TG), True)
            steps = U * 10
            with dve.Fori(0, trips - 1) as i:
                step.enter(i, steps)
                for u in range(U):
                    group(i, u)
                step.leave(trips - 1)
            for u in range(U):
                group(trips - 1, u, last=u == U - 1)

        @block.tensor
        def _(pe):
            def turn(k, o):
                pe.wait_ge(one_hot_ready, k + 1)
                for t in range(TG):
                    last = nc.tensor.transpose(ps_t[:, t * P:(t + 1) * P], one_hot[o][:, t, :], m.ident[:, :])
                last.then_inc(turned, 1)

            def maxima(k, o):
                pe.wait_ge(one_hot_b_ready, k + 1)
                pe.wait_ge(spread_ready, k + 1)
                for t in range(TG):
                    last = nc.tensor.matmul(m.four[:, t * H * P:(t + 1) * H * P], one_hot_b[o][:, t, :],
                                            spread[:, t].rearrange("p h e -> p (h e)"), start=True, stop=True)
                last.then_inc(max_ready, 1)

            def group(i, u, last_group=False):
                k, o = i * U + u, u % 2
                pe.wait_ge(term_ready, k + 1)
                pe.wait_ge(one_hot_t_ready, k + 1)
                for t in range(TG):
                    last = nc.tensor.matmul(ps_e[:, t, :], one_hot_t[o][:, t, :], term, start=True, stop=True)
                last.then_inc(terms_at_edges, 1)
                if not last_group:
                    turn(k + 1, 1 - o)
                pe.wait_ge(messages_ready, k + 1)
                for t in range(TG):
                    last = nc.tensor.matmul(ps_sum, one_hot[o][:, t, :], rows[u][:, t, 0:g.acc], start=t == 0, stop=t == TG - 1)
                last.then_inc(summed, 1)
                if not last_group:
                    maxima(k + 1, 1 - o)

            turn(0, 0)
            maxima(0, 0)
            with pe.Fori(0, trips - 1) as i:
                for u in range(U):
                    group(i, u)
            for u in range(U):
                group(trips - 1, u, last_group=u == U - 1)


def least_v(dve, m, ps, least, v_ready, step):
    low = m.small[:, 0:H]
    dve.drain()
    dve.tensor_reduce(low, m.att[:, :, H:].rearrange("p b h -> p h b"), AX.X, ALU.min).then_inc(least[0], 1)
    dve.wait_ge(least[1], 1)
    step(dve.tensor_reduce(m.small[0:H, 8:9], ps[0:H, 128:256], AX.X, ALU.min))
    dve.tensor_scalar(m.small[0:H, 16:16 + H], m.ident[0:H, 0:H], m.small[0:H, 8:9], None, ALU.mult).then_inc(least[2], 1)
    dve.wait_ge(least[3], 1)
    step(dve.tensor_copy(m.low[:, :], ps[:, 256:256 + H]))
    low_b = m.low[:, :].unsqueeze(1).broadcast_to([P, NB, H])
    dve.tensor_tensor(m.v[:, :, :], m.att[:, :, H:], low_b, ALU.subtract).then_inc(v_ready, 1)
    step(dve.tensor_tensor(m.ttab[:, 0:NB, 0:H], m.att[:, :, 0:H], low_b, ALU.add))
    step(dve.memset(m.ttab[:, NB, :], 0.0))
    dve.wait_ge(v_ready, 1)


def least_v_products(nc, pe, m, ps, least):
    pe.wait_ge(least[0], 1)
    nc.tensor.transpose(ps[0:H, 128:256], m.small[:, 0:H], m.ident[:, :]).then_inc(least[1], 1)
    pe.wait_ge(least[2], 1)
    nc.tensor.matmul(ps[:, 256:256 + H], m.ones[0:H, :], m.small[0:H, 16:16 + H], start=True, stop=True).then_inc(least[3], 1)


def combine(nc, m, io, sem):
    w = region(m.weights, [("wo", 2 * D), ("bo", D), ("w_gat", 2 * H * NE), ("att", 2 * H * NE), ("table", NB * FFN.row),
                           ("prod", NB * H * NE)])
    s = region(m.slots, [("phi0", D), ("phi1", D), ("mixed", D), ("mixed_t", D), ("x2n", D), ("x2t", D), ("near", D),
                         ("norm", 2 * H), ("den", H), ("mean", 1), ("var", 1), ("room", 1), ("rstd", 1)])
    wo, w_gat = w["wo"].rearrange("p (k n) -> p k n", k=2), w["w_gat"].rearrange("p (k n) -> p k n", k=2)
    acc = m.acc[:, :].rearrange("p (b w) -> p b w", w=GNN.acc)
    wide = m.wide[:, :].rearrange("p (b d) -> p b d", d=D)
    phi = [s["phi0"], s["phi1"]]
    table = w["table"].rearrange("p (b w) -> p b w", b=NB)
    ps_o = m.ps[0][:, 0:2 * (P + H)].rearrange("p (j w) -> p j w", j=2)
    ps_t, ps_r, ps_x, ps_h, ps_s = m.four[:, 0:D], m.four[:, 512:512 + D], m.four[:, 1024:1024 + D], m.ps[1][:, 0:H * NE], m.ps[2]

    weights_in, phi_in, kv_ready = sem("c_weights_in"), [sem("phi_in0"), sem("phi_in1")], sem("kv_ready")
    queried, mixed_ready, mixed_turned, mixed_t_ready, mix_ready = (sem("c_" + x) for x in (
        "queried", "mixed_ready", "mixed_turned", "mixed_t_ready", "mix_ready"))
    var_ready, std_ready, x2n_ready, x2n_turned, x2t_ready, h_ready, h_read = (sem("c_" + x) for x in (
        "var_ready", "std_ready", "x2n_ready", "x2n_turned", "x2t_ready", "h_ready", "h_read"))
    least, v_ready, table_saved, dve_step, table_ready = [sem(f"ffn_least{i}") for i in range(4)], sem("ffn_v_ready"), sem(
        "table_saved"), sem("c_step"), sem("c_table_ready")

    with nc.Block() as block:
        @block.sync
        def _(sp):
            def load_phi(i, o):
                sp.dma_start(phi[o], m.phi_q[bass.ds(i * P, P), :]).then_inc(phi_in[o], 16)

            load_phi(0, 0)
            load_phi(1, 1)
            sp.dma_start(wo, io["wo"].rearrange("(k p) n -> p k n", p=P)).then_inc(weights_in, 16)
            sp.dma_start(w["bo"], bcast(io["bo"], P)).then_inc(weights_in, 16)
            sp.dma_start(w_gat, io["W_gat"].rearrange("(k p) n -> p k n", p=P)).then_inc(weights_in, 16)
            for i, n in enumerate(("att_dst", "att_src")):
                c = slice(i * H * NE, (i + 1) * H * NE)
                sp.dma_start(w["att"][:, c], bcast(io[n].rearrange("h d -> (h d)"), P)).then_inc(weights_in, 16)
            with sp.Fori(0, (NB - 3) // 2) as i:
                for o in range(2):
                    sp.wait_ge(queried, i * 2 + o + 1)
                    load_phi(i * 2 + o + 2, o)
            sp.wait_ge(queried, NB - 2)
            load_phi(NB - 1, 0)
            sp.wait_ge(table_ready, 1)
            sp.dma_start(m.table[FFN].rearrange("(b p) w -> p b w", p=P), table).then_inc(table_saved, 16)
            sp.wait_ge(table_saved, 16)

        @block.scalar
        def _(act):
            with act.Fori(0, NB) as i:
                act.wait_ge(mixed_turned, i + 1)
                act.copy(s["mixed_t"], ps_t).then_inc(mixed_t_ready, 1)
                act.wait_ge(var_ready, i + 1)
                act.activation(s["rstd"], s["var"], ACT.Sqrt).then_inc(std_ready, 1)
                act.wait_ge(x2n_turned, i + 1)
                act.copy(s["x2t"], ps_x).then_inc(x2t_ready, 1)
                act.wait_ge(x2t_ready, i + 1)
                act.copy(wide[:, bass.ds(i, 1), :].rearrange("p o d -> p (o d)"), s["x2t"])

        @block.vector
        def _(dve):
            step = Steps(dve, dve_step)
            for j in range(2):
                step(dve.tensor_tensor(m.kvm[:, j, 0:P], m.kv[:, j, 0:P], m.head_mask[:, :], ALU.mult))
                step(dve.tensor_scalar(m.kvm[:, j, P:], m.head_of[:, :], m.kv[:, j, P:], None, ALU.mult))
            dve.sem_inc(kv_ready, 1)
            dve.wait_ge(weights_in, 16 * 5)
            with dve.Fori(0, NB) as i:
                step.enter(i, 16)
                b = bass.ds(i, 1)
                sums = acc[:, b, :].rearrange("p o (h w) -> p (o h) w", h=H)
                x2 = acc[:, b, 0:D].rearrange("p o d -> p (o d)")
                near = s["near"].rearrange("p (h d) -> p h d", h=H)
                step(dve.tensor_scalar(s["den"], sums[:, :, DH], 1e-30, None, ALU.max))
                step(dve.reciprocal(s["den"], s["den"]))
                step(dve.tensor_tensor(near, sums[:, :, 0:DH], s["den"].unsqueeze(2).broadcast_to([P, H, DH]), ALU.mult))
                step(dve.tensor_tensor(s["near"], s["near"], wide[:, b, :].rearrange("p o d -> p (o d)"), ALU.add))
                step(dve.tensor_tensor(s["near"], s["near"], w["bo"], ALU.add))
                dve.wait_ge(queried, i + 1)
                norm = s["norm"].rearrange("p (j h) -> p j h", j=2)
                step(dve.tensor_scalar(norm, ps_o[:, :, P:], 1e-6, None, ALU.add))
                step(dve.reciprocal(s["norm"], s["norm"]))
                for j in range(2):
                    ins = dve.tensor_tensor(s["mixed"][:, j * P:(j + 1) * P].rearrange("p (h d) -> p h d", d=MD),
                                            ps_o[:, j, 0:P].rearrange("p (h d) -> p h d", d=MD),
                                            norm[:, j, :].unsqueeze(2).broadcast_to([P, H, MD]), ALU.mult)
                ins.then_inc(mixed_ready, 1)
                dve.wait_ge(mix_ready, i + 1)
                step(dve.tensor_tensor(x2, s["near"], ps_r, ALU.add))
                alone(dve)
                step(dve.bn_stats(m.bn[:, :], x2))
                halves = m.bn[:, :].unsqueeze(1)
                mean_var(dve, step, halves, s["mean"], s["var"], s["room"])
                dve.tensor_scalar(s["var"], s["var"], EPS, None, ALU.add).then_inc(var_ready, 1)
                dve.wait_ge(std_ready, i + 1)
                step(dve.reciprocal(s["rstd"], s["rstd"]))
                dve.tensor_scalar(s["x2n"], x2, s["mean"], s["rstd"], ALU.subtract, ALU.mult).then_inc(x2n_ready, 1)
                dve.wait_ge(h_ready, i + 1)
                alone(dve)
                dve.tensor_copy(m.h2[:, b, :].rearrange("p o d -> p (o d)"), ps_h).then_inc(h_read, 1)
                step.leave(NB)
            dve.wait_ge(h_read, NB)
            prod = w["prod"].rearrange("p (b h e) -> p b h e", b=NB, h=H)
            h2 = m.h2[:, :, :].rearrange("p b (h e) -> p b h e", h=H)
            for j in range(2):
                a = w["att"][:, j * H * NE:(j + 1) * H * NE].unsqueeze(1).broadcast_to([P, NB, H * NE])
                step(dve.tensor_tensor(w["prod"].rearrange("p (b c) -> p b c", b=NB), m.h2[:, :, :], a, ALU.mult))
                step(dve.tensor_reduce(m.att[:, :, j * H:(j + 1) * H], prod, AX.X, ALU.add))
            least_v(dve, m, ps_s, least, v_ready, step)
            step(dve.memset(w["table"], 1.0))
            for h in range(H):
                step(dve.tensor_copy(table[:, :, h * (FFN.wh + 1):h * (FFN.wh + 1) + FFN.wh], h2[:, :, h, :]))
            dve.tensor_copy(table[:, :, FFN.acc:], m.v[:, :, :]).then_inc(table_ready, 1)

        @block.tensor
        def _(pe):
            pe.wait_ge(kv_ready, 1)
            pe.wait_ge(weights_in, 16 * 5)

            def tile(i, o, n):
                pe.wait_ge(phi_in[o], n)
                for j in range(2):
                    last = nc.tensor.matmul(ps_o[:, j, :], phi[o][:, j * P:(j + 1) * P], m.kvm[:, j, :], start=True, stop=True)
                last.then_inc(queried, 1)
                pe.wait_ge(mixed_ready, i + 1)
                for k in range(2):
                    last = nc.tensor.transpose(ps_t[:, k * P:(k + 1) * P], s["mixed"][:, k * P:(k + 1) * P], m.ident[:, :])
                last.then_inc(mixed_turned, 1)
                pe.wait_ge(mixed_t_ready, i + 1)
                for k in range(2):
                    last = nc.tensor.matmul(ps_r, s["mixed_t"][:, k * P:(k + 1) * P], wo[:, k, :], start=k == 0, stop=k == 1)
                last.then_inc(mix_ready, 1)
                pe.wait_ge(x2n_ready, i + 1)
                for k in range(2):
                    last = nc.tensor.transpose(ps_x[:, k * P:(k + 1) * P], s["x2n"][:, k * P:(k + 1) * P], m.ident[:, :])
                last.then_inc(x2n_turned, 1)
                pe.wait_ge(x2t_ready, i + 1)
                for k in range(2):
                    last = nc.tensor.matmul(ps_h, s["x2t"][:, k * P:(k + 1) * P], w_gat[:, k, :], start=k == 0, stop=k == 1)
                last.then_inc(h_ready, 1)

            with pe.Fori(0, NB // 2) as i:
                for o in range(2):
                    tile(i * 2 + o, o, i * 16 + 16)
            tile(NB - 1, 0, 16 * (NB // 2) + 16)
            least_v_products(nc, pe, m, ps_s, least)


def score(nc, m, io, sem):
    K = H * NE
    s = region(m.slots, [("agg", NB * K), ("sq", NB * K), ("den", NB * H), ("mean", NB), ("rstd", NB), ("scores", NB * NE),
                         ("beaten", NB * NE), ("one", NB), ("top", NB), ("e", NB * NE), ("b_gat", K), ("gamma", K), ("beta", K)])
    agg4 = s["agg"].rearrange("p (b h e) -> p b h e", b=NB, h=H)
    agg, sq = (s[n].rearrange("p (b k) -> p b k", b=NB) for n in ("agg", "sq"))
    scores, beaten, e = (s[n].rearrange("p (b e) -> p b e", b=NB) for n in ("scores", "beaten", "e"))
    params_in, var_ready, std_ready, dve_step = (sem("s_" + x) for x in ("params_in", "var_ready", "std_ready", "step"))
    gap_ready, exp_ready = sem("s_gap_ready"), sem("s_exp_ready")

    def wide(ap):
        return ap.unsqueeze(1).broadcast_to([P, NB, K])

    def each(ap, n):
        return ap.unsqueeze(2).broadcast_to([P, NB, n])

    with nc.Block() as block:
        @block.sync
        def _(sp):
            for n, k in (("b_gat", "b_gat"), ("gamma", "ln_gamma"), ("beta", "ln_beta")):
                sp.dma_start(s[n], bcast(io[k], P)).then_inc(params_in, 16)

        @block.scalar
        def _(act):
            act.wait_ge(var_ready, 1)
            act.activation(s["rstd"], s["rstd"], ACT.Sqrt).then_inc(std_ready, 1)
            act.wait_ge(gap_ready, 1)
            act.activation(s["e"], s["e"], ACT.Exp).then_inc(exp_ready, 1)

        @block.vector
        def _(dve):
            step = Steps(dve, dve_step)
            sums = m.acc_f[:, 0:NB, :].rearrange("p b (h w) -> p b h w", h=H)
            den = s["den"].rearrange("p (b h) -> p b h", b=NB)
            step(dve.tensor_scalar(den, sums[:, :, :, FFN.wh], 1e-16, None, ALU.add))
            step(dve.reciprocal(s["den"], s["den"]))
            for h in range(H):
                step(dve.tensor_tensor(agg4[:, :, h, :], sums[:, :, h, 0:FFN.wh], each(den[:, :, h], NE), ALU.mult))
            dve.wait_ge(params_in, 48)
            step(dve.tensor_tensor(agg, agg, wide(s["b_gat"]), ALU.add))
            step(dve.tensor_reduce(s["mean"], agg, AX.X, ALU.add))
            step(dve.tensor_scalar(s["mean"], s["mean"], 1.0 / K, None, ALU.mult))
            step(dve.tensor_tensor(agg, agg, each(s["mean"], K), ALU.subtract))
            step(dve.tensor_tensor(sq, agg, agg, ALU.mult))
            step(dve.tensor_reduce(s["rstd"], sq, AX.X, ALU.add))
            dve.tensor_scalar(s["rstd"], s["rstd"], 1.0 / K, EPS, ALU.mult, ALU.add).then_inc(var_ready, 1)
            dve.wait_ge(std_ready, 1)
            step(dve.reciprocal(s["rstd"], s["rstd"]))
            step(dve.tensor_tensor(agg, agg, each(s["rstd"], K), ALU.mult))
            step(dve.tensor_tensor(agg, agg, wide(s["gamma"]), ALU.mult))
            step(dve.tensor_tensor(agg, agg, wide(s["beta"]), ALU.add))
            step(dve.tensor_reduce(scores, s["agg"].rearrange("p (b h e) -> p b e h", b=NB, h=H), AX.X, ALU.add))
            step(dve.tensor_scalar(s["scores"], s["scores"], 1.0 / H, None, ALU.mult))
            step(dve.memset(s["beaten"], 0.0))
            for a in range(NE):
                for b in range(NE):
                    if a != b:
                        step(dve.tensor_tensor(s["one"], scores[:, :, b], scores[:, :, a], ALU.is_ge if b < a else ALU.is_gt))
                        step(dve.tensor_tensor(beaten[:, :, a], beaten[:, :, a], s["one"], ALU.add))
            step(dve.tensor_reduce(s["top"], scores, AX.X, ALU.max))
            dve.tensor_tensor(e, scores, each(s["top"], NE), ALU.subtract).then_inc(gap_ready, 1)
            step(dve.tensor_scalar(s["beaten"], s["beaten"], 2.0, None, ALU.is_lt))
            dve.wait_ge(exp_ready, 1)
            step(dve.tensor_tensor(s["e"], s["e"], s["beaten"], ALU.mult))
            step(dve.tensor_reduce(s["one"], e, AX.X, ALU.add))
            step(dve.reciprocal(s["one"], s["one"]))
            step(dve.tensor_tensor(m.gates[:, :, :], e, each(s["one"], NE), ALU.mult))


def experts(nc, m, io, out, sem):
    T, PARTS, FC = 7, ((0, 4), (4, 3)), F // P
    w = region(m.weights, [("w1", NE * 2 * F), ("w2", NE * FC * D), ("b2", NE * D)])
    w1 = w["w1"].rearrange("p (e k f) -> p e k f", e=NE, k=2)
    w2 = w["w2"].rearrange("p (e c d) -> p e c d", e=NE, c=FC)
    s = region(m.slots, [("hidden0", FC * T * P), ("hidden1", FC * T * P), ("b1", NE * FC)])
    hidden = [s[f"hidden{o}"].rearrange("p (c n) -> p c n", c=FC) for o in range(2)]
    wide = m.wide[:, :].rearrange("p (b k n) -> p b k n", k=2, n=P)
    acc = m.acc[:, :].rearrange("p (b w) -> p b w", w=GNN.acc)
    ps_y = [m.ps[i][:, 0:D] for i in range(4)]
    stretches = NB // T
    assert stretches * T == NB
    HID, Y, CREDIT = NE * len(PARTS) * FC, NE * T, 2 * T

    weights_in, made, gelu_done, y_ready, y_added, b2_added, saved = (sem("e_" + x) for x in (
        "weights_in", "made", "gelu_done", "y_ready", "y_added", "b2_added", "saved"))

    with nc.Block() as block:
        @block.sync
        def _(sp):
            for e in range(NE):
                sp.dma_start(w1[:, e], io["W1"][e].rearrange("(k p) f -> p k f", p=P)).then_inc(weights_in, 16)
                sp.dma_start(w2[:, e], io["W2"][e].rearrange("(c p) d -> p c d", p=P)).then_inc(weights_in, 16)
            sp.dma_start(w["b2"], bcast(io["b2"].rearrange("e d -> (e d)"), P)).then_inc(weights_in, 16)
            sp.dma_start(s["b1"], io["b1"]).then_inc(weights_in, 16)

            with sp.Fori(0, stretches - 1) as i:
                sp.wait_ge(y_added, i * Y + Y + CREDIT)
                sp.dma_start(out[bass.ds(i * (T * P), T * P), :].rearrange("(t p) d -> p t d", p=P),
                             acc[:, bass.ds(i * T, T), 0:D]).then_inc(saved, 16)
            sp.wait_ge(y_added, stretches * Y + CREDIT)
            sp.dma_start(out[(NB - T) * P:(NB - 1) * P, :].rearrange("(t p) d -> p t d", p=P),
                         acc[:, NB - T:NB - 1, 0:D]).then_inc(saved, 16)
            sp.dma_start(out[(NB - 1) * P:N, :], acc[0:LAST, NB - 1, 0:D]).then_inc(saved, 16)
            sp.wait_ge(saved, 16 * (stretches + 1))

        @block.tensor
        def _(pe):
            pe.wait_ge(weights_in, 16 * 10)
            with pe.Fori(0, stretches) as i:
                def make(e):
                    for part, (t0, nt) in enumerate(PARTS):
                        for c in range(FC):
                            at = (e * len(PARTS) + part) * FC + c
                            pe.wait_ge(gelu_done, i * HID + at + 1)
                            for k in range(2):
                                last = nc.tensor.matmul(m.four[:, c * 512:c * 512 + nt * P], w1[:, e, k, c * P:(c + 1) * P],
                                                        wide[:, bass.ds(i * T + t0, nt), k, :], start=k == 0, stop=k == 1)
                            last.then_inc(made, 1)

                def contract(e):
                    pe.wait_ge(gelu_done, i * HID + (e + 1) * HID // NE + FC)
                    for t in range(T):
                        at = e * T + t
                        pe.wait_ge(y_added, i * Y + at - 3 + CREDIT)
                        for c in range(FC):
                            last = nc.tensor.matmul(ps_y[at % 4], hidden[e % 2][:, c, t * P:(t + 1) * P], w2[:, e, c, :],
                                                    start=c == 0, stop=c == FC - 1)
                        last.then_inc(y_ready, 1)

                make(0)
                for e in range(1, NE):
                    make(e)
                    contract(e - 1)
                contract(NE - 1)

        @block.scalar
        def _(act):
            act.sem_inc(gelu_done, FC)
            act.wait_ge(weights_in, 16 * 10)
            with act.Fori(0, stretches) as i:
                for e in range(NE):
                    act.wait_ge(y_added, i * Y + (e - 1) * T + CREDIT)
                    for part, (t0, nt) in enumerate(PARTS):
                        for c in range(FC):
                            at = (e * len(PARTS) + part) * FC + c
                            act.wait_ge(made, i * HID + at + 1)
                            act.activation(hidden[e % 2][:, c, t0 * P:(t0 + nt) * P], m.four[:, c * 512:c * 512 + nt * P],
                                           ACT.Gelu, bias=s["b1"][:, e * FC + c:e * FC + c + 1]).then_inc(gelu_done, 1)

        @block.vector
        def _(dve):
            dve.sem_inc(y_added, CREDIT)
            dve.wait_ge(weights_in, 16 * 10)
            gates = m.gates[:, :, :].rearrange("p b e -> p (b e)")
            with dve.Fori(0, stretches) as i:
                for e in range(NE):
                    for t in range(T):
                        at = e * T + t
                        x2 = acc[:, bass.ds(i * T + t, 1), 0:D].rearrange("p o d -> p (o d)")
                        gate = gates[:, bass.ds((i * T + t) * NE + e, 1)]
                        dve.scalar_tensor_tensor(x2, w["b2"][:, e * D:(e + 1) * D], gate, x2, ALU.mult, ALU.add).then_inc(b2_added, 1)
                        dve.wait_ge(b2_added, i * Y + at + 1)
                        dve.wait_ge(y_ready, i * Y + at + 1)
                        dve.scalar_tensor_tensor(x2, ps_y[at % 4], gate, x2, ALU.mult, ALU.add).then_inc(y_added, 1)
                        dve.wait_ge(y_added, i * Y + at + 1 + CREDIT)


_INS = [("x", "x"), ("src", "src"), ("dst", "dst"), ("L0_gnn_W", "W_t"), ("L0_gnn_b", "b"), ("L0_gnn_a_src", "a_src"),
        ("L0_gnn_a_dst", "a_dst"), ("L0_mix_wq", "wq"), ("L0_mix_bq", "bq"), ("L0_mix_wk", "wk"), ("L0_mix_bk", "bk"),
        ("L0_mix_wv", "wv"), ("L0_mix_bv", "bv"), ("L0_mix_wo", "wo"), ("L0_mix_bo", "bo"), ("L0_ffn_W_gat", "W_gat"),
        ("L0_ffn_att_src", "att_src"), ("L0_ffn_att_dst", "att_dst"), ("L0_ffn_b_gat", "b_gat"),
        ("L0_ffn_ln_gamma", "ln_gamma"), ("L0_ffn_ln_beta", "ln_beta"), ("L0_ffn_W1", "W1"), ("L0_ffn_b1", "b1"),
        ("L0_ffn_W2", "W2"), ("L0_ffn_b2", "b2"), ("L0_ffn_edge_index", "edge_index")]


def laid_out(inputs):
    import numpy as np
    got = {}
    for name, short in _INS:
        a = np.ascontiguousarray(inputs[name])
        if short == "W_t":
            a = np.ascontiguousarray(a.T)
        if short == "bq":
            a = np.ascontiguousarray(a.reshape(2, P).T).reshape(-1)
        if short == "b1":
            a = np.ascontiguousarray(a.reshape(NE * F // P, P).T)
        got[short] = a
    return got


def kernel(**inputs):
    import concourse.bacc as _bacc
    from concourse.bass_utils import run_bass_kernel_spmd as _run

    nc = _bacc.Bacc("TRN2", target_bir_lowering=False, num_devices=1)
    arrays, io = {}, {}
    for short, a in laid_out(inputs).items():
        arrays[f"in_{short}"] = a
        io[short] = nc.dram_tensor(f"in_{short}", a.shape, mybir.dt.from_np(a.dtype), kind="ExternalInput").ap()
    out = nc.dram_tensor("out", (N, D), F32, kind="ExternalOutput").ap()
    build(nc, io, out)
    r = _run(nc, [arrays], core_ids=[0])
    return r.results[0]["out"]
```

```python
import concourse.bass as bass
from concourse import mybir
from contextlib import ExitStack

F32 = mybir.dt.float32
BF16 = mybir.dt.bfloat16
I32 = mybir.dt.int32
U16 = mybir.dt.uint16
ALU = mybir.AluOpType
ACT = mybir.ActivationFunctionType
AX = mybir.AxisListType

P = 128
N, D, H = 6250, 256, 4
DH = D // H
NB = -(-N // P)
NP = NB * P
LAST = N - (NB - 1) * P
E1, E2 = 206250, 131072
TG = 4
GE = TG * P
MH, MD = 8, 32
HALF = P + 1
NE, F = 4, 512
EPS = 1e-5
SLOPE = 0.2
SPREAD = 16.0
NOWHERE = float(1 << 22)
NO_LANE = 255
U = 4
BASE = NB + 1
assert BASE ** U < 1 << 24
RUN = 13


class Graph:

    def __init__(self, name, edges, wh):
        self.name, self.edges, self.wh = name, edges, wh
        self.c = -(-edges // P)
        self.cp = -(-self.c // (2 * RUN)) * 2 * RUN
        self.s = -(-(edges // GE + NB) // U) * U
        self.acc = H * (wh + 1)
        self.row = self.acc + 2 * H


GNN = Graph("gnn", E1, DH)
FFN = Graph("ffn", E2, 4)


class Steps:

    def __init__(self, eng, sem):
        self.eng, self.sem, self.base, self.n = eng, sem, 0, 0

    def __call__(self, ins):
        self.n += 1
        ins.then_inc(self.sem, 1)
        self.eng.wait_ge(self.sem, self.base + self.n)

    def enter(self, i, k):
        self.before, self.k = self.base + self.n, k
        self.base, self.n = self.before + i * k, 0

    def leave(self, trips):
        assert self.n == self.k, (self.n, self.k)
        self.base, self.n = self.before + trips * self.k, 0


def alone(eng):
    eng.nop(nofuse=True)


def mean_var(dve, step, halves, mean, var, room):
    step(dve.tensor_tensor(mean, halves[:, :, 1], halves[:, :, 4], ALU.add))
    step(dve.tensor_scalar(mean, mean, 0.5, None, ALU.mult))
    step(dve.tensor_tensor(room, halves[:, :, 1], mean, ALU.subtract))
    step(dve.tensor_tensor(room, room, room, ALU.mult))
    step(dve.tensor_tensor(var, halves[:, :, 2], halves[:, :, 5], ALU.add))
    step(dve.scalar_tensor_tensor(var, var, 1.0 / D, room, ALU.mult, ALU.add))


def bcast(ap, n):
    return ap.unsqueeze(0).broadcast_to([n, ap.shape[0]])


def build(nc, io, out, debug=None):
    ctx = ExitStack()
    with ctx:
        def sb(name, shape, dt=F32):
            return ctx.enter_context(nc.sbuf_tensor(name, shape, dt))

        def sem(name):
            return ctx.enter_context(nc.semaphore(name))

        def dram(name, shape, dt=F32):
            return nc.dram_tensor(name, shape, dt, kind="Internal").ap()

        m = type("Memory", (), {})()
        m.table = {GNN: dram("gnn_table", (NP, GNN.row)), FFN: dram("ffn_table", (NP, FFN.row))}
        m.sorted = {g: dram(g.name + "_sorted", (g.s * GE, 1), I32) for g in (GNN, FFN)}
        m.phi_q = dram("phi_q", (NB * P, 2 * P))

        m.wide = sb("wide", [P, NP * 2])
        m.acc = sb("acc", [P, (NB + 1) * GNN.acc])
        m.acc_f = sb("acc_f", [P, NB + 1, FFN.acc])
        m.weights = sb("weights", [P, 9232])
        m.slots = sb("slots", [P, 9400])
        m.sinit = sb("sinit", [P, 2, NB])
        m.ends = sb("ends", [P, 2, NB])
        m.block_of = {g: sb(g.name + "_block_of", [1, g.s], I32) for g in (GNN, FFN)}
        m.blocks_of = {g: sb(g.name + "_blocks_of", [1, g.s // U], I32) for g in (GNN, FFN)}
        m.att = sb("att", [P, NB, 2 * H])
        m.v = sb("v", [P, NB, 2 * H])
        m.low = sb("low", [P, 2 * H])
        m.near = sb("near", [1, 1], I32)
        m.terms = sb("terms", [P, NB + 1, 3, 2 * H], BF16)
        m.mtab = sb("mtab", [P, NB + 1, H])
        m.ttab = sb("ttab", [P, NB + 1, 2 * H])
        m.kv = sb("kv", [P, 2, HALF])
        m.kvm = sb("kvm", [P, 2, P + H])
        m.stats = sb("stats", [P, NB, 2])
        m.rstd = sb("rstd", [P, NB])
        m.bn = sb("bn", [P, 6])
        m.small = sb("small", [P, 256])
        m.node_of = sb("node_of", [P, NB])
        m.h2 = sb("h2", [P, NB, H * FFN.wh])
        m.both = sb("both", [P, NB, 2 * H])
        m.gates = sb("gates", [P, NB, NE])
        m.ident = sb("ident", [P, P])
        m.ident_b = sb("ident_b", [P, P], BF16)
        m.before = sb("before", [P, P])
        m.ones = sb("ones", [P, P])
        m.iota_n = sb("iota_n", [P, P])
        m.head_mask = sb("head_mask", [P, P])
        m.head_of = sb("head_of", [P, H])
        m.four = ctx.enter_context(nc.psum_tensor("four_banks", [P, 2048], F32))
        m.ps = [ctx.enter_context(nc.psum_tensor(f"bank{i}", [P, 512], F32)) for i in range(4)]

        sort_and_project(nc, m, io, sem)
        if debug == "sort":
            return
        graph_groups(nc, m, GNN, sem)
        if debug == "gnn":
            return
        combine(nc, m, io, sem)
        if debug == "combine":
            return
        graph_groups(nc, m, FFN, sem)
        if debug == "ffn":
            return
        score(nc, m, io, sem)
        experts(nc, m, io, out, sem)


def region(tensor, layout):
    at, views = 0, {}
    for name, words in layout:
        views[name] = tensor[:, at:at + words]
        at += words
    assert at <= tensor.shape[1], (at, tensor.shape)
    return views


def sort_and_project(nc, m, io, sem):
    C, CF = GNN.cp, FFN.cp
    r = region(m.acc, [("pos1", C), ("pack1", C), ("pos2", CF), ("pack2", CF),
                       ("key", C), ("scan", C), ("blk", C // 2), ("mask", C // 2), ("one", C // 2),
                       ("fill", 512)])
    pos = {GNN: r["pos1"], FFN: r["pos2"]}
    pack = {GNN: r["pack1"].bitcast(I32), FFN: r["pack2"].bitcast(I32)}
    key, scan, scani = r["key"].bitcast(I32), r["scan"], r["scan"].bitcast(I32)
    blk, mask, one = (r[n].bitcast(BF16) for n in ("blk", "mask", "one"))
    fill = r["fill"].bitcast(I32)
    x = m.wide[:, :].rearrange("p (b d) -> p b d", d=D)
    w = region(m.weights, [("wt", 2 * D), ("wk", 2 * D), ("wv", 2 * D), ("wq", 2 * D), ("bias", 3 * D),
                           ("a", 2 * D), ("bq", 2)])
    wt, wk, wv, wq = (w[n].rearrange("p (k n) -> p k n", k=2) for n in ("wt", "wk", "wv", "wq"))
    s = region(m.slots, [("xn", D), ("xnt", D), ("row", GNN.row), ("k", D), ("v", 2 * HALF),
                         ("neg", 2 * D), ("prod", 2 * D), ("phi", D), ("qpos", D),
                         ("stage_pos", 2 * RUN), ("stage_pack", 2 * RUN), ("iota_s", GNN.s), ("count", GNN.s),
                         ("lane_in", 1), ("iota_p", 1)])
    row = s["row"][:, 0:GNN.acc].rearrange("p (h w) -> p h w", h=H)
    vrow = s["v"].rearrange("p (j w) -> p j w", j=2)
    tot, totall, pad, starts, iota_f = (m.small[:, i * NB:(i + 1) * NB] for i in range(5))
    padi = pad.bitcast(I32)
    stage_pos, stage_pack = s["stage_pos"].bitcast(I32), s["stage_pack"].bitcast(I32)
    trips = [g.cp // (2 * RUN) for g in (GNN, FFN)]
    fills = [len(range(0, g.s * GE // P, 512)) for g in (GNN, FFN)]

    edges_in = [sem("gnn_edges_in"), sem("ffn_edges_in")]
    x_in, weights_in = sem("x_in"), sem("weights_in")
    const_ready, pads_ready, iota_ready = sem("const_ready"), sem("pads_ready"), sem("iota_ready")
    fill_ready, filled = sem("fill_ready"), [sem("gnn_filled"), sem("ffn_filled")]
    totals_ready, sums_ready, key_free, places_ready = (sem(n) for n in ("totals_ready", "sums_ready", "key_free", "places_ready"))
    staged = [sem("staged0"), sem("staged1")]
    scattered = [sem("scattered0"), sem("scattered1")]
    dve_step, var_ready, std_ready = sem("project_step"), sem("var_ready"), sem("std_ready")
    xn_ready, turned, xnt_ready, products_ready, products_read = (
        sem(n) for n in ("xn_ready", "turned", "xnt_ready", "products_ready", "products_read"))
    neg_ready, exp_ready, kv_in_ready, kv_made = (sem(n) for n in ("neg_ready", "exp_ready", "kv_in_ready", "kv_made"))
    row_ready, row_saved, phi_saved, slots_free = (sem(n) for n in ("row_ready", "row_saved", "phi_saved", "slots_free"))
    least = [sem(f"gnn_least{i}") for i in range(4)]
    prod_ready, v_ready, v_saved = sem("prod_ready"), sem("gnn_v_ready"), sem("gnn_v_saved")
    ps_w, ps_v, ps_q, ps_t = m.four[:, 0:512], m.four[:, 512:768], m.four[:, 1024:1280], m.four[:, 1536:1792]
    ps_kv = m.ps[0][:, 0:2 * HALF].rearrange("p (j w) -> p j w", j=2)
    ps_s = m.ps[1]

    with nc.Block() as block:
        @block.sync
        def _(sp):
            sp.wait_ge(pads_ready, 1)
            last = E1 - (P - 1) * GNN.c
            for t, n in ((key, "src"), (pack[GNN], "dst")):
                sp.dma_start(t[0:P - 1, 0:GNN.c], io[n][0:(P - 1) * GNN.c].rearrange("(p c) -> p c", c=GNN.c)).then_inc(edges_in[0], 16)
                sp.dma_start(t[P - 1:P, 0:last], io[n][(P - 1) * GNN.c:E1].unsqueeze(0)).then_inc(edges_in[0], 16)
            for i, g in enumerate((GNN, FFN)):
                flat = m.sorted[g].rearrange("(p c) o -> p (c o)", p=P)
                cols = g.s * GE // P
                for c0 in range(0, cols, 512):
                    c1 = min(cols, c0 + 512)
                    sp.dma_start(flat[:, c0:c1], fill[:, 0:c1 - c0]).then_inc(filled[i], 16)
            sp.wait_ge(key_free, 1)
            sp.dma_start(key[:, 0:FFN.c], io["edge_index"][1, :].rearrange("(p c) -> p c", p=P)).then_inc(edges_in[1], 16)
            sp.dma_start(pack[FFN][:, 0:FFN.c], io["edge_index"][0, :].rearrange("(p c) -> p c", p=P)).then_inc(edges_in[1], 16)
            done = 0
            for gi, g in enumerate((GNN, FFN)):
                sp.wait_ge(places_ready, gi + 1)

                def stage(i, half, free=None):
                    if free is not None:
                        sp.wait_ge(scattered[half], free)
                    at = slice(half * RUN, (half + 1) * RUN)
                    src = bass.ds(i * (2 * RUN) + half * RUN, RUN)
                    sp.dma_start(stage_pos[:, at], pos[g].bitcast(I32)[:, src]).then_inc(staged[half], 16)
                    sp.dma_start(stage_pack[:, at], pack[g][:, src]).then_inc(staged[half], 16)

                for half in range(2):
                    stage(0, half, 16 * RUN * done if done else None)
                with sp.Fori(1, trips[gi]) as i:
                    for half in range(2):
                        stage(i, half, i * (16 * RUN) + 16 * RUN * done)
                done += trips[gi]

        @block.gpsimd
        def _(pool):
            pool.iota(m.iota_n[:, :].bitcast(I32), [[1, P]], base=0, channel_multiplier=0).then_inc(iota_ready, 1)
            pool.iota(m.before[:, :].bitcast(I32), [[1, P]], base=0, channel_multiplier=-1).then_inc(iota_ready, 1)
            pool.iota(s["iota_p"].bitcast(I32), [[0, 1]], base=0, channel_multiplier=1).then_inc(iota_ready, 1)
            pool.iota(s["iota_s"].bitcast(I32), [[GE, GNN.s]], base=0, channel_multiplier=0).then_inc(iota_ready, 1)
            done = 0
            for gi, g in enumerate((GNN, FFN)):
                pool.wait_ge(filled[gi], 16 * fills[gi])
                with pool.Fori(0, trips[gi]) as i:
                    for half in range(2):
                        pool.wait_ge(staged[half], i * 32 + 32 * (done + 1))
                        alone(pool)
                        for c in range(half * RUN, (half + 1) * RUN):
                            pool.indirect_dma_start(
                                out=m.sorted[g], out_offset=bass.IndirectOffsetOnAxis(ap=stage_pos[:, c:c + 1], axis=0),
                                in_=stage_pack[:, c:c + 1], in_offset=None, bounds_check=g.s * GE - 1,
                                oob_is_err=False).then_inc(scattered[half], 16)
                done += trips[gi]
            for half in range(2):
                pool.wait_ge(scattered[half], 16 * RUN * done)

        @block.scalar
        def _(act):
            act.dma_start(x[:, 0:NB - 1, :], io["x"][0:(NB - 1) * P, :].rearrange("(b p) d -> p b d", p=P)).then_inc(x_in, 16)
            act.wait_ge(pads_ready, 1)
            act.dma_start(x[0:LAST, NB - 1, :], io["x"][(NB - 1) * P:N, :]).then_inc(x_in, 16)
            for t, n in ((wt, "W_t"), (wk, "wk"), (wv, "wv"), (wq, "wq")):
                act.dma_start(t, io[n].rearrange("(k p) n -> p k n", p=P)).then_inc(weights_in, 16)
            for i, n in enumerate(("b", "bk", "bv")):
                act.dma_start(w["bias"][:, i * D:(i + 1) * D], bcast(io[n], P)).then_inc(weights_in, 16)
            for i, n in enumerate(("a_src", "a_dst")):
                act.dma_start(w["a"][:, i * D:(i + 1) * D], bcast(io[n].rearrange("h d -> (h d)"), P)).then_inc(weights_in, 16)
            act.dma_start(w["bq"], io["bq"].rearrange("(p k) -> p k", k=2)).then_inc(weights_in, 16)
            act.wait_ge(var_ready, 1)
            act.activation(m.rstd[:, :], m.rstd[:, :], ACT.Sqrt).then_inc(std_ready, 1)
            act.sem_inc(slots_free, 1)
            with act.Fori(0, NB) as i:
                act.wait_ge(turned, i + 1)
                act.copy(s["xnt"], ps_t).then_inc(xnt_ready, 1)
                act.wait_ge(neg_ready, i + 1)
                act.activation(s["neg"], s["neg"], ACT.Exp).then_inc(exp_ready, 1)
                act.wait_ge(row_ready, i + 1)
                act.dma_start(m.table[GNN][bass.ds(i * P, P), 0:GNN.acc], s["row"][:, 0:GNN.acc]).then_inc(row_saved, 16)
                act.wait_ge(kv_in_ready, i + 1)
                act.dma_start(m.phi_q[bass.ds(i * P, P), :], s["phi"]).then_inc(phi_saved, 16)
                act.wait_ge(row_saved, i * 16 + 16)
                act.wait_ge(phi_saved, i * 16 + 16)
                act.sem_inc(slots_free, 1)
            act.wait_ge(v_ready, 1)
            act.dma_start(m.table[GNN].rearrange("(b p) w -> p b w", p=P)[:, :, GNN.acc:], m.v[:, :, :]).then_inc(v_saved, 16)
            act.wait_ge(v_saved, 16)

        @block.vector
        def _(dve):
            step = Steps(dve, dve_step)
            step(dve.memset(key, 8191))
            step(dve.memset(pack[GNN], 0))
            step(dve.memset(pack[FFN], 0))
            step(dve.memset(fill, NO_LANE))
            step(dve.memset(x[96:P, NB - 1, :], 0.0))
            step(dve.memset(one, 1.0))
            step(dve.memset(m.ones[:, :], 1.0))
            step(dve.memset(m.kv[:, :, :], 0.0))
            step(dve.memset(s["v"], 1.0))
            step(dve.memset(s["row"], 1.0))
            dve.memset(pos[GNN], NOWHERE).then_inc(pads_ready, 1)
            step(dve.memset(pos[FFN], NOWHERE))
            dve.wait_ge(iota_ready, 4)
            step(dve.tensor_copy(m.iota_n[:, :], m.iota_n[:, :].bitcast(I32)))
            step(dve.tensor_copy(m.before[:, :], m.before[:, :].bitcast(I32)))
            step(dve.tensor_copy(iota_f, m.iota_n[:, 0:NB]))
            step(dve.tensor_copy(s["iota_s"], s["iota_s"].bitcast(I32)))
            step(dve.tensor_scalar(m.ident[:, :], m.before[:, :], 0.0, None, ALU.is_equal))
            step(dve.tensor_copy(m.ident_b[:, :], m.ident[:, :]))
            step(dve.tensor_scalar(m.before[:, :], m.before[:, :], 0.0, None, ALU.is_gt))
            step(dve.memset(m.node_of[:, :], 1.0))
            step(dve.tensor_copy(s["lane_in"], s["iota_p"].bitcast(I32)))
            step(dve.tensor_scalar(m.node_of[:, NB - 1:NB], s["lane_in"], float(LAST), None, ALU.is_lt))
            step(dve.tensor_scalar(s["iota_p"].bitcast(I32), s["iota_p"].bitcast(I32), 5, None, ALU.arith_shift_right))
            step(dve.tensor_copy(s["lane_in"], s["iota_p"].bitcast(I32)))
            step(dve.tensor_copy(m.head_mask[:, :].bitcast(I32), m.iota_n[:, :]))
            step(dve.tensor_scalar(m.head_mask[:, :].bitcast(I32), m.head_mask[:, :].bitcast(I32), 5, None, ALU.arith_shift_right))
            step(dve.tensor_copy(m.head_mask[:, :], m.head_mask[:, :].bitcast(I32)))
            step(dve.tensor_scalar(m.head_mask[:, :], m.head_mask[:, :], s["lane_in"], None, ALU.is_equal))
            step(dve.tensor_scalar(m.head_of[:, :], m.iota_n[:, 0:H], s["lane_in"], None, ALU.is_equal))
            dve.wait_ge(pads_ready, 1)
            for gi, g in enumerate((GNN, FFN)):
                c = g.cp
                dve.wait_ge(edges_in[gi], (64, 32)[gi])
                step(dve.tensor_scalar(scani[:, 0:c], key[:, 0:c], 7, None, ALU.arith_shift_right))
                step(dve.tensor_copy(blk[:, 0:c], scani[:, 0:c]))
                step(dve.tensor_scalar(pack[g], pack[g], float(N - 1), 256.0, ALU.min, ALU.mult))
                step(dve.tensor_scalar(scani[:, 0:c], key[:, 0:c], P - 1, None, ALU.bitwise_and))
                step(dve.tensor_tensor(pack[g], pack[g], scani[:, 0:c], ALU.add))
                if gi == 0:
                    dve.memset(key[:, FFN.c:FFN.cp], 8191).then_inc(key_free, 1)
                with dve.Fori(0, NB) as b:
                    step.enter(b, 1)
                    step(dve.tensor_scalar(mask[:, 0:c], blk[:, 0:c], iota_f[:, bass.ds(b, 1)], 0.0, ALU.is_equal,
                                           ALU.add, accum_out=tot[:, bass.ds(b, 1)]))
                    step.leave(NB)
                dve.sem_inc(totals_ready, 1)
                dve.wait_ge(sums_ready, gi + 1)
                step(dve.tensor_scalar(padi, ps_s[:, 64:64 + NB], float(GE - 1), None, ALU.add))
                step(dve.tensor_scalar(padi, padi, GE.bit_length() - 1, GE.bit_length() - 1, ALU.arith_shift_right,
                                       ALU.logical_shift_left))
                step(dve.tensor_copy(totall, padi))
                step(dve.tensor_tensor_scan(m.ends[:, gi, :], m.ones[:, 0:NB], totall, 0.0, ALU.mult, ALU.add))
                step(dve.tensor_tensor(starts, m.ends[:, gi, :], totall, ALU.subtract))
                step(dve.scalar_tensor_tensor(m.sinit[:, gi, :], starts, -1.0, ps_s[:, 0:NB], ALU.add, ALU.add))
                with dve.Fori(0, NB) as b:
                    step.enter(b, 3)
                    step(dve.tensor_scalar(mask[:, 0:c], blk[:, 0:c], iota_f[:, bass.ds(b, 1)], None, ALU.is_equal))
                    step(dve.tensor_tensor_scan(scan[:, 0:c], one[:, 0:c], mask[:, 0:c],
                                                m.sinit[:, gi, bass.ds(b, 1)], ALU.mult, ALU.add))
                    alone(dve)
                    step(dve.copy_predicated(pos[g], mask[:, 0:c].bitcast(U16), scan[:, 0:c]))
                    step.leave(NB)
                dve.tensor_copy(pos[g].bitcast(I32), pos[g]).then_inc(places_ready, 1)
                count = s["count"][0:1, 0:g.s]
                step(dve.memset(count, 0.0))
                with dve.Fori(0, NB) as b:
                    step.enter(b, 1)
                    step(dve.scalar_tensor_tensor(count, s["iota_s"][0:1, 0:g.s], m.ends[0:1, gi, bass.ds(b, 1)],
                                                  count, ALU.is_ge, ALU.add))
                    step.leave(NB)
                step(dve.tensor_copy(m.block_of[g][:, :], count))
                count = count.rearrange("p (i u) -> p i u", u=U)
                for u in reversed(range(1, U)):
                    step(dve.scalar_tensor_tensor(count[:, :, u - 1], count[:, :, u], float(BASE), count[:, :, u - 1], ALU.mult, ALU.add))
                step(dve.tensor_copy(m.blocks_of[g][:, :], count[:, :, 0]))

            dve.wait_ge(x_in, 32)
            halves = m.att[:, :, 0:6]
            with dve.Fori(0, NB) as b:
                step.enter(b, 1)
                step(dve.bn_stats(m.att[:, bass.ds(b, 1), 0:6].rearrange("p o d -> p (o d)"),
                                  x[:, bass.ds(b, 1), :].rearrange("p o d -> p (o d)")))
                step.leave(NB)
            mean_var(dve, step, halves, m.stats[:, :, 0], m.rstd[:, :], m.stats[:, :, 1])
            dve.tensor_scalar(m.rstd[:, :], m.rstd[:, :], EPS, None, ALU.add).then_inc(var_ready, 1)
            dve.wait_ge(std_ready, 1)
            step(dve.reciprocal(m.rstd[:, :], m.rstd[:, :]))
            dve.wait_ge(weights_in, 16 * 10)
            with dve.Fori(0, NB) as i:
                step.enter(i, 8)
                one_of = bass.ds(i, 1)
                dve.tensor_scalar(s["xn"], x[:, one_of, :].rearrange("p o d -> p (o d)"), m.stats[:, one_of, 0],
                                  m.rstd[:, one_of], ALU.subtract, ALU.mult).then_inc(xn_ready, 1)
                dve.wait_ge(products_ready, i + 1)
                dve.wait_ge(slots_free, i + 1)
                step(dve.tensor_tensor(row[:, :, 0:DH], ps_w[:, 0:D].rearrange("p (h d) -> p h d", h=H),
                                       w["bias"][:, 0:D].rearrange("p (h d) -> p h d", h=H), ALU.add))
                step(dve.tensor_tensor(s["k"], ps_w[:, D:2 * D], w["bias"][:, D:2 * D], ALU.add))
                step(dve.tensor_tensor(vrow[:, :, 0:P], ps_v.rearrange("p (j w) -> p j w", j=2),
                                       w["bias"][:, 2 * D:].rearrange("p (j w) -> p j w", j=2), ALU.add))
                step(dve.tensor_scalar(s["v"], s["v"], m.node_of[:, one_of], None, ALU.mult))
                step(dve.tensor_scalar(s["neg"][:, 0:D], s["k"], 0.0, None, ALU.min))
                for j in range(2):
                    c = slice(j * P, (j + 1) * P)
                    step(dve.tensor_scalar(s["qpos"][:, c], ps_q[:, c], w["bq"][:, j:j + 1], 0.0, ALU.add, ALU.max))
                dve.tensor_scalar(s["neg"][:, D:D + P], ps_q[:, 0:P], w["bq"][:, 0:1], 0.0, ALU.add, ALU.min)
                dve.tensor_scalar(s["neg"][:, D + P:], ps_q[:, P:], w["bq"][:, 1:2], 0.0, ALU.add, ALU.min).then_inc(neg_ready, 1)
                for j, signals in ((0, row_ready), (1, prod_ready)):
                    c = slice(j * D, (j + 1) * D)
                    dve.tensor_tensor(s["prod"][:, c].rearrange("p (h d) -> p h d", h=H), row[:, :, 0:DH],
                                      w["a"][:, c].rearrange("p (h d) -> p h d", h=H), ALU.mult).then_inc(signals, 1)
                dve.wait_ge(row_ready, i + 1)
                dve.wait_ge(prod_ready, i + 1)
                dve.tensor_reduce(m.att[:, one_of, :], s["prod"].rearrange("p (g d) -> p g d", d=DH), AX.X, ALU.add)
                dve.wait_ge(exp_ready, i + 1)
                step(dve.scalar_tensor_tensor(s["k"], s["k"], 0.0, s["neg"][:, 0:D], ALU.max, ALU.add))
                dve.tensor_tensor(s["phi"], s["qpos"], s["neg"][:, D:], ALU.add).then_inc(kv_in_ready, 1)
                dve.wait_ge(kv_made, i + 1)
                dve.tensor_tensor(m.kv[:, :, :], m.kv[:, :, :], ps_kv, ALU.add).then_inc(products_read, 1)
                dve.wait_ge(products_read, i + 1)
                step.leave(NB)
            least_v(dve, m, ps_s, least, v_ready, step)

        @block.tensor
        def _(pe):
            for gi in range(2):
                pe.wait_ge(totals_ready, gi + 1)
                nc.tensor.matmul(ps_s[:, 0:NB], m.before[:, :], tot, start=True, stop=True)
                nc.tensor.matmul(ps_s[:, 64:64 + NB], m.ones[:, :], tot, start=True, stop=True).then_inc(sums_ready, 1)
            pe.wait_ge(weights_in, 16 * 10)
            with pe.Fori(0, NB) as i:
                pe.wait_ge(xn_ready, i + 1)
                for k in range(2):
                    c = slice(k * P, (k + 1) * P)
                    last = nc.tensor.transpose(ps_t[:, c], s["xn"][:, c], m.ident[:, :])
                last.then_inc(turned, 1)
                pe.wait_ge(xnt_ready, i + 1)
                for k in range(2):
                    c, st = slice(k * P, (k + 1) * P), dict(start=k == 0, stop=k == 1)
                    nc.tensor.matmul(ps_w[:, 0:D], s["xnt"][:, c], wt[:, k, :], **st)
                for k in range(2):
                    c, st = slice(k * P, (k + 1) * P), dict(start=k == 0, stop=k == 1)
                    nc.tensor.matmul(ps_w[:, D:], s["xnt"][:, c], wk[:, k, :], **st)
                for k in range(2):
                    c, st = slice(k * P, (k + 1) * P), dict(start=k == 0, stop=k == 1)
                    nc.tensor.matmul(ps_v, s["xnt"][:, c], wv[:, k, :], **st)
                for j in range(2):
                    for k in range(2):
                        c, st = slice(k * P, (k + 1) * P), dict(start=k == 0, stop=k == 1)
                        last = nc.tensor.matmul(ps_q[:, j * P:(j + 1) * P], wq[:, k, j * P:(j + 1) * P], s["xnt"][:, c], **st)
                last.then_inc(products_ready, 1)
                pe.wait_ge(kv_in_ready, i + 1)
                for j in range(2):
                    last = nc.tensor.matmul(ps_kv[:, j, :], s["k"][:, j * P:(j + 1) * P], vrow[:, j, :], start=True, stop=True)
                last.then_inc(kv_made, 1)
            least_v_products(nc, pe, m, ps_s, least)


def graph_groups(nc, m, g, sem):
    lists = region(m.weights, [("raw", g.s * TG), ("lane", g.s * TG), ("index", g.s * TG)])
    raw, index, lane = lists["raw"].bitcast(I32), lists["index"].bitcast(I32), lists["lane"]
    list_in, dve_step = sem(g.name + "_list_in"), sem(g.name + "_list_step")

    with nc.Block() as block:
        @block.sync
        def _(sp):
            sp.dma_start(raw.rearrange("p (s t) -> p s t", t=TG),
                         m.sorted[g].rearrange("(s p t) o -> p s (t o)", p=P, t=TG)).then_inc(list_in, 16)

        @block.vector
        def _(dve):
            step = Steps(dve, dve_step)
            dve.wait_ge(list_in, 16)
            lane_i = lane.bitcast(I32)
            step(dve.tensor_scalar(index, raw, 8, None, ALU.arith_shift_right))
            step(dve.tensor_scalar(lane_i, raw, 255, None, ALU.bitwise_and))
            step(dve.tensor_copy(lane, lane_i))

    shared = {}

    def own(name):
        if name not in shared:
            shared[name] = sem(f"{g.name}_{name}")
        return shared[name]

    near, far = groups_near(nc, m, g, own, index, lane), groups_far(nc, m, g, own, index, lane)

    with nc.Block() as block:
        def either(eng, name):
            with eng.If(eng.value_load(m.near[0:1, 0:1], min_val=0, max_val=1) == 1):
                near[name](eng)
            with eng.Else():
                far[name](eng)

        @block.gpsimd
        def _(pool):
            either(pool, "pool")

        @block.scalar
        def _(act):
            either(act, "act")

        @block.vector
        def _(dve):
            either(dve, "dve")

        @block.tensor
        def _(pe):
            either(pe, "pe")


def groups_near(nc, m, g, n, index, lane):
    groups, trips, W = g.s, g.s // U, g.wh + 1
    s = region(m.slots, [(f"rows{u}", TG * g.row) for u in range(U)] + [(f"one_hot{u}", TG * P) for u in range(U)]
               + [(f"one_hot_b{o}", TG * P // 2) for o in range(2)] + [(f"one_hot_t{o}", TG * P // 2) for o in range(2)]
               + [(f"index{u}", TG) for u in range(U)] + [(f"z{o}", TG * 2 * H) for o in range(2)]
               + [(f"weight{o}", TG * H) for o in range(2)])
    rows = [s[f"rows{u}"].rearrange("p (t w) -> p t w", t=TG) for u in range(U)]
    one_hot = [s[f"one_hot{u}"].rearrange("p (t n) -> p t n", t=TG) for u in range(U)]
    one_hot_b, one_hot_t = ([s[f"{n}{o}"].bitcast(BF16).rearrange("p (t n) -> p t n", t=TG) for o in range(2)]
                            for n in ("one_hot_b", "one_hot_t"))
    slot_index = [s[f"index{u}"].bitcast(I32) for u in range(U)]
    z = [s[f"z{o}"] for o in range(2)]
    z3 = [x.rearrange("p (t c) -> p t c", t=TG) for x in z]
    weight = [s[f"weight{o}"].rearrange("p (t h) -> p t h", t=TG) for o in range(2)]
    acc = m.acc[:, :].rearrange("p (b w) -> p b w", w=GNN.acc) if g is GNN else m.acc_f[:, :, :]
    ps_t = [m.four[:, o * 512:o * 512 + TG * P // 2].bitcast(BF16).rearrange("p (t n) -> p t n", t=TG) for o in range(2)]
    ps_e = [m.four[:, (2 + o) * 512:(2 + o) * 512 + TG * 2 * H].rearrange("p (t c) -> p t c", t=TG) for o in range(2)]
    ps_sum = [m.ps[o][:, 0:g.acc] for o in range(2)]

    indexed, gathered = n("indexed"), [n(f"gathered{u}") for u in range(U)]
    one_hot_ready, one_hot_b_ready, turned, one_hot_t_ready, terms_at_edges, z_ready, exp_ready = (n(x) for x in (
        "one_hot_ready", "one_hot_b_ready", "turned", "one_hot_t_ready", "terms_at_edges", "z_ready", "exp_ready"))
    weight_ready, messages_ready, summed, added = (n(x) for x in ("weight_ready", "messages_ready", "summed", "added"))
    start_step, loop_ready, loop_exp = n("start_step"), n("loop_ready"), n("loop_exp")

    def loop(eng, group, peel_first=False):
        first = int(peel_first)
        for i in range(first):
            for u in range(U):
                group(i, u, lambda ahead: True)
        with eng.Fori(first, trips - 1) as i:
            for u in range(U):
                group(i, u, lambda ahead: True)
        for u in range(U):
            group(trips - 1, u, lambda ahead: u + ahead < U)

    def pool(eng):
        def gather(i, u, more):
            eng.wait_ge(indexed, i * U + u + 1)
            alone(eng)
            if not isinstance(i, int) or i:
                eng.wait_ge(summed, (i - 1) * U + u + 1)
                alone(eng)
            for t in range(TG):
                eng.indirect_dma_start(out=rows[u][:, t, :], out_offset=None, in_=m.table[g],
                                       in_offset=bass.IndirectOffsetOnAxis(ap=slot_index[u][:, t:t + 1], axis=0)
                                       ).then_inc(gathered[u], 16)
        loop(eng, gather, peel_first=True)

    def act(eng):
        def one_hots(k, u):
            o = u % 2
            eng.wait_ge(one_hot_ready, k + 1)
            eng.copy(one_hot_b[o], one_hot[u]).then_inc(one_hot_b_ready, 1)
            eng.wait_ge(turned, k + 1)
            eng.copy(one_hot_t[o], ps_t[o]).then_inc(one_hot_t_ready, 1)

        def exponentials(k, o):
            eng.wait_ge(z_ready, k + 1)
            eng.activation(z[o], z[o], ACT.Exp).then_inc(exp_ready, 1)

        def indices(i, u):
            eng.copy(slot_index[u], index[:, bass.ds((i * U + u) * TG, TG)]).then_inc(indexed, 1)

        def group(i, u, more):
            k = i * U + u
            if more(2):
                exponentials(k + 2, u % 2)
            if more(3):
                one_hots(k + 3, (u + 3) % U)
            if more(U):
                eng.wait_ge(gathered[u], i * (16 * TG) + 16 * TG)
                alone(eng)
                indices(i + 1, u)

        for u in range(U):
            indices(0, u)
        if g is FFN:
            eng.wait_ge(loop_ready, 1)
            eng.activation(m.att[:, :, :], m.att[:, :, :], ACT.Exp).then_inc(loop_exp, 1)
        one_hots(0, 0)
        one_hots(1, 1)
        exponentials(0, 0)
        one_hots(2, 2)
        exponentials(1, 1)
        loop(eng, group)

    def dve(eng):
        def one_hots(k, u):
            lanes = lane[:, bass.ds(k * TG, TG)].unsqueeze(2).broadcast_to([P, TG, P])
            eng.tensor_tensor(one_hot[u], m.iota_n[:, :].unsqueeze(1).broadcast_to([P, TG, P]), lanes,
                              ALU.is_equal).then_inc(one_hot_ready, 1)

        def exponents(k, u, arrivals):
            o = u % 2
            eng.wait_ge(terms_at_edges, k + 1)
            eng.wait_ge(gathered[u], arrivals * (16 * TG))
            eng.tensor_tensor(z3[o], rows[u][:, :, g.acc:], ps_e[o], ALU.add).then_inc(z_ready, 1)

        def messages(k, u):
            o = u % 2
            eng.wait_ge(exp_ready, k + 1)
            eng.tensor_tensor(weight[o], z3[o][:, :, 0:H], z3[o][:, :, H:], ALU.max).then_inc(weight_ready, 1)
            eng.wait_ge(weight_ready, k + 1)
            msg = rows[u][:, :, 0:g.acc].rearrange("p t (h w) -> p t h w", h=H)
            eng.tensor_tensor(msg, msg, weight[o].unsqueeze(3).broadcast_to([P, TG, H, W]), ALU.mult).then_inc(messages_ready, 1)

        def add(k, o, b):
            at = acc[:, bass.ds(b, 1), :].rearrange("p o w -> p (o w)")
            eng.wait_ge(summed, k + 1)
            if not isinstance(k, int) or k:
                eng.wait_ge(added, k)
            eng.tensor_tensor(at, at, ps_sum[o], ALU.add).then_inc(added, 1)

        def group(i, u, more):
            nonlocal word
            k = i * U + u
            if u == 0:
                word = eng.value_load(m.blocks_of[g][0:1, bass.ds(i, 1)], min_val=0, max_val=BASE ** U - 1)
            if more(3):
                one_hots(k + 3, (u + 3) % U)
            if more(2):
                exponents(k + 2, (u + 2) % U, i + 1 + (u + 2) // U)
            add(k, u % 2, word // BASE ** u % BASE)
            if more(1):
                messages(k + 1, (u + 1) % U)

        word = None
        step = Steps(eng, start_step)
        if g is GNN:
            step(eng.memset(m.acc[:, :], 0.0))
        else:
            own = m.acc_f[:, 0:NB, :].rearrange("p b (h w) -> p b h w", h=H)
            loops = m.att[:, :, :]
            eng.tensor_tensor(loops, m.both[:, :, :], m.v[:, :, :], ALU.add).then_inc(loop_ready, 1)
            step(eng.memset(m.acc_f[:, :, :], 1.0))
            for h in range(H):
                step(eng.tensor_copy(own[:, :, h, 0:g.wh], m.h2[:, :, h * g.wh:(h + 1) * g.wh]))
            eng.wait_ge(loop_exp, 1)
            step(eng.tensor_tensor(loops[:, :, 0:H], loops[:, :, 0:H], loops[:, :, H:], ALU.max))
            step(eng.tensor_tensor(own, own, loops[:, :, 0:H].unsqueeze(3).broadcast_to([P, NB, H, W]), ALU.mult))
        one_hots(0, 0)
        one_hots(1, 1)
        exponents(0, 0, 1)
        one_hots(2, 2)
        exponents(1, 1, 1)
        messages(0, 0)
        loop(eng, group, peel_first=True)

    def pe(eng):
        def turn_and_terms(k, u, b):
            o = u % 2
            eng.wait_ge(one_hot_b_ready, k + 1)
            for t in range(TG):
                last = nc.tensor.transpose(ps_t[o][:, t, :], one_hot_b[o][:, t, :], m.ident_b[:, :])
            last.then_inc(turned, 1)
            eng.wait_ge(one_hot_t_ready, k + 1)
            if not isinstance(k, int) or k >= 2:
                eng.wait_ge(z_ready, k - 1)
            for t in range(TG):
                for c in range(3):
                    last = nc.tensor.matmul(ps_e[o][:, t, :], one_hot_t[o][:, t, :],
                                            m.terms[:, bass.ds(b, 1), c, :].rearrange("p o w -> p (o w)"),
                                            start=c == 0, stop=c == 2)
            last.then_inc(terms_at_edges, 1)

        def sums(k, u):
            eng.wait_ge(messages_ready, k + 1)
            for t in range(TG):
                last = nc.tensor.matmul(ps_sum[u % 2], one_hot[u][:, t, :], rows[u][:, t, 0:g.acc], start=t == 0, stop=t == TG - 1)
            last.then_inc(summed, 1)

        def group(i, u, more):
            nonlocal word
            k = i * U + u
            if u == 0:
                word = eng.value_load(m.blocks_of[g][0:1, bass.ds(i, 1)], min_val=0, max_val=BASE ** U - 1)
            turn_and_terms(k, u, word // BASE ** u % BASE)
            if not isinstance(k, int) or k >= 2:
                sums(k - 2, (u - 2) % U)

        word = None
        loop(eng, group, peel_first=True)
        for k in (groups - 2, groups - 1):
            sums(k, k % U)

    return dict(pool=pool, act=act, dve=dve, pe=pe)


def groups_far(nc, m, g, n, index, lane):
    groups, W = g.s, g.wh + 1
    s = region(m.slots, [(f"rows{u}", TG * g.row) for u in range(U)] + [(f"one_hot{o}", TG * P) for o in range(2)]
               + [(f"one_hot_t{o}", TG * P) for o in range(2)] + [(f"one_hot_b{o}", TG * P // 2) for o in range(2)]
               + [("spread", TG * H * P // 2)] + [(f"index{u}", TG) for u in range(U)]
               + [("term", 2 * H), ("scale", H), ("gmax", H), ("z", TG * H), ("weight", TG * H)])
    rows = [s[f"rows{u}"].rearrange("p (t w) -> p t w", t=TG) for u in range(U)]
    one_hot = [s[f"one_hot{o}"].rearrange("p (t n) -> p t n", t=TG) for o in range(2)]
    one_hot_t = [s[f"one_hot_t{o}"].rearrange("p (t n) -> p t n", t=TG) for o in range(2)]
    one_hot_b = [s[f"one_hot_b{o}"].bitcast(BF16).rearrange("p (t n) -> p t n", t=TG) for o in range(2)]
    spread = s["spread"].bitcast(BF16).rearrange("p (t h e) -> p t h e", t=TG, h=H)
    slot_index = [s[f"index{u}"].bitcast(I32) for u in range(U)]
    term, scale, gmax, z, weight = (s[n] for n in ("term", "scale", "gmax", "z", "weight"))
    z3, weight3 = z.rearrange("p (t h) -> p t h", h=H), weight.rearrange("p (t h) -> p t h", h=H)
    acc = m.acc[:, :].rearrange("p (b w) -> p b w", w=GNN.acc) if g is GNN else m.acc_f[:, :, :]
    ps_max = m.four[:, :].rearrange("p (t h e) -> p h t e", t=TG, h=H)
    ps_t, ps_e, ps_sum = m.ps[0], m.ps[1][:, 0:TG * 2 * H].rearrange("p (t c) -> p t c", t=TG), m.ps[2][:, 0:g.acc]

    indexed, gathered = n("indexed"), [n(f"gathered{u}") for u in range(U)]
    one_hot_ready, one_hot_b_ready, turned, one_hot_t_ready = (n(x) for x in (
        "one_hot_ready", "one_hot_b_ready", "turned", "one_hot_t_ready"))
    spread_ready, max_ready, term_ready, scale_ready, terms_at_edges = (n(x) for x in (
        "spread_ready", "max_ready", "term_ready", "scale_ready", "terms_at_edges"))
    e_ready, weight_ready, messages_ready, summed, dve_step = (n(x) for x in (
        "e_ready", "weight_ready", "messages_ready", "summed", "dve_step"))
    trips = groups // U

    def pool_program(pool):
        def gather(i, u, free):
            pool.wait_ge(indexed, i * U + u + 1)
            alone(pool)
            if free:
                pool.wait_ge(summed, i * U + u - U + 1)
                alone(pool)
            for t in range(TG):
                pool.indirect_dma_start(out=rows[u][:, t, :], out_offset=None, in_=m.table[g],
                                        in_offset=bass.IndirectOffsetOnAxis(ap=slot_index[u][:, t:t + 1], axis=0)
                                        ).then_inc(gathered[u], 16)

        for u in range(U):
            gather(0, u, False)
        with pool.Fori(1, trips) as i:
            for u in range(U):
                gather(i, u, True)

    def act_program(act):
        def one_hots(k, o):
            act.wait_ge(one_hot_ready, k + 1)
            act.copy(one_hot_b[o], one_hot[o]).then_inc(one_hot_b_ready, 1)

        def turned_out(k, o):
            act.wait_ge(turned, k + 1)
            act.copy(one_hot_t[o], ps_t[:, :].rearrange("p (t n) -> p t n", t=TG)).then_inc(one_hot_t_ready, 1)

        def group(i, u, last=False):
            k, o = i * U + u, (u + 1) % 2
            act.wait_ge(term_ready, k + 1)
            act.activation(scale, scale, ACT.Exp).then_inc(scale_ready, 1)
            if not last:
                one_hots(k + 1, o)
            act.wait_ge(e_ready, k + 1)
            act.activation(weight, z, ACT.Exp).then_inc(weight_ready, 1)
            if not last:
                turned_out(k + 1, o)

        def indices(i, u):
            act.copy(slot_index[u], index[:, bass.ds((i * U + u) * TG, TG)]).then_inc(indexed, 1)

        for u in range(U):
            indices(0, u)
        one_hots(0, 0)
        turned_out(0, 0)
        with act.Fori(0, trips - 1) as i:
            for u in range(U):
                group(i, u)
                act.wait_ge(gathered[u], i * (16 * TG) + 16 * TG)
                alone(act)
                indices(i + 1, u)
        for u in range(U):
            group(trips - 1, u, last=u == U - 1)

    def dve_program(dve):
        step = Steps(dve, dve_step)
        if g is GNN:
            step(dve.memset(m.acc[:, :], 0.0))
            step(dve.memset(m.mtab[:, :, :], 0.0))
        else:
            own = m.acc_f[:, 0:NB, :].rearrange("p b (h w) -> p b h w", h=H)
            step(dve.memset(m.acc_f[:, :, :], 1.0))
            for h in range(H):
                step(dve.tensor_copy(own[:, :, h, 0:g.wh], m.h2[:, :, h * g.wh:(h + 1) * g.wh]))
            step(dve.memset(m.mtab[:, NB, :], 0.0))
            step(dve.tensor_copy(m.mtab[:, 0:NB, :], m.v[:, :, 0:H]))
        top = m.ttab[:, :, H:]
        step(dve.tensor_tensor(top, m.ttab[:, :, 0:H], m.mtab[:, :, :], ALU.add))
        step(dve.scalar_tensor_tensor(top, top, SLOPE, top, ALU.mult, ALU.max))

        def one_hots(k, o):
            lanes = lane[:, bass.ds(k * TG, TG)].unsqueeze(2).broadcast_to([P, TG, P])
            dve.tensor_tensor(one_hot[o], m.iota_n[:, :].unsqueeze(1).broadcast_to([P, TG, P]), lanes,
                              ALU.is_equal).then_inc(one_hot_ready, 1)

        def spreads(u, tiles, last):
            for t in tiles:
                for h in range(H):
                    ins = dve.tensor_scalar(spread[:, t, h, :], m.ident_b[:, :], rows[u][:, t, g.acc + h:g.acc + h + 1],
                                            None, ALU.mult)
            if last:
                ins.then_inc(spread_ready, 1)

        def group(i, u, last=False):
            k, o = i * U + u, (u + 1) % 2
            b = bass.ds(dve.value_load(m.block_of[g][0:1, bass.ds(k, 1)], min_val=0, max_val=NB), 1)
            old = m.ttab[:, b, H:].rearrange("p o h -> p (o h)")
            own = m.ttab[:, b, 0:H].rearrange("p o h -> p (o h)")
            best = m.mtab[:, b, :].rearrange("p o h -> p (o h)")
            dve.wait_ge(max_ready, k + 1)
            step(dve.tensor_reduce(gmax, ps_max, AX.XY, ALU.max))
            step(dve.tensor_tensor(best, best, gmax, ALU.max))
            step(dve.tensor_tensor(gmax, own, best, ALU.add))
            step(dve.scalar_tensor_tensor(term[:, H:], gmax, SLOPE, gmax, ALU.mult, ALU.max))
            step(dve.tensor_tensor(scale, old, term[:, H:], ALU.subtract))
            alone(dve)
            step(dve.tensor_copy(old, term[:, H:]))
            alone(dve)
            dve.tensor_copy(term[:, 0:H], own).then_inc(term_ready, 1)
            if not last:
                one_hots(k + 1, o)
            dve.wait_ge(terms_at_edges, k + 1)
            step(dve.tensor_tensor(z3, rows[u][:, :, g.acc:g.acc + H], ps_e[:, :, 0:H], ALU.add))
            step(dve.scalar_tensor_tensor(z, z, SLOPE, z, ALU.mult, ALU.max))
            dve.tensor_tensor(z3, z3, ps_e[:, :, H:], ALU.subtract).then_inc(e_ready, 1)
            if not last:
                v = (u + 1) % U
                dve.wait_ge(gathered[v], i * (16 * TG) + 16 * TG * (1 + (u + 1) // U))
                spreads(v, (0,), False)
            dve.wait_ge(weight_ready, k + 1)
            msg = rows[u][:, :, 0:g.acc].rearrange("p t (h w) -> p t h w", h=H)
            for t in range(TG):
                ins = dve.tensor_tensor(msg[:, t], msg[:, t], weight3[:, t, :].unsqueeze(2).broadcast_to([P, H, W]), ALU.mult)
            ins.then_inc(messages_ready, 1)
            if not last:
                spreads(v, range(1, TG), True)
            dve.wait_ge(scale_ready, k + 1)
            sums = acc[:, b, :].rearrange("p o (h w) -> p (o h) w", h=H)
            step(dve.tensor_tensor(sums, sums, scale.unsqueeze(2).broadcast_to([P, H, W]), ALU.mult))
            dve.wait_ge(summed, k + 1)
            step(dve.tensor_tensor(sums, sums, ps_sum.rearrange("p (h w) -> p h w", h=H), ALU.add))

        one_hots(0, 0)
        dve.wait_ge(gathered[0], 16 * TG)
        spreads(0, range(TG), True)
        steps = U * 10
        with dve.Fori(0, trips - 1) as i:
            step.enter(i, steps)
            for u in range(U):
                group(i, u)
            step.leave(trips - 1)
        for u in range(U):
            group(trips - 1, u, last=u == U - 1)

    def pe_program(pe):
        def turn(k, o):
            pe.wait_ge(one_hot_ready, k + 1)
            for t in range(TG):
                last = nc.tensor.transpose(ps_t[:, t * P:(t + 1) * P], one_hot[o][:, t, :], m.ident[:, :])
            last.then_inc(turned, 1)

        def maxima(k, o):
            pe.wait_ge(one_hot_b_ready, k + 1)
            pe.wait_ge(spread_ready, k + 1)
            for t in range(TG):
                last = nc.tensor.matmul(m.four[:, t * H * P:(t + 1) * H * P], one_hot_b[o][:, t, :],
                                        spread[:, t].rearrange("p h e -> p (h e)"), start=True, stop=True)
            last.then_inc(max_ready, 1)

        def group(i, u, last_group=False):
            k, o = i * U + u, u % 2
            pe.wait_ge(term_ready, k + 1)
            pe.wait_ge(one_hot_t_ready, k + 1)
            for t in range(TG):
                last = nc.tensor.matmul(ps_e[:, t, :], one_hot_t[o][:, t, :], term, start=True, stop=True)
            last.then_inc(terms_at_edges, 1)
            if not last_group:
                turn(k + 1, 1 - o)
            pe.wait_ge(messages_ready, k + 1)
            for t in range(TG):
                last = nc.tensor.matmul(ps_sum, one_hot[o][:, t, :], rows[u][:, t, 0:g.acc], start=t == 0, stop=t == TG - 1)
            last.then_inc(summed, 1)
            if not last_group:
                maxima(k + 1, 1 - o)

        turn(0, 0)
        maxima(0, 0)
        with pe.Fori(0, trips - 1) as i:
            for u in range(U):
                group(i, u)
        for u in range(U):
            group(trips - 1, u, last_group=u == U - 1)

    return dict(pool=pool_program, act=act_program, dve=dve_program, pe=pe_program)


def least_v(dve, m, ps, least, v_ready, step):
    ends, own = m.small[:, 0:2 * H], m.ttab[:, 0:NB, 0:H]
    gathered = m.att[:, :, H:].rearrange("p b h -> p h b")
    step(dve.tensor_reduce(ends[:, 0:H], gathered, AX.X, ALU.min))
    step(dve.tensor_reduce(ends[:, H:], gathered, AX.X, ALU.max))
    dve.tensor_scalar(ends[:, H:], ends[:, H:], -1.0, None, ALU.mult).then_inc(least[0], 1)
    dve.wait_ge(least[1], 1)
    step(dve.tensor_reduce(m.small[0:2 * H, 8:9], ps[0:2 * H, 128:256], AX.X, ALU.min))
    dve.tensor_scalar(m.small[0:2 * H, 16:16 + 2 * H], m.ident[0:2 * H, 0:2 * H], m.small[0:2 * H, 8:9], None,
                      ALU.mult).then_inc(least[2], 1)
    dve.wait_ge(least[3], 1)
    step(dve.tensor_copy(m.low[:, :], ps[:, 256:256 + 2 * H]))
    low = m.low[:, 0:H].unsqueeze(1).broadcast_to([P, NB, H])
    step(dve.tensor_tensor(m.v[:, :, 0:H], m.att[:, :, H:], low, ALU.subtract))
    dve.tensor_scalar(m.v[:, :, H:], m.v[:, :, 0:H], SLOPE, None, ALU.mult).then_inc(v_ready, 1)
    step(dve.memset(m.ttab[:, :, :], 0.0))
    step(dve.tensor_tensor(own, m.att[:, :, 0:H], low, ALU.add))
    spread = m.small[:, 24:24 + H]
    step(dve.tensor_tensor(spread, m.low[:, 0:H], m.low[:, H:], ALU.add))
    step(dve.tensor_scalar(spread, spread, -1.0, None, ALU.mult))
    step(dve.tensor_reduce(m.small[:, 28:29], spread, AX.X, ALU.max))
    step(dve.tensor_scalar(m.near[:, :], m.small[0:1, 28:29], SPREAD, None, ALU.is_le))
    top, both, rest = m.mtab[:, 0:NB, :], m.both[:, :, :], m.att[:, :, :]
    step(dve.tensor_tensor(top, own, spread.unsqueeze(1).broadcast_to([P, NB, H]), ALU.add))
    step(dve.scalar_tensor_tensor(top, top, SLOPE, top, ALU.mult, ALU.max))
    step(dve.tensor_tensor(both[:, :, 0:H], own, top, ALU.subtract))
    step(dve.scalar_tensor_tensor(both[:, :, H:], own, SLOPE, top, ALU.mult, ALU.subtract))
    step(dve.memset(m.terms[:, :, :, :], 0.0))
    step(dve.tensor_copy(m.terms[:, 0:NB, 0, :], both))
    step(dve.tensor_tensor(rest, both, m.terms[:, 0:NB, 0, :], ALU.subtract))
    step(dve.tensor_copy(m.terms[:, 0:NB, 1, :], rest))
    step(dve.tensor_tensor(m.terms[:, 0:NB, 2, :], rest, m.terms[:, 0:NB, 1, :], ALU.subtract))
    dve.wait_ge(v_ready, 1)


def least_v_products(nc, pe, m, ps, least):
    pe.wait_ge(least[0], 1)
    nc.tensor.transpose(ps[0:2 * H, 128:256], m.small[:, 0:2 * H], m.ident[:, :]).then_inc(least[1], 1)
    pe.wait_ge(least[2], 1)
    nc.tensor.matmul(ps[:, 256:256 + 2 * H], m.ones[0:2 * H, :], m.small[0:2 * H, 16:16 + 2 * H], start=True,
                     stop=True).then_inc(least[3], 1)


def combine(nc, m, io, sem):
    w = region(m.weights, [("wo", 2 * D), ("bo", D), ("w_gat", 2 * H * NE), ("att", 2 * H * NE), ("table", NB * FFN.row),
                           ("prod", NB * H * NE)])
    s = region(m.slots, [("phi0", D), ("phi1", D), ("mixed", D), ("mixed_t", D), ("x2n", D), ("x2t", D), ("near", D),
                         ("norm", 2 * H), ("den", H), ("mean", 1), ("var", 1), ("room", 1), ("rstd", 1)])
    wo, w_gat = w["wo"].rearrange("p (k n) -> p k n", k=2), w["w_gat"].rearrange("p (k n) -> p k n", k=2)
    acc = m.acc[:, :].rearrange("p (b w) -> p b w", w=GNN.acc)
    wide = m.wide[:, :].rearrange("p (b d) -> p b d", d=D)
    phi = [s["phi0"], s["phi1"]]
    table = w["table"].rearrange("p (b w) -> p b w", b=NB)
    ps_o = m.ps[0][:, 0:2 * (P + H)].rearrange("p (j w) -> p j w", j=2)
    ps_t, ps_r, ps_x, ps_h, ps_s = m.four[:, 0:D], m.four[:, 512:512 + D], m.four[:, 1024:1024 + D], m.ps[1][:, 0:H * NE], m.ps[2]

    weights_in, phi_in, kv_ready = sem("c_weights_in"), [sem("phi_in0"), sem("phi_in1")], sem("kv_ready")
    queried, mixed_ready, mixed_turned, mixed_t_ready, mix_ready = (sem("c_" + x) for x in (
        "queried", "mixed_ready", "mixed_turned", "mixed_t_ready", "mix_ready"))
    var_ready, std_ready, x2n_ready, x2n_turned, x2t_ready, h_ready, h_read = (sem("c_" + x) for x in (
        "var_ready", "std_ready", "x2n_ready", "x2n_turned", "x2t_ready", "h_ready", "h_read"))
    least, v_ready, table_saved, dve_step, table_ready = [sem(f"ffn_least{i}") for i in range(4)], sem("ffn_v_ready"), sem(
        "table_saved"), sem("c_step"), sem("c_table_ready")

    with nc.Block() as block:
        @block.sync
        def _(sp):
            def load_phi(i, o):
                sp.dma_start(phi[o], m.phi_q[bass.ds(i * P, P), :]).then_inc(phi_in[o], 16)

            load_phi(0, 0)
            load_phi(1, 1)
            sp.dma_start(wo, io["wo"].rearrange("(k p) n -> p k n", p=P)).then_inc(weights_in, 16)
            sp.dma_start(w["bo"], bcast(io["bo"], P)).then_inc(weights_in, 16)
            sp.dma_start(w_gat, io["W_gat"].rearrange("(k p) n -> p k n", p=P)).then_inc(weights_in, 16)
            for i, n in enumerate(("att_dst", "att_src")):
                c = slice(i * H * NE, (i + 1) * H * NE)
                sp.dma_start(w["att"][:, c], bcast(io[n].rearrange("h d -> (h d)"), P)).then_inc(weights_in, 16)
            with sp.Fori(0, (NB - 3) // 2) as i:
                for o in range(2):
                    sp.wait_ge(queried, i * 2 + o + 1)
                    load_phi(i * 2 + o + 2, o)
            sp.wait_ge(queried, NB - 2)
            load_phi(NB - 1, 0)
            sp.wait_ge(table_ready, 1)
            sp.dma_start(m.table[FFN].rearrange("(b p) w -> p b w", p=P), table).then_inc(table_saved, 16)
            sp.wait_ge(table_saved, 16)

        @block.scalar
        def _(act):
            with act.Fori(0, NB) as i:
                act.wait_ge(mixed_turned, i + 1)
                act.copy(s["mixed_t"], ps_t).then_inc(mixed_t_ready, 1)
                act.wait_ge(var_ready, i + 1)
                act.activation(s["rstd"], s["var"], ACT.Sqrt).then_inc(std_ready, 1)
                act.wait_ge(x2n_turned, i + 1)
                act.copy(s["x2t"], ps_x).then_inc(x2t_ready, 1)
                act.wait_ge(x2t_ready, i + 1)
                act.copy(wide[:, bass.ds(i, 1), :].rearrange("p o d -> p (o d)"), s["x2t"])

        @block.vector
        def _(dve):
            step = Steps(dve, dve_step)
            for j in range(2):
                step(dve.tensor_tensor(m.kvm[:, j, 0:P], m.kv[:, j, 0:P], m.head_mask[:, :], ALU.mult))
                step(dve.tensor_scalar(m.kvm[:, j, P:], m.head_of[:, :], m.kv[:, j, P:], None, ALU.mult))
            dve.sem_inc(kv_ready, 1)
            dve.wait_ge(weights_in, 16 * 5)
            with dve.Fori(0, NB) as i:
                step.enter(i, 16)
                b = bass.ds(i, 1)
                sums = acc[:, b, :].rearrange("p o (h w) -> p (o h) w", h=H)
                x2 = acc[:, b, 0:D].rearrange("p o d -> p (o d)")
                near = s["near"].rearrange("p (h d) -> p h d", h=H)
                step(dve.tensor_scalar(s["den"], sums[:, :, DH], 1e-30, None, ALU.max))
                step(dve.reciprocal(s["den"], s["den"]))
                step(dve.tensor_tensor(near, sums[:, :, 0:DH], s["den"].unsqueeze(2).broadcast_to([P, H, DH]), ALU.mult))
                step(dve.tensor_tensor(s["near"], s["near"], wide[:, b, :].rearrange("p o d -> p (o d)"), ALU.add))
                step(dve.tensor_tensor(s["near"], s["near"], w["bo"], ALU.add))
                dve.wait_ge(queried, i + 1)
                norm = s["norm"].rearrange("p (j h) -> p j h", j=2)
                step(dve.tensor_scalar(norm, ps_o[:, :, P:], 1e-6, None, ALU.add))
                step(dve.reciprocal(s["norm"], s["norm"]))
                for j in range(2):
                    ins = dve.tensor_tensor(s["mixed"][:, j * P:(j + 1) * P].rearrange("p (h d) -> p h d", d=MD),
                                            ps_o[:, j, 0:P].rearrange("p (h d) -> p h d", d=MD),
                                            norm[:, j, :].unsqueeze(2).broadcast_to([P, H, MD]), ALU.mult)
                ins.then_inc(mixed_ready, 1)
                dve.wait_ge(mix_ready, i + 1)
                step(dve.tensor_tensor(x2, s["near"], ps_r, ALU.add))
                alone(dve)
                step(dve.bn_stats(m.bn[:, :], x2))
                halves = m.bn[:, :].unsqueeze(1)
                mean_var(dve, step, halves, s["mean"], s["var"], s["room"])
                dve.tensor_scalar(s["var"], s["var"], EPS, None, ALU.add).then_inc(var_ready, 1)
                dve.wait_ge(std_ready, i + 1)
                step(dve.reciprocal(s["rstd"], s["rstd"]))
                dve.tensor_scalar(s["x2n"], x2, s["mean"], s["rstd"], ALU.subtract, ALU.mult).then_inc(x2n_ready, 1)
                dve.wait_ge(h_ready, i + 1)
                alone(dve)
                dve.tensor_copy(m.h2[:, b, :].rearrange("p o d -> p (o d)"), ps_h).then_inc(h_read, 1)
                step.leave(NB)
            dve.wait_ge(h_read, NB)
            prod = w["prod"].rearrange("p (b h e) -> p b h e", b=NB, h=H)
            h2 = m.h2[:, :, :].rearrange("p b (h e) -> p b h e", h=H)
            for j in range(2):
                a = w["att"][:, j * H * NE:(j + 1) * H * NE].unsqueeze(1).broadcast_to([P, NB, H * NE])
                step(dve.tensor_tensor(w["prod"].rearrange("p (b c) -> p b c", b=NB), m.h2[:, :, :], a, ALU.mult))
                step(dve.tensor_reduce(m.att[:, :, j * H:(j + 1) * H], prod, AX.X, ALU.add))
            least_v(dve, m, ps_s, least, v_ready, step)
            step(dve.memset(w["table"], 1.0))
            for h in range(H):
                step(dve.tensor_copy(table[:, :, h * (FFN.wh + 1):h * (FFN.wh + 1) + FFN.wh], h2[:, :, h, :]))
            dve.tensor_copy(table[:, :, FFN.acc:], m.v[:, :, :]).then_inc(table_ready, 1)

        @block.tensor
        def _(pe):
            pe.wait_ge(kv_ready, 1)
            pe.wait_ge(weights_in, 16 * 5)

            def tile(i, o, n):
                pe.wait_ge(phi_in[o], n)
                for j in range(2):
                    last = nc.tensor.matmul(ps_o[:, j, :], phi[o][:, j * P:(j + 1) * P], m.kvm[:, j, :], start=True, stop=True)
                last.then_inc(queried, 1)
                pe.wait_ge(mixed_ready, i + 1)
                for k in range(2):
                    last = nc.tensor.transpose(ps_t[:, k * P:(k + 1) * P], s["mixed"][:, k * P:(k + 1) * P], m.ident[:, :])
                last.then_inc(mixed_turned, 1)
                pe.wait_ge(mixed_t_ready, i + 1)
                for k in range(2):
                    last = nc.tensor.matmul(ps_r, s["mixed_t"][:, k * P:(k + 1) * P], wo[:, k, :], start=k == 0, stop=k == 1)
                last.then_inc(mix_ready, 1)
                pe.wait_ge(x2n_ready, i + 1)
                for k in range(2):
                    last = nc.tensor.transpose(ps_x[:, k * P:(k + 1) * P], s["x2n"][:, k * P:(k + 1) * P], m.ident[:, :])
                last.then_inc(x2n_turned, 1)
                pe.wait_ge(x2t_ready, i + 1)
                for k in range(2):
                    last = nc.tensor.matmul(ps_h, s["x2t"][:, k * P:(k + 1) * P], w_gat[:, k, :], start=k == 0, stop=k == 1)
                last.then_inc(h_ready, 1)

            with pe.Fori(0, NB // 2) as i:
                for o in range(2):
                    tile(i * 2 + o, o, i * 16 + 16)
            tile(NB - 1, 0, 16 * (NB // 2) + 16)
            least_v_products(nc, pe, m, ps_s, least)


def score(nc, m, io, sem):
    K = H * NE
    s = region(m.slots, [("agg", NB * K), ("sq", NB * K), ("den", NB * H), ("mean", NB), ("rstd", NB), ("scores", NB * NE),
                         ("beaten", NB * NE), ("one", NB), ("top", NB), ("e", NB * NE), ("b_gat", K), ("gamma", K), ("beta", K)])
    agg4 = s["agg"].rearrange("p (b h e) -> p b h e", b=NB, h=H)
    agg, sq = (s[n].rearrange("p (b k) -> p b k", b=NB) for n in ("agg", "sq"))
    scores, beaten, e = (s[n].rearrange("p (b e) -> p b e", b=NB) for n in ("scores", "beaten", "e"))
    params_in, var_ready, std_ready, dve_step = (sem("s_" + x) for x in ("params_in", "var_ready", "std_ready", "step"))
    gap_ready, exp_ready = sem("s_gap_ready"), sem("s_exp_ready")

    def wide(ap):
        return ap.unsqueeze(1).broadcast_to([P, NB, K])

    def each(ap, n):
        return ap.unsqueeze(2).broadcast_to([P, NB, n])

    with nc.Block() as block:
        @block.sync
        def _(sp):
            for n, k in (("b_gat", "b_gat"), ("gamma", "ln_gamma"), ("beta", "ln_beta")):
                sp.dma_start(s[n], bcast(io[k], P)).then_inc(params_in, 16)

        @block.scalar
        def _(act):
            act.wait_ge(var_ready, 1)
            act.activation(s["rstd"], s["rstd"], ACT.Sqrt).then_inc(std_ready, 1)
            act.wait_ge(gap_ready, 1)
            act.activation(s["e"], s["e"], ACT.Exp).then_inc(exp_ready, 1)

        @block.vector
        def _(dve):
            step = Steps(dve, dve_step)
            sums = m.acc_f[:, 0:NB, :].rearrange("p b (h w) -> p b h w", h=H)
            den = s["den"].rearrange("p (b h) -> p b h", b=NB)
            step(dve.tensor_scalar(den, sums[:, :, :, FFN.wh], 1e-16, None, ALU.add))
            step(dve.reciprocal(s["den"], s["den"]))
            for h in range(H):
                step(dve.tensor_tensor(agg4[:, :, h, :], sums[:, :, h, 0:FFN.wh], each(den[:, :, h], NE), ALU.mult))
            dve.wait_ge(params_in, 48)
            step(dve.tensor_tensor(agg, agg, wide(s["b_gat"]), ALU.add))
            step(dve.tensor_reduce(s["mean"], agg, AX.X, ALU.add))
            step(dve.tensor_scalar(s["mean"], s["mean"], 1.0 / K, None, ALU.mult))
            step(dve.tensor_tensor(agg, agg, each(s["mean"], K), ALU.subtract))
            step(dve.tensor_tensor(sq, agg, agg, ALU.mult))
            step(dve.tensor_reduce(s["rstd"], sq, AX.X, ALU.add))
            dve.tensor_scalar(s["rstd"], s["rstd"], 1.0 / K, EPS, ALU.mult, ALU.add).then_inc(var_ready, 1)
            dve.wait_ge(std_ready, 1)
            step(dve.reciprocal(s["rstd"], s["rstd"]))
            step(dve.tensor_tensor(agg, agg, each(s["rstd"], K), ALU.mult))
            step(dve.tensor_tensor(agg, agg, wide(s["gamma"]), ALU.mult))
            step(dve.tensor_tensor(agg, agg, wide(s["beta"]), ALU.add))
            step(dve.tensor_reduce(scores, s["agg"].rearrange("p (b h e) -> p b e h", b=NB, h=H), AX.X, ALU.add))
            step(dve.tensor_scalar(s["scores"], s["scores"], 1.0 / H, None, ALU.mult))
            step(dve.memset(s["beaten"], 0.0))
            for a in range(NE):
                for b in range(NE):
                    if a != b:
                        step(dve.tensor_tensor(s["one"], scores[:, :, b], scores[:, :, a], ALU.is_ge if b < a else ALU.is_gt))
                        step(dve.tensor_tensor(beaten[:, :, a], beaten[:, :, a], s["one"], ALU.add))
            step(dve.tensor_reduce(s["top"], scores, AX.X, ALU.max))
            dve.tensor_tensor(e, scores, each(s["top"], NE), ALU.subtract).then_inc(gap_ready, 1)
            step(dve.tensor_scalar(s["beaten"], s["beaten"], 2.0, None, ALU.is_lt))
            dve.wait_ge(exp_ready, 1)
            step(dve.tensor_tensor(s["e"], s["e"], s["beaten"], ALU.mult))
            step(dve.tensor_reduce(s["one"], e, AX.X, ALU.add))
            step(dve.reciprocal(s["one"], s["one"]))
            step(dve.tensor_tensor(m.gates[:, :, :], e, each(s["one"], NE), ALU.mult))


def experts(nc, m, io, out, sem):
    T, PARTS, FC = 7, ((0, 4), (4, 3)), F // P
    w = region(m.weights, [("w1", NE * 2 * F), ("w2", NE * FC * D), ("b2", NE * D)])
    w1 = w["w1"].rearrange("p (e k f) -> p e k f", e=NE, k=2)
    w2 = w["w2"].rearrange("p (e c d) -> p e c d", e=NE, c=FC)
    s = region(m.slots, [("hidden0", FC * T * P), ("hidden1", FC * T * P), ("b1", NE * FC)])
    hidden = [s[f"hidden{o}"].rearrange("p (c n) -> p c n", c=FC) for o in range(2)]
    wide = m.wide[:, :].rearrange("p (b k n) -> p b k n", k=2, n=P)
    acc = m.acc[:, :].rearrange("p (b w) -> p b w", w=GNN.acc)
    ps_y = [m.ps[i][:, 0:D] for i in range(4)]
    stretches = NB // T
    assert stretches * T == NB
    HID, Y, CREDIT = NE * len(PARTS) * FC, NE * T, 2 * T

    weights_in, made, gelu_done, y_ready, y_added, b2_added, saved = (sem("e_" + x) for x in (
        "weights_in", "made", "gelu_done", "y_ready", "y_added", "b2_added", "saved"))

    with nc.Block() as block:
        @block.sync
        def _(sp):
            for e in range(NE):
                sp.dma_start(w1[:, e], io["W1"][e].rearrange("(k p) f -> p k f", p=P)).then_inc(weights_in, 16)
                sp.dma_start(w2[:, e], io["W2"][e].rearrange("(c p) d -> p c d", p=P)).then_inc(weights_in, 16)
            sp.dma_start(w["b2"], bcast(io["b2"].rearrange("e d -> (e d)"), P)).then_inc(weights_in, 16)
            sp.dma_start(s["b1"], io["b1"]).then_inc(weights_in, 16)

            with sp.Fori(0, stretches - 1) as i:
                sp.wait_ge(y_added, i * Y + Y + CREDIT)
                sp.dma_start(out[bass.ds(i * (T * P), T * P), :].rearrange("(t p) d -> p t d", p=P),
                             acc[:, bass.ds(i * T, T), 0:D]).then_inc(saved, 16)
            sp.wait_ge(y_added, stretches * Y + CREDIT)
            sp.dma_start(out[(NB - T) * P:(NB - 1) * P, :].rearrange("(t p) d -> p t d", p=P),
                         acc[:, NB - T:NB - 1, 0:D]).then_inc(saved, 16)
            sp.dma_start(out[(NB - 1) * P:N, :], acc[0:LAST, NB - 1, 0:D]).then_inc(saved, 16)
            sp.wait_ge(saved, 16 * (stretches + 1))

        @block.tensor
        def _(pe):
            pe.wait_ge(weights_in, 16 * 10)
            with pe.Fori(0, stretches) as i:
                def make(e):
                    for part, (t0, nt) in enumerate(PARTS):
                        for c in range(FC):
                            at = (e * len(PARTS) + part) * FC + c
                            pe.wait_ge(gelu_done, i * HID + at + 1)
                            for k in range(2):
                                last = nc.tensor.matmul(m.four[:, c * 512:c * 512 + nt * P], w1[:, e, k, c * P:(c + 1) * P],
                                                        wide[:, bass.ds(i * T + t0, nt), k, :], start=k == 0, stop=k == 1)
                            last.then_inc(made, 1)

                def contract(e):
                    pe.wait_ge(gelu_done, i * HID + (e + 1) * HID // NE + FC)
                    for t in range(T):
                        at = e * T + t
                        pe.wait_ge(y_added, i * Y + at - 3 + CREDIT)
                        for c in range(FC):
                            last = nc.tensor.matmul(ps_y[at % 4], hidden[e % 2][:, c, t * P:(t + 1) * P], w2[:, e, c, :],
                                                    start=c == 0, stop=c == FC - 1)
                        last.then_inc(y_ready, 1)

                make(0)
                for e in range(1, NE):
                    make(e)
                    contract(e - 1)
                contract(NE - 1)

        @block.scalar
        def _(act):
            act.sem_inc(gelu_done, FC)
            act.wait_ge(weights_in, 16 * 10)
            with act.Fori(0, stretches) as i:
                for e in range(NE):
                    act.wait_ge(y_added, i * Y + (e - 1) * T + CREDIT)
                    for part, (t0, nt) in enumerate(PARTS):
                        for c in range(FC):
                            at = (e * len(PARTS) + part) * FC + c
                            act.wait_ge(made, i * HID + at + 1)
                            act.activation(hidden[e % 2][:, c, t0 * P:(t0 + nt) * P], m.four[:, c * 512:c * 512 + nt * P],
                                           ACT.Gelu, bias=s["b1"][:, e * FC + c:e * FC + c + 1]).then_inc(gelu_done, 1)

        @block.vector
        def _(dve):
            dve.sem_inc(y_added, CREDIT)
            dve.wait_ge(weights_in, 16 * 10)
            gates = m.gates[:, :, :].rearrange("p b e -> p (b e)")
            with dve.Fori(0, stretches) as i:
                for e in range(NE):
                    for t in range(T):
                        at = e * T + t
                        x2 = acc[:, bass.ds(i * T + t, 1), 0:D].rearrange("p o d -> p (o d)")
                        gate = gates[:, bass.ds((i * T + t) * NE + e, 1)]
                        dve.scalar_tensor_tensor(x2, w["b2"][:, e * D:(e + 1) * D], gate, x2, ALU.mult, ALU.add).then_inc(b2_added, 1)
                        dve.wait_ge(b2_added, i * Y + at + 1)
                        dve.wait_ge(y_ready, i * Y + at + 1)
                        dve.scalar_tensor_tensor(x2, ps_y[at % 4], gate, x2, ALU.mult, ALU.add).then_inc(y_added, 1)
                        dve.wait_ge(y_added, i * Y + at + 1 + CREDIT)


_INS = [("x", "x"), ("src", "src"), ("dst", "dst"), ("L0_gnn_W", "W_t"), ("L0_gnn_b", "b"), ("L0_gnn_a_src", "a_src"),
        ("L0_gnn_a_dst", "a_dst"), ("L0_mix_wq", "wq"), ("L0_mix_bq", "bq"), ("L0_mix_wk", "wk"), ("L0_mix_bk", "bk"),
        ("L0_mix_wv", "wv"), ("L0_mix_bv", "bv"), ("L0_mix_wo", "wo"), ("L0_mix_bo", "bo"), ("L0_ffn_W_gat", "W_gat"),
        ("L0_ffn_att_src", "att_src"), ("L0_ffn_att_dst", "att_dst"), ("L0_ffn_b_gat", "b_gat"),
        ("L0_ffn_ln_gamma", "ln_gamma"), ("L0_ffn_ln_beta", "ln_beta"), ("L0_ffn_W1", "W1"), ("L0_ffn_b1", "b1"),
        ("L0_ffn_W2", "W2"), ("L0_ffn_b2", "b2"), ("L0_ffn_edge_index", "edge_index")]


def laid_out(inputs):
    import numpy as np
    got = {}
    for name, short in _INS:
        a = np.ascontiguousarray(inputs[name])
        if short == "W_t":
            a = np.ascontiguousarray(a.T)
        if short == "bq":
            a = np.ascontiguousarray(a.reshape(2, P).T).reshape(-1)
        if short == "b1":
            a = np.ascontiguousarray(a.reshape(NE * F // P, P).T)
        got[short] = a
    return got


def kernel(**inputs):
    import concourse.bacc as _bacc
    from concourse.bass_utils import run_bass_kernel_spmd as _run

    nc = _bacc.Bacc("TRN2", target_bir_lowering=False, num_devices=1)
    arrays, io = {}, {}
    for short, a in laid_out(inputs).items():
        arrays[f"in_{short}"] = a
        io[short] = nc.dram_tensor(f"in_{short}", a.shape, mybir.dt.from_np(a.dtype), kind="ExternalInput").ap()
    out = nc.dram_tensor("out", (N, D), F32, kind="ExternalOutput").ap()
    build(nc, io, out)
    r = _run(nc, [arrays], core_ids=[0])
    return r.results[0]["out"]
```

```python
import concourse.bass as bass
from concourse import mybir
from contextlib import ExitStack

F32 = mybir.dt.float32
BF16 = mybir.dt.bfloat16
I32 = mybir.dt.int32
U16 = mybir.dt.uint16
ALU = mybir.AluOpType
ACT = mybir.ActivationFunctionType
AX = mybir.AxisListType

P = 128
N, D, H = 6250, 256, 4
DH = D // H
NB = -(-N // P)
NP = NB * P
LAST = N - (NB - 1) * P
E1, E2 = 206250, 131072
TG = 4
MD = 32
HALF = P + 1
NE, F = 4, 512
EPS = 1e-5
SLOPE = 0.2
SPREAD = 16.0
NOWHERE = float(1 << 22)
NO_LANE = 255
U = 4
BASE = NB + 1
assert BASE ** U < 1 << 24
BU = 7
assert NB % BU == 0
EARLY = 11


class Graph:

    def __init__(self, name, edges, wh, run, tp):
        self.name, self.edges, self.wh, self.run = name, edges, wh, run
        self.c = -(-edges // P)
        assert self.c % (2 * run) == 0
        self.tp, self.pe, self.j = tp, tp * P, TG // tp
        self.s = -(-((edges + NB * (self.pe - 1)) // self.pe) // (U * self.j)) * U * self.j
        self.acc = H * (wh + 1)
        self.row = self.acc + 2 * H


GNN = Graph("gnn", E1, DH, 13, 2)
FFN = Graph("ffn", E2, 4, 16, 2)


class Steps:

    def __init__(self, eng, sem):
        self.eng, self.sem, self.base, self.n = eng, sem, 0, 0

    def __call__(self, ins):
        self.n += 1
        ins.then_inc(self.sem, 1)
        self.eng.wait_ge(self.sem, self.base + self.n)

    def enter(self, i, k):
        self.before, self.k = self.base + self.n, k
        self.base, self.n = self.before + i * k, 0

    def leave(self, trips):
        assert self.n == self.k, (self.n, self.k)
        self.base, self.n = self.before + trips * self.k, 0


def alone(eng):
    eng.nop(nofuse=True)


def mean_var(dve, step, halves, mean, var, room):
    dve.tensor_tensor(mean, halves[:, :, 1], halves[:, :, 4], ALU.add)
    dve.tensor_tensor(room, halves[:, :, 1], halves[:, :, 4], ALU.subtract)
    step(dve.scalar_tensor_tensor(var, halves[:, :, 2], EPS * D, halves[:, :, 5], ALU.add, ALU.add))
    dve.tensor_scalar(mean, mean, 0.5, None, ALU.mult)
    step(dve.scalar_tensor_tensor(room, room, 0.25, room, ALU.mult, ALU.mult))
    return dve.scalar_tensor_tensor(var, var, 1.0 / D, room, ALU.mult, ALU.add)


def bcast(ap, n):
    return ap.unsqueeze(0).broadcast_to([n, ap.shape[0]])


def build(nc, io, out):
    ctx = ExitStack()
    with ctx:
        def sb(name, shape, dt=F32):
            return ctx.enter_context(nc.sbuf_tensor(name, shape, dt))

        def sem(name):
            return ctx.enter_context(nc.semaphore(name))

        def dram(name, shape, dt=F32):
            return nc.dram_tensor(name, shape, dt, kind="Internal").ap()

        m = type("Memory", (), {})()
        m.table = {GNN: dram("gnn_table", (NP, GNN.row)), FFN: dram("ffn_table", (NP, FFN.row))}
        m.sorted = {g: dram(g.name + "_sorted", (g.s * g.pe, 1), I32) for g in (GNN, FFN)}
        m.phi_q = dram("phi_q", (NB * P, 2 * P))
        m.places = dram("ffn_places", (P, 2, FFN.c), I32)
        m.y = dram("expert_rows", (NB * P, NE * D))

        m.wide = sb("wide", [P, NP * 2])
        m.acc = sb("acc", [P, (NB + 1) * GNN.acc])
        m.acc_f = sb("acc_f", [P, NB + 1, FFN.acc])
        m.weights = sb("weights", [P, 2 * NE * F * D // P + NB * FFN.row])
        m.slots = sb("slots", [P, 10416])
        m.sinit = sb("sinit", [P, 2, NB])
        m.ends = sb("ends", [P, 2, NB])
        m.blocks_of = {g: sb(g.name + "_blocks_of", [1, g.s // U], I32) for g in (GNN, FFN)}
        m.att = sb("att", [P, NB, 2 * H])
        m.v = sb("v", [P, NB, 2 * H])
        m.low = sb("low", [P, 2 * H])
        m.near = sb("near", [1, 1], I32)
        m.terms = sb("terms", [P, NB + 1, 3, 2 * H], BF16)
        m.mtab = sb("mtab", [P, NB + 1, H])
        m.ttab = sb("ttab", [P, NB + 1, 2 * H])
        m.kv = sb("kv", [P, 2, HALF])
        m.kvm = sb("kvm", [P, 2, P + H])
        m.stats = sb("stats", [P, NB, 2])
        m.rstd = sb("rstd", [P, NB])
        m.bn = sb("bn", [P, 6])
        m.small = sb("small", [P, 256])
        m.node_of = sb("node_of", [P, NB])
        m.h2 = sb("h2", [P, NB, H * FFN.wh])
        m.both = sb("both", [P, NB, 2 * H])
        m.gates = sb("gates", [P, NB, NE])
        m.ident = sb("ident", [P, P])
        m.ident_b = sb("ident_b", [P, P], BF16)
        m.before = sb("before", [P, P])
        m.ones = sb("ones", [P, P])
        m.iota_n = sb("iota_n", [P, P])
        m.head_mask = sb("head_mask", [P, P])
        m.head_of = sb("head_of", [P, H])
        m.four = ctx.enter_context(nc.psum_tensor("four_banks", [P, 2048], F32))
        m.ps = [ctx.enter_context(nc.psum_tensor(f"bank{i}", [P, 512], F32)) for i in range(4)]

        sort_and_project(nc, m, io, sem)
        graph_groups(nc, m, GNN, sem)
        combine_and_experts(nc, m, io, sem)
        graph_groups(nc, m, FFN, sem)
        gate(nc, m, io, out, sem)


def region(tensor, layout):
    at, views = 0, {}
    for name, words in layout:
        views[name] = tensor[:, at:at + words]
        at += words
    assert at <= tensor.shape[1], (at, tensor.shape)
    return views


def stage_edges(sp, g, places, entries, stage, staged, scattered, parts):
    run = g.run

    def load(i, half):
        at, src = slice(half * run, (half + 1) * run), bass.ds(i * (2 * run) + half * run, run)
        sp.dma_start(stage[:, 0, at], places[:, src]).then_inc(staged[half], 16)
        sp.dma_start(stage[:, 1, at], entries[:, src]).then_inc(staged[half], 16)

    ends = [first for first, _ in parts[1:]] + [g.c // (2 * run)]
    for (first, before), end in zip(parts, ends):
        if before:
            before()
        if first == 0:
            for half in range(2):
                load(0, half)
        if end > 1:
            with sp.Fori(max(first, 1), end) as i:
                for half in range(2):
                    sp.wait_ge(scattered[half], i * (16 * run))
                    load(i, half)


def scatter_edges(pool, m, g, stage, staged, scattered):
    run, trips = g.run, g.c // (2 * g.run)
    with pool.Fori(0, trips) as i:
        for half in range(2):
            pool.wait_ge(staged[half], i * 32 + 32)
            alone(pool)
            for c in range(half * run, (half + 1) * run):
                pool.indirect_dma_start(
                    out=m.sorted[g], out_offset=bass.IndirectOffsetOnAxis(ap=stage[:, 0, c:c + 1], axis=0),
                    in_=stage[:, 1, c:c + 1], in_offset=None, bounds_check=g.s * g.pe - 1,
                    oob_is_err=False).then_inc(scattered[half], 16)
    for half in range(2):
        pool.wait_ge(scattered[half], 16 * run * trips)


def sort_and_project(nc, m, io, sem):
    C, CF = GNN.c, FFN.c
    r = region(m.acc, [("pos1", C), ("pack1", C), ("pos2", CF), ("pack2", CF),
                       ("key", C), ("scan", C), ("blk", C // 2), ("mask", C // 2), ("one", C // 2),
                       ("fill", 512)])
    pos = {GNN: r["pos1"], FFN: r["pos2"]}
    pack = {GNN: r["pack1"].bitcast(I32), FFN: r["pack2"].bitcast(I32)}
    key, scan, scani = r["key"].bitcast(I32), r["scan"], r["scan"].bitcast(I32)
    blk, mask, one = (r[n].bitcast(BF16) for n in ("blk", "mask", "one"))
    fill = r["fill"].bitcast(I32)
    x = m.wide[:, :].rearrange("p (b d) -> p b d", d=D)
    w = region(m.weights, [("wt", 2 * D), ("wk", 2 * D), ("wv", 2 * D), ("wq", 2 * D), ("bias", 3 * D),
                           ("a", 2 * D), ("bq", 2)])
    wt, wk, wv, wq = (w[n].rearrange("p (k n) -> p k n", k=2) for n in ("wt", "wk", "wv", "wq"))
    most = max(GNN.s, FFN.s)
    s = region(m.slots, [("xn", D), ("xnt", D), ("row", GNN.row), ("k", D), ("v", 2 * HALF),
                         ("neg", 2 * D), ("prod", 2 * D), ("phi", D), ("qpos", D),
                         ("stage", 4 * GNN.run), ("iota_s", most), ("count", most),
                         ("lane_in", 1), ("iota_p", 1)])
    row = s["row"][:, 0:GNN.acc].rearrange("p (h w) -> p h w", h=H)
    vrow = s["v"].rearrange("p (j w) -> p j w", j=2)
    tot, totall, pad, starts, iota_f = (m.small[:, i * NB:(i + 1) * NB] for i in range(5))
    padi = pad.bitcast(I32)
    stage = s["stage"].bitcast(I32).rearrange("p (k c) -> p k c", k=2)
    last = E1 - (P - 1) * GNN.c
    assert FFN.c * P == E2 and LAST >= 96
    fills = [len(range(0, g.s * g.pe // P, 512)) for g in (GNN, FFN)]

    edges_in = [sem("gnn_edges_in"), sem("ffn_edges_in")]
    x_in, weights_in = sem("x_in"), sem("weights_in")
    const_ready, pads_ready, iota_ready = sem("const_ready"), sem("pads_ready"), sem("iota_ready")
    fill_ready, filled = sem("fill_ready"), [sem("gnn_filled"), sem("ffn_filled")]
    totals_ready, sums_ready, key_free, places_ready = (sem(n) for n in ("totals_ready", "sums_ready", "key_free", "places_ready"))
    staged = [sem("staged0"), sem("staged1")]
    scattered, places_saved = [sem("scattered0"), sem("scattered1")], sem("places_saved")
    dve_step, var_ready, std_ready = sem("project_step"), sem("var_ready"), sem("std_ready")
    xn_ready, turned, xnt_ready, products_ready, products_read = (
        sem(n) for n in ("xn_ready", "turned", "xnt_ready", "products_ready", "products_read"))
    neg_ready, exp_ready, kv_in_ready, kv_made = (sem(n) for n in ("neg_ready", "exp_ready", "kv_in_ready", "kv_made"))
    row_ready, row_saved, phi_saved, slots_free = (sem(n) for n in ("row_ready", "row_saved", "phi_saved", "slots_free"))
    least = [sem(f"gnn_least{i}") for i in range(4)]
    prod_ready, v_ready, v_saved = sem("prod_ready"), sem("gnn_v_ready"), sem("gnn_v_saved")
    ps_w, ps_v, ps_q, ps_t = m.four[:, 0:512], m.four[:, 512:768], m.four[:, 1024:1280], m.four[:, 1536:1792]
    ps_kv = m.ps[0][:, 0:2 * HALF].rearrange("p (j w) -> p j w", j=2)
    ps_s = m.ps[1]

    def blocks(i):
        return [bass.ds(i * BU + k, 1) for k in range(BU)]

    with nc.Block() as block:
        @block.sync
        def _(sp):
            sp.wait_ge(pads_ready, 1)
            for t, n in ((key, "src"), (pack[GNN], "dst")):
                sp.dma_start(t[0:P - 1, 0:GNN.c], io[n][0:(P - 1) * GNN.c].rearrange("(p c) -> p c", c=GNN.c)).then_inc(edges_in[0], 16)
                sp.dma_start(t[P - 1:P, 0:last], io[n][(P - 1) * GNN.c:E1].unsqueeze(0)).then_inc(edges_in[0], 16)
            sp.wait_ge(fill_ready, 1)
            for i, g in enumerate((GNN, FFN)):
                flat = m.sorted[g].rearrange("(p c) o -> p (c o)", p=P)
                cols = g.s * g.pe // P
                for c0 in range(0, cols, 512):
                    c1 = min(cols, c0 + 512)
                    sp.dma_start(flat[:, c0:c1], fill[:, 0:c1 - c0]).then_inc(filled[i], 16)
            sp.wait_ge(key_free, 1)
            sp.dma_start(key[:, 0:FFN.c], io["edge_index"][1, :].rearrange("(p c) -> p c", p=P)).then_inc(edges_in[1], 16)
            sp.dma_start(pack[FFN][:, 0:FFN.c], io["edge_index"][0, :].rearrange("(p c) -> p c", p=P)).then_inc(edges_in[1], 16)
            stage_edges(sp, GNN, pos[GNN].bitcast(I32), pack[GNN], stage, staged, scattered,
                        [(0, lambda: sp.wait_ge(places_ready, 1)), (EARLY, lambda: sp.wait_ge(places_ready, 2))])
            sp.wait_ge(places_ready, 3)
            sp.dma_start(m.places[:, 0, :], pos[FFN].bitcast(I32)).then_inc(places_saved, 16)
            sp.dma_start(m.places[:, 1, :], pack[FFN]).then_inc(places_saved, 16)
            sp.wait_ge(places_saved, 32)
            sp.wait_ge(filled[1], 16 * fills[1])

        @block.gpsimd
        def _(pool):
            pool.iota(m.iota_n[:, :].bitcast(I32), [[1, P]], base=0, channel_multiplier=0).then_inc(iota_ready, 1)
            pool.iota(m.before[:, :].bitcast(I32), [[1, P]], base=0, channel_multiplier=-1).then_inc(iota_ready, 1)
            pool.iota(s["iota_p"].bitcast(I32), [[0, 1]], base=0, channel_multiplier=1).then_inc(iota_ready, 1)
            pool.iota(s["iota_s"].bitcast(I32), [[1, most]], base=0, channel_multiplier=0).then_inc(iota_ready, 1)
            pool.wait_ge(filled[0], 16 * fills[0])
            scatter_edges(pool, m, GNN, stage, staged, scattered)

        @block.scalar
        def _(act):
            act.wait_ge(edges_in[0], 64)
            act.dma_start(x[:, 0:NB - 1, :], io["x"][0:(NB - 1) * P, :].rearrange("(b p) d -> p b d", p=P)).then_inc(x_in, 16)
            act.wait_ge(pads_ready, 1)
            act.dma_start(x[0:LAST, NB - 1, :], io["x"][(NB - 1) * P:N, :]).then_inc(x_in, 16)
            for t, n in ((wt, "W_t"), (wk, "wk"), (wv, "wv"), (wq, "wq")):
                act.dma_start(t, io[n].rearrange("(k p) n -> p k n", p=P)).then_inc(weights_in, 16)
            for i, n in enumerate(("b", "bk", "bv")):
                act.dma_start(w["bias"][:, i * D:(i + 1) * D], bcast(io[n], P)).then_inc(weights_in, 16)
            for i, n in enumerate(("a_src", "a_dst")):
                act.dma_start(w["a"][:, i * D:(i + 1) * D], bcast(io[n].rearrange("h d -> (h d)"), P)).then_inc(weights_in, 16)
            act.dma_start(w["bq"], io["bq"].rearrange("(p k) -> p k", k=2)).then_inc(weights_in, 16)
            act.wait_ge(var_ready, 1)
            act.activation(m.rstd[:, :], m.rstd[:, :], ACT.Sqrt).then_inc(std_ready, 1)
            act.sem_inc(slots_free, 1)
            with act.Fori(0, NB) as i:
                act.wait_ge(turned, i + 1)
                act.copy(s["xnt"], ps_t).then_inc(xnt_ready, 1)
                act.wait_ge(neg_ready, i + 1)
                act.activation(s["neg"], s["neg"], ACT.Exp).then_inc(exp_ready, 1)
                act.wait_ge(row_ready, i + 1)
                act.dma_start(m.table[GNN][bass.ds(i * P, P), 0:GNN.acc], s["row"][:, 0:GNN.acc]).then_inc(row_saved, 16)
                act.wait_ge(kv_in_ready, i + 1)
                act.dma_start(m.phi_q[bass.ds(i * P, P), :], s["phi"]).then_inc(phi_saved, 16)
                act.wait_ge(row_saved, i * 16 + 16)
                act.wait_ge(phi_saved, i * 16 + 16)
                act.sem_inc(slots_free, 1)
            act.wait_ge(v_ready, 1)
            act.dma_start(m.table[GNN].rearrange("(b p) w -> p b w", p=P)[:, :, GNN.acc:], m.v[:, :, :]).then_inc(v_saved, 16)
            act.wait_ge(v_saved, 16)

        @block.vector
        def _(dve):
            step = Steps(dve, dve_step)
            step(dve.memset(key[96:P, last:], 8191))
            step(dve.memset(pack[GNN][96:P, last:], 0))
            dve.memset(x[96:P, NB - 1, :], 0.0).then_inc(pads_ready, 1)
            dve.memset(fill, NO_LANE).then_inc(fill_ready, 1)
            step(dve.memset(one, 1.0))
            step(dve.memset(m.ones[:, :], 1.0))
            step(dve.memset(m.kv[:, :, :], 0.0))
            step(dve.memset(s["v"], 1.0))
            step(dve.memset(s["row"], 1.0))
            step(dve.memset(pos[GNN], NOWHERE))
            step(dve.memset(pos[FFN], NOWHERE))
            dve.wait_ge(iota_ready, 4)
            step(dve.tensor_copy(m.iota_n[:, :], m.iota_n[:, :].bitcast(I32)))
            step(dve.tensor_copy(m.before[:, :], m.before[:, :].bitcast(I32)))
            step(dve.tensor_copy(iota_f, m.iota_n[:, 0:NB]))
            step(dve.tensor_copy(s["iota_s"], s["iota_s"].bitcast(I32)))
            step(dve.tensor_scalar(m.ident[:, :], m.before[:, :], 0.0, None, ALU.is_equal))
            step(dve.tensor_copy(m.ident_b[:, :], m.ident[:, :]))
            step(dve.tensor_scalar(m.before[:, :], m.before[:, :], 0.0, None, ALU.is_gt))
            step(dve.memset(m.node_of[:, :], 1.0))
            step(dve.tensor_copy(s["lane_in"], s["iota_p"].bitcast(I32)))
            step(dve.tensor_scalar(m.node_of[:, NB - 1:NB], s["lane_in"], float(LAST), None, ALU.is_lt))
            step(dve.tensor_scalar(s["iota_p"].bitcast(I32), s["iota_p"].bitcast(I32), 5, None, ALU.arith_shift_right))
            step(dve.tensor_copy(s["lane_in"], s["iota_p"].bitcast(I32)))
            step(dve.tensor_copy(m.head_mask[:, :].bitcast(I32), m.iota_n[:, :]))
            step(dve.tensor_scalar(m.head_mask[:, :].bitcast(I32), m.head_mask[:, :].bitcast(I32), 5, None, ALU.arith_shift_right))
            step(dve.tensor_copy(m.head_mask[:, :], m.head_mask[:, :].bitcast(I32)))
            step(dve.tensor_scalar(m.head_mask[:, :], m.head_mask[:, :], s["lane_in"], None, ALU.is_equal))
            step(dve.tensor_scalar(m.head_of[:, :], m.iota_n[:, 0:H], s["lane_in"], None, ALU.is_equal))
            for gi, g in enumerate((GNN, FFN)):
                c = g.c
                dve.wait_ge(edges_in[gi], (64, 32)[gi])
                step(dve.tensor_scalar(scani[:, 0:c], key[:, 0:c], 7, None, ALU.arith_shift_right))
                step(dve.tensor_copy(blk[:, 0:c], scani[:, 0:c]))
                step(dve.tensor_scalar(pack[g], pack[g], float(N - 1), 256.0, ALU.min, ALU.mult))
                step(dve.tensor_scalar(scani[:, 0:c], key[:, 0:c], P - 1, None, ALU.bitwise_and))
                step(dve.tensor_tensor(pack[g], pack[g], scani[:, 0:c], ALU.add))
                if gi == 0:
                    dve.sem_inc(key_free, 1)
                with dve.Fori(0, NB // BU) as i:
                    step.enter(i, BU)
                    for b in blocks(i):
                        step(dve.tensor_scalar(mask[:, 0:c], blk[:, 0:c], iota_f[:, b], 0.0, ALU.is_equal,
                                               ALU.add, accum_out=tot[:, b]))
                    step.leave(NB // BU)
                dve.sem_inc(totals_ready, 1)
                dve.wait_ge(sums_ready, gi + 1)
                step(dve.tensor_scalar(padi, ps_s[:, 64:64 + NB], float(g.pe - 1), None, ALU.add))
                step(dve.tensor_scalar(padi, padi, g.pe.bit_length() - 1, g.pe.bit_length() - 1, ALU.arith_shift_right,
                                       ALU.logical_shift_left))
                step(dve.tensor_copy(totall, padi))
                step(dve.tensor_tensor_scan(m.ends[:, gi, :], m.ones[:, 0:NB], totall, 0.0, ALU.mult, ALU.add))
                step(dve.tensor_tensor(starts, m.ends[:, gi, :], totall, ALU.subtract))
                step(dve.scalar_tensor_tensor(m.sinit[:, gi, :], starts, -1.0, ps_s[:, 0:NB], ALU.add, ALU.add))
                cuts = (0, EARLY * 2 * g.run, c) if g is GNN else (0, c)
                for a, z in zip(cuts, cuts[1:]):
                    more = z < c
                    with dve.Fori(0, NB // BU) as i:
                        step.enter(i, (3 + more) * BU)
                        for b in blocks(i):
                            start = m.sinit[:, gi, b]
                            step(dve.tensor_scalar(mask[:, a:z], blk[:, a:z], iota_f[:, b], None, ALU.is_equal))
                            step(dve.tensor_tensor_scan(scan[:, a:z], one[:, a:z], mask[:, a:z], start, ALU.mult, ALU.add))
                            alone(dve)
                            step(dve.copy_predicated(pos[g][:, a:z], mask[:, a:z].bitcast(U16), scan[:, a:z]))
                            if more:
                                alone(dve)
                                step(dve.tensor_copy(start, scan[:, z - 1:z]))
                        step.leave(NB // BU)
                    at, tile, log = pos[g].bitcast(I32)[:, a:z], scani[:, a:z], TG.bit_length() - 1
                    step(dve.tensor_copy(at, pos[g][:, a:z]))
                    step(dve.tensor_scalar(tile, at, 7, None, ALU.arith_shift_right))
                    step(dve.scalar_tensor_tensor(at, tile, -float(P), at, ALU.mult, ALU.add))
                    step(dve.scalar_tensor_tensor(at, at, float(TG), tile, ALU.mult, ALU.add))
                    step(dve.tensor_scalar(tile, tile, log, log, ALU.arith_shift_right, ALU.logical_shift_left))
                    dve.scalar_tensor_tensor(at, tile, P - 1.0, at, ALU.mult, ALU.add).then_inc(places_ready, 1)
                step(dve.tensor_scalar(m.ends[:, gi, :], m.ends[:, gi, :], 1.0 / g.pe, None, ALU.mult))
                count = s["count"][0:1, 0:g.s]
                step(dve.memset(count, 0.0))
                with dve.Fori(0, NB // BU) as i:
                    step.enter(i, BU)
                    for b in blocks(i):
                        step(dve.scalar_tensor_tensor(count, s["iota_s"][0:1, 0:g.s], m.ends[0:1, gi, b],
                                                      count, ALU.is_ge, ALU.add))
                    step.leave(NB // BU)
                count = count.rearrange("p (i u) -> p i u", u=U)
                for u in reversed(range(1, U)):
                    step(dve.scalar_tensor_tensor(count[:, :, u - 1], count[:, :, u], float(BASE), count[:, :, u - 1], ALU.mult, ALU.add))
                step(dve.tensor_copy(m.blocks_of[g][:, :], count[:, :, 0]))

            dve.wait_ge(x_in, 32)
            halves = m.att[:, :, 0:6]
            with dve.Fori(0, NB) as b:
                step.enter(b, 1)
                step(dve.bn_stats(m.att[:, bass.ds(b, 1), 0:6].rearrange("p o d -> p (o d)"),
                                  x[:, bass.ds(b, 1), :].rearrange("p o d -> p (o d)")))
                step.leave(NB)
            mean_var(dve, step, halves, m.stats[:, :, 0], m.rstd[:, :], m.stats[:, :, 1]).then_inc(var_ready, 1)
            dve.wait_ge(std_ready, 1)
            step(dve.reciprocal(m.rstd[:, :], m.rstd[:, :]))
            dve.wait_ge(weights_in, 16 * 10)
            with dve.Fori(0, NB) as i:
                step.enter(i, 8)
                one_of = bass.ds(i, 1)
                dve.tensor_scalar(s["xn"], x[:, one_of, :].rearrange("p o d -> p (o d)"), m.stats[:, one_of, 0],
                                  m.rstd[:, one_of], ALU.subtract, ALU.mult).then_inc(xn_ready, 1)
                dve.wait_ge(products_ready, i + 1)
                dve.wait_ge(slots_free, i + 1)
                step(dve.tensor_tensor(row[:, :, 0:DH], ps_w[:, 0:D].rearrange("p (h d) -> p h d", h=H),
                                       w["bias"][:, 0:D].rearrange("p (h d) -> p h d", h=H), ALU.add))
                step(dve.tensor_tensor(s["k"], ps_w[:, D:2 * D], w["bias"][:, D:2 * D], ALU.add))
                step(dve.tensor_tensor(vrow[:, :, 0:P], ps_v.rearrange("p (j w) -> p j w", j=2),
                                       w["bias"][:, 2 * D:].rearrange("p (j w) -> p j w", j=2), ALU.add))
                step(dve.tensor_scalar(s["v"], s["v"], m.node_of[:, one_of], None, ALU.mult))
                step(dve.tensor_scalar(s["neg"][:, 0:D], s["k"], 0.0, None, ALU.min))
                for j in range(2):
                    c = slice(j * P, (j + 1) * P)
                    step(dve.tensor_scalar(s["qpos"][:, c], ps_q[:, c], w["bq"][:, j:j + 1], 0.0, ALU.add, ALU.max))
                dve.tensor_scalar(s["neg"][:, D:D + P], ps_q[:, 0:P], w["bq"][:, 0:1], 0.0, ALU.add, ALU.min)
                dve.tensor_scalar(s["neg"][:, D + P:], ps_q[:, P:], w["bq"][:, 1:2], 0.0, ALU.add, ALU.min).then_inc(neg_ready, 1)
                for j, signals in ((0, row_ready), (1, prod_ready)):
                    c = slice(j * D, (j + 1) * D)
                    dve.tensor_tensor(s["prod"][:, c].rearrange("p (h d) -> p h d", h=H), row[:, :, 0:DH],
                                      w["a"][:, c].rearrange("p (h d) -> p h d", h=H), ALU.mult).then_inc(signals, 1)
                dve.wait_ge(row_ready, i + 1)
                dve.wait_ge(prod_ready, i + 1)
                dve.tensor_reduce(m.att[:, one_of, :], s["prod"].rearrange("p (g d) -> p g d", d=DH), AX.X, ALU.add)
                dve.wait_ge(exp_ready, i + 1)
                step(dve.scalar_tensor_tensor(s["k"], s["k"], 0.0, s["neg"][:, 0:D], ALU.max, ALU.add))
                dve.tensor_tensor(s["phi"], s["qpos"], s["neg"][:, D:], ALU.add).then_inc(kv_in_ready, 1)
                dve.wait_ge(kv_made, i + 1)
                dve.tensor_tensor(m.kv[:, :, :], m.kv[:, :, :], ps_kv, ALU.add).then_inc(products_read, 1)
                dve.wait_ge(products_read, i + 1)
                step.leave(NB)
            least_v(dve, m, ps_s, least, v_ready, step)

        @block.tensor
        def _(pe):
            for gi in range(2):
                pe.wait_ge(totals_ready, gi + 1)
                nc.tensor.matmul(ps_s[:, 0:NB], m.before[:, :], tot, start=True, stop=True)
                nc.tensor.matmul(ps_s[:, 64:64 + NB], m.ones[:, :], tot, start=True, stop=True).then_inc(sums_ready, 1)
            pe.wait_ge(weights_in, 16 * 10)
            with pe.Fori(0, NB) as i:
                pe.wait_ge(xn_ready, i + 1)
                for k in range(2):
                    c = slice(k * P, (k + 1) * P)
                    last = nc.tensor.transpose(ps_t[:, c], s["xn"][:, c], m.ident[:, :])
                last.then_inc(turned, 1)
                pe.wait_ge(xnt_ready, i + 1)
                for k in range(2):
                    c, st = slice(k * P, (k + 1) * P), dict(start=k == 0, stop=k == 1)
                    nc.tensor.matmul(ps_w[:, 0:D], s["xnt"][:, c], wt[:, k, :], **st)
                for k in range(2):
                    c, st = slice(k * P, (k + 1) * P), dict(start=k == 0, stop=k == 1)
                    nc.tensor.matmul(ps_w[:, D:], s["xnt"][:, c], wk[:, k, :], **st)
                for k in range(2):
                    c, st = slice(k * P, (k + 1) * P), dict(start=k == 0, stop=k == 1)
                    nc.tensor.matmul(ps_v, s["xnt"][:, c], wv[:, k, :], **st)
                for j in range(2):
                    for k in range(2):
                        c, st = slice(k * P, (k + 1) * P), dict(start=k == 0, stop=k == 1)
                        last = nc.tensor.matmul(ps_q[:, j * P:(j + 1) * P], wq[:, k, j * P:(j + 1) * P], s["xnt"][:, c], **st)
                last.then_inc(products_ready, 1)
                pe.wait_ge(kv_in_ready, i + 1)
                for j in range(2):
                    last = nc.tensor.matmul(ps_kv[:, j, :], s["k"][:, j * P:(j + 1) * P], vrow[:, j, :], start=True, stop=True)
                last.then_inc(kv_made, 1)
            least_v_products(nc, pe, m, ps_s, least)


def graph_groups(nc, m, g, sem):
    lists = region(m.weights, [("raw", g.s * g.tp), ("lane", g.s * g.tp), ("index", g.s * g.tp)])
    raw, index, lane = lists["raw"].bitcast(I32), lists["index"].bitcast(I32), lists["lane"]
    parts = [(0, U * TG), (U * TG, g.s * g.tp)]
    list_in, dve_step = [sem(f"{g.name}_list_in{i}") for i in range(2)], sem(g.name + "_list_step")

    shared = {}

    def own(name):
        if name not in shared:
            shared[name] = sem(f"{g.name}_{name}")
        return shared[name]

    decoded = own("decoded")
    near, far = groups_near(nc, m, g, own, index, lane), groups_far(nc, m, g, own, index, lane)

    with nc.Block() as block:
        def either(eng, name):
            with eng.If(eng.value_load(m.near[0:1, 0:1], min_val=0, max_val=1) == 1):
                near[name](eng)
            with eng.Else():
                far[name](eng)

        @block.sync
        def _(sp):
            for i, (a, b) in enumerate(parts):
                sp.dma_start(raw[:, a:b].rearrange("p (s t) -> p s t", t=TG),
                             m.sorted[g][a * P:b * P, :].rearrange("(s p t) o -> p s (t o)", p=P, t=TG)).then_inc(list_in[i], 16)

        @block.gpsimd
        def _(pool):
            either(pool, "pool")

        @block.scalar
        def _(act):
            act.wait_ge(decoded, 1)
            either(act, "act")

        @block.vector
        def _(dve):
            step = Steps(dve, dve_step)
            for i, (a, b) in enumerate(parts):
                dve.wait_ge(list_in[i], 16)
                dve.tensor_scalar(index[:, a:b], raw[:, a:b], 8, None, ALU.arith_shift_right).then_inc(decoded, 1)
                step(dve.tensor_scalar(lane.bitcast(I32)[:, a:b], raw[:, a:b], 255, None, ALU.bitwise_and))
                step(dve.tensor_copy(lane[:, a:b], lane.bitcast(I32)[:, a:b]))
                if i == 0 and g is GNN:
                    step(dve.memset(m.acc[:, :], 0.0))
            either(dve, "dve")

        @block.tensor
        def _(pe):
            either(pe, "pe")


def groups_near(nc, m, g, n, index, lane):
    groups, trips, W = g.s // g.j, g.s // g.j // U, g.wh + 1
    s = region(m.slots, [(f"rows{u}", TG * g.row) for u in range(U)] + [(f"one_hot{u}", TG * P) for u in range(U)]
               + [(f"one_hot_b{o}", TG * P // 2) for o in range(2)] + [(f"one_hot_t{o}", TG * P // 2) for o in range(2)]
               + [(f"index{u}", TG) for u in range(U)] + [(f"z{o}", TG * 2 * H) for o in range(2)]
               + [(f"weight{o}", TG * H) for o in range(2)])
    rows = [s[f"rows{u}"].rearrange("p (t w) -> p t w", t=TG) for u in range(U)]
    one_hot = [s[f"one_hot{u}"].rearrange("p (t n) -> p t n", t=TG) for u in range(U)]
    one_hot_b, one_hot_t = ([s[f"{n}{o}"].bitcast(BF16).rearrange("p (t n) -> p t n", t=TG) for o in range(2)]
                            for n in ("one_hot_b", "one_hot_t"))
    slot_index = [s[f"index{u}"].bitcast(I32) for u in range(U)]
    z = [s[f"z{o}"] for o in range(2)]
    z3 = [x.rearrange("p (t c) -> p t c", t=TG) for x in z]
    weight = [s[f"weight{o}"].rearrange("p (t h) -> p t h", t=TG) for o in range(2)]
    acc = m.acc[:, :].rearrange("p (b w) -> p b w", w=GNN.acc) if g is GNN else m.acc_f[:, :, :]
    ps_t = [m.four[:, o * 512:o * 512 + TG * P // 2].bitcast(BF16).rearrange("p (t n) -> p t n", t=TG) for o in range(2)]
    ps_e = [m.four[:, (2 + o) * 512:(2 + o) * 512 + TG * 2 * H].rearrange("p (t c) -> p t c", t=TG) for o in range(2)]
    ps_sum = [[m.ps[2 * o + j % 2][:, j // 2 * g.acc:(j // 2 + 1) * g.acc] for j in range(g.j)] for o in range(2)]

    indexed, gathered = n("indexed"), [n(f"gathered{u}") for u in range(U)]
    one_hot_ready, one_hot_b_ready, turned, one_hot_t_ready, terms_at_edges, z_ready, exp_ready = (n(x) for x in (
        "one_hot_ready", "one_hot_b_ready", "turned", "one_hot_t_ready", "terms_at_edges", "z_ready", "exp_ready"))
    weight_ready, messages_ready, summed, added = (n(x) for x in ("weight_ready", "messages_ready", "summed", "added"))
    start_step, loop_ready, loop_exp = n("start_step"), n("loop_ready"), n("loop_exp")

    def loop(eng, group, peel_first=False):
        first = int(peel_first)
        for i in range(first):
            for u in range(U):
                group(i, u, lambda ahead: True)
        with eng.Fori(first, trips - 1) as i:
            for u in range(U):
                group(i, u, lambda ahead: True)
        for u in range(U):
            group(trips - 1, u, lambda ahead: u + ahead < U)

    def next_word(eng, i, u, word):
        if u * g.j % U:
            return word
        return eng.value_load(m.blocks_of[g][0:1, bass.ds(i * g.j + u * g.j // U, 1)], min_val=0, max_val=BASE ** U - 1)

    def block_of(word, u, j):
        return word // BASE ** ((u * g.j + j) % U) % BASE

    def pool(eng):
        def gather(i, u, more):
            eng.wait_ge(indexed, i * U + u + 1)
            alone(eng)
            if not isinstance(i, int) or i:
                eng.wait_ge(summed, (i - 1) * U + u + 1)
                alone(eng)
            for t in range(TG):
                eng.indirect_dma_start(out=rows[u][:, t, :], out_offset=None, in_=m.table[g],
                                       in_offset=bass.IndirectOffsetOnAxis(ap=slot_index[u][:, t:t + 1], axis=0)
                                       ).then_inc(gathered[u], 16)
        loop(eng, gather, peel_first=True)

    def act(eng):
        def one_hots(k, u):
            o = u % 2
            eng.wait_ge(one_hot_ready, k + 1)
            eng.copy(one_hot_b[o], one_hot[u]).then_inc(one_hot_b_ready, 1)
            eng.wait_ge(turned, k + 1)
            eng.copy(one_hot_t[o], ps_t[o]).then_inc(one_hot_t_ready, 1)

        def exponentials(k, o):
            eng.wait_ge(z_ready, k + 1)
            eng.activation(z[o], z[o], ACT.Exp).then_inc(exp_ready, 1)

        def indices(i, u):
            eng.copy(slot_index[u], index[:, bass.ds((i * U + u) * TG, TG)]).then_inc(indexed, 1)

        def group(i, u, more):
            k = i * U + u
            if more(U):
                eng.wait_ge(gathered[u], i * (16 * TG) + 16 * TG)
                alone(eng)
                indices(i + 1, u)
            if more(3):
                one_hots(k + 3, (u + 3) % U)
            if more(2):
                exponentials(k + 2, u % 2)

        for u in range(U):
            indices(0, u)
        eng.wait_ge(n("decoded"), 2)
        if g is FFN:
            eng.wait_ge(loop_ready, 1)
            eng.activation(m.att[:, :, :], m.att[:, :, :], ACT.Exp).then_inc(loop_exp, 1)
        one_hots(0, 0)
        one_hots(1, 1)
        exponentials(0, 0)
        one_hots(2, 2)
        exponentials(1, 1)
        loop(eng, group)

    def dve(eng):
        def one_hots(k, u):
            lanes = lane[:, bass.ds(k * TG, TG)].unsqueeze(2).broadcast_to([P, TG, P])
            eng.tensor_tensor(one_hot[u], m.iota_n[:, :].unsqueeze(1).broadcast_to([P, TG, P]), lanes,
                              ALU.is_equal).then_inc(one_hot_ready, 1)

        def exponents(k, u, arrivals):
            o = u % 2
            eng.wait_ge(terms_at_edges, k + 1)
            eng.wait_ge(gathered[u], arrivals * (16 * TG))
            eng.tensor_tensor(z3[o], rows[u][:, :, g.acc:], ps_e[o], ALU.add).then_inc(z_ready, 1)

        def messages(k, u):
            o = u % 2
            eng.wait_ge(exp_ready, k + 1)
            eng.tensor_tensor(weight[o], z3[o][:, :, 0:H], z3[o][:, :, H:], ALU.max).then_inc(weight_ready, 1)
            eng.wait_ge(weight_ready, k + 1)
            msg = rows[u][:, :, 0:g.acc].rearrange("p t (h w) -> p t h w", h=H)
            eng.tensor_tensor(msg, msg, weight[o].unsqueeze(3).broadcast_to([P, TG, H, W]), ALU.mult).then_inc(messages_ready, 1)

        def add(k, u, word):
            eng.wait_ge(summed, k + 1)
            for j in range(g.j):
                at = acc[:, bass.ds(block_of(word, u, j), 1), :].rearrange("p o w -> p (o w)")
                if not isinstance(k, int) or k or j:
                    eng.wait_ge(added, k * g.j + j)
                eng.tensor_tensor(at, at, ps_sum[u % 2][j], ALU.add).then_inc(added, 1)

        def group(i, u, more):
            nonlocal word
            k = i * U + u
            word = next_word(eng, i, u, word)
            if more(3):
                one_hots(k + 3, (u + 3) % U)
            if more(2):
                exponents(k + 2, (u + 2) % U, i + 1 + (u + 2) // U)
            if more(1):
                messages(k + 1, (u + 1) % U)
            add(k, u, word)

        word = None
        step = Steps(eng, start_step)
        if g is FFN:
            own = m.acc_f[:, 0:NB, :].rearrange("p b (h w) -> p b h w", h=H)
            loops = m.att[:, :, :]
            eng.tensor_tensor(loops, m.both[:, :, :], m.v[:, :, :], ALU.add).then_inc(loop_ready, 1)
            step(eng.memset(m.acc_f[:, :, :], 1.0))
            for h in range(H):
                step(eng.tensor_copy(own[:, :, h, 0:g.wh], m.h2[:, :, h * g.wh:(h + 1) * g.wh]))
            eng.wait_ge(loop_exp, 1)
            step(eng.tensor_tensor(loops[:, :, 0:H], loops[:, :, 0:H], loops[:, :, H:], ALU.max))
            step(eng.tensor_tensor(own, own, loops[:, :, 0:H].unsqueeze(3).broadcast_to([P, NB, H, W]), ALU.mult))
        one_hots(0, 0)
        one_hots(1, 1)
        exponents(0, 0, 1)
        one_hots(2, 2)
        exponents(1, 1, 1)
        messages(0, 0)
        loop(eng, group, peel_first=True)

    def pe(eng):
        def turn(k, u):
            o = u % 2
            eng.wait_ge(one_hot_b_ready, k + 1)
            for t in range(TG):
                last = nc.tensor.transpose(ps_t[o][:, t, :], one_hot_b[o][:, t, :], m.ident_b[:, :])
            last.then_inc(turned, 1)

        def terms(k, u, word):
            o = u % 2
            eng.wait_ge(one_hot_t_ready, k + 1)
            if not isinstance(k, int) or k >= 2:
                eng.wait_ge(z_ready, k - 1)
            for t in range(TG):
                b = block_of(word, u, t // g.tp)
                for c in range(3):
                    last = nc.tensor.matmul(ps_e[o][:, t, :], one_hot_t[o][:, t, :],
                                            m.terms[:, bass.ds(b, 1), c, :].rearrange("p o w -> p (o w)"),
                                            start=c == 0, stop=c == 2)
            last.then_inc(terms_at_edges, 1)

        def sums(k, u):
            eng.wait_ge(messages_ready, k + 1)
            for t in range(TG):
                last = nc.tensor.matmul(ps_sum[u % 2][t // g.tp], one_hot[u][:, t, :], rows[u][:, t, 0:g.acc],
                                        start=t % g.tp == 0, stop=t % g.tp == g.tp - 1)
            last.then_inc(summed, 1)

        def group(i, u, more):
            nonlocal word
            k = i * U + u
            word = next_word(eng, i, u, word)
            turn(k, u)
            terms(k, u, word)
            if not isinstance(k, int) or k >= 2:
                sums(k - 2, (u - 2) % U)

        word = None
        loop(eng, group, peel_first=True)
        for k in (groups - 2, groups - 1):
            sums(k, k % U)

    return dict(pool=pool, act=act, dve=dve, pe=pe)


def groups_far(nc, m, g, n, index, lane):
    groups, tiles, W = g.s, g.tp, g.wh + 1
    s = region(m.slots, [(f"rows{u}", tiles * g.row) for u in range(U)] + [(f"one_hot{o}", tiles * P) for o in range(2)]
               + [(f"one_hot_t{o}", tiles * P) for o in range(2)] + [(f"one_hot_b{o}", tiles * P // 2) for o in range(2)]
               + [("spread", tiles * H * P // 2)] + [(f"index{u}", tiles) for u in range(U)]
               + [("term", 2 * H), ("scale", H), ("gmax", H), ("z", tiles * H), ("weight", tiles * H)])
    rows = [s[f"rows{u}"].rearrange("p (t w) -> p t w", t=tiles) for u in range(U)]
    one_hot = [s[f"one_hot{o}"].rearrange("p (t n) -> p t n", t=tiles) for o in range(2)]
    one_hot_t = [s[f"one_hot_t{o}"].rearrange("p (t n) -> p t n", t=tiles) for o in range(2)]
    one_hot_b = [s[f"one_hot_b{o}"].bitcast(BF16).rearrange("p (t n) -> p t n", t=tiles) for o in range(2)]
    spread = s["spread"].bitcast(BF16).rearrange("p (t h e) -> p t h e", t=tiles, h=H)
    slot_index = [s[f"index{u}"].bitcast(I32) for u in range(U)]
    term, scale, gmax, z, weight = (s[n] for n in ("term", "scale", "gmax", "z", "weight"))
    z3, weight3 = z.rearrange("p (t h) -> p t h", h=H), weight.rearrange("p (t h) -> p t h", h=H)
    acc = m.acc[:, :].rearrange("p (b w) -> p b w", w=GNN.acc) if g is GNN else m.acc_f[:, :, :]
    ps_max = m.four[:, 0:tiles * H * P].rearrange("p (t h e) -> p h t e", t=tiles, h=H)
    ps_t, ps_e, ps_sum = m.ps[0], m.ps[1][:, 0:tiles * 2 * H].rearrange("p (t c) -> p t c", t=tiles), m.ps[2][:, 0:g.acc]

    indexed, gathered = n("indexed"), [n(f"gathered{u}") for u in range(U)]
    one_hot_ready, one_hot_b_ready, turned, one_hot_t_ready = (n(x) for x in (
        "one_hot_ready", "one_hot_b_ready", "turned", "one_hot_t_ready"))
    spread_ready, max_ready, term_ready, scale_ready, terms_at_edges = (n(x) for x in (
        "spread_ready", "max_ready", "term_ready", "scale_ready", "terms_at_edges"))
    e_ready, weight_ready, messages_ready, summed, dve_step = (n(x) for x in (
        "e_ready", "weight_ready", "messages_ready", "summed", "dve_step"))
    trips = groups // U

    def pool_program(pool):
        def gather(i, u, free):
            pool.wait_ge(indexed, i * U + u + 1)
            alone(pool)
            if free:
                pool.wait_ge(summed, i * U + u - U + 1)
                alone(pool)
            for t in range(tiles):
                pool.indirect_dma_start(out=rows[u][:, t, :], out_offset=None, in_=m.table[g],
                                        in_offset=bass.IndirectOffsetOnAxis(ap=slot_index[u][:, t:t + 1], axis=0)
                                        ).then_inc(gathered[u], 16)

        for u in range(U):
            gather(0, u, False)
        with pool.Fori(1, trips) as i:
            for u in range(U):
                gather(i, u, True)

    def act_program(act):
        def one_hots(k, o):
            act.wait_ge(one_hot_ready, k + 1)
            act.copy(one_hot_b[o], one_hot[o]).then_inc(one_hot_b_ready, 1)

        def turned_out(k, o):
            act.wait_ge(turned, k + 1)
            act.copy(one_hot_t[o], ps_t[:, 0:tiles * P].rearrange("p (t n) -> p t n", t=tiles)).then_inc(one_hot_t_ready, 1)

        def group(i, u, last=False):
            k, o = i * U + u, (u + 1) % 2
            act.wait_ge(term_ready, k + 1)
            act.activation(scale, scale, ACT.Exp).then_inc(scale_ready, 1)
            if not last:
                one_hots(k + 1, o)
            act.wait_ge(e_ready, k + 1)
            act.activation(weight, z, ACT.Exp).then_inc(weight_ready, 1)
            if not last:
                turned_out(k + 1, o)

        def indices(i, u):
            act.copy(slot_index[u], index[:, bass.ds((i * U + u) * tiles, tiles)]).then_inc(indexed, 1)

        for u in range(U):
            indices(0, u)
        act.wait_ge(n("decoded"), 2)
        one_hots(0, 0)
        turned_out(0, 0)
        with act.Fori(0, trips - 1) as i:
            for u in range(U):
                group(i, u)
                act.wait_ge(gathered[u], i * (16 * tiles) + 16 * tiles)
                alone(act)
                indices(i + 1, u)
        for u in range(U):
            group(trips - 1, u, last=u == U - 1)

    def dve_program(dve):
        step = Steps(dve, dve_step)
        if g is GNN:
            step(dve.memset(m.mtab[:, :, :], 0.0))
        else:
            own = m.acc_f[:, 0:NB, :].rearrange("p b (h w) -> p b h w", h=H)
            step(dve.memset(m.acc_f[:, :, :], 1.0))
            for h in range(H):
                step(dve.tensor_copy(own[:, :, h, 0:g.wh], m.h2[:, :, h * g.wh:(h + 1) * g.wh]))
            step(dve.memset(m.mtab[:, NB, :], 0.0))
            step(dve.tensor_copy(m.mtab[:, 0:NB, :], m.v[:, :, 0:H]))
        top = m.ttab[:, :, H:]
        step(dve.tensor_tensor(top, m.ttab[:, :, 0:H], m.mtab[:, :, :], ALU.add))
        step(dve.scalar_tensor_tensor(top, top, SLOPE, top, ALU.mult, ALU.max))

        def one_hots(k, o):
            lanes = lane[:, bass.ds(k * tiles, tiles)].unsqueeze(2).broadcast_to([P, tiles, P])
            dve.tensor_tensor(one_hot[o], m.iota_n[:, :].unsqueeze(1).broadcast_to([P, tiles, P]), lanes,
                              ALU.is_equal).then_inc(one_hot_ready, 1)

        def spreads(u, which, last):
            for t in which:
                for h in range(H):
                    ins = dve.tensor_scalar(spread[:, t, h, :], m.ident_b[:, :], rows[u][:, t, g.acc + h:g.acc + h + 1],
                                            None, ALU.mult)
            if last:
                ins.then_inc(spread_ready, 1)

        def group(i, u, last=False):
            nonlocal word
            k, o = i * U + u, (u + 1) % 2
            if u == 0:
                word = dve.value_load(m.blocks_of[g][0:1, bass.ds(i, 1)], min_val=0, max_val=BASE ** U - 1)
            b = bass.ds(word // BASE ** u % BASE, 1)
            old = m.ttab[:, b, H:].rearrange("p o h -> p (o h)")
            own = m.ttab[:, b, 0:H].rearrange("p o h -> p (o h)")
            best = m.mtab[:, b, :].rearrange("p o h -> p (o h)")
            dve.wait_ge(max_ready, k + 1)
            step(dve.tensor_reduce(gmax, ps_max, AX.XY, ALU.max))
            step(dve.tensor_tensor(best, best, gmax, ALU.max))
            step(dve.tensor_tensor(gmax, own, best, ALU.add))
            step(dve.scalar_tensor_tensor(term[:, H:], gmax, SLOPE, gmax, ALU.mult, ALU.max))
            step(dve.tensor_tensor(scale, old, term[:, H:], ALU.subtract))
            alone(dve)
            step(dve.tensor_copy(old, term[:, H:]))
            alone(dve)
            dve.tensor_copy(term[:, 0:H], own).then_inc(term_ready, 1)
            if not last:
                one_hots(k + 1, o)
            dve.wait_ge(terms_at_edges, k + 1)
            step(dve.tensor_tensor(z3, rows[u][:, :, g.acc:g.acc + H], ps_e[:, :, 0:H], ALU.add))
            step(dve.scalar_tensor_tensor(z, z, SLOPE, z, ALU.mult, ALU.max))
            dve.tensor_tensor(z3, z3, ps_e[:, :, H:], ALU.subtract).then_inc(e_ready, 1)
            if not last:
                v = (u + 1) % U
                dve.wait_ge(gathered[v], i * (16 * tiles) + 16 * tiles * (1 + (u + 1) // U))
                spreads(v, (0,), tiles == 1)
            dve.wait_ge(weight_ready, k + 1)
            msg = rows[u][:, :, 0:g.acc].rearrange("p t (h w) -> p t h w", h=H)
            for t in range(tiles):
                ins = dve.tensor_tensor(msg[:, t], msg[:, t], weight3[:, t, :].unsqueeze(2).broadcast_to([P, H, W]), ALU.mult)
            ins.then_inc(messages_ready, 1)
            if not last and tiles > 1:
                spreads(v, range(1, tiles), True)
            dve.wait_ge(scale_ready, k + 1)
            sums = acc[:, b, :].rearrange("p o (h w) -> p (o h) w", h=H)
            step(dve.tensor_tensor(sums, sums, scale.unsqueeze(2).broadcast_to([P, H, W]), ALU.mult))
            dve.wait_ge(summed, k + 1)
            step(dve.tensor_tensor(sums, sums, ps_sum.rearrange("p (h w) -> p h w", h=H), ALU.add))

        word = None
        one_hots(0, 0)
        dve.wait_ge(gathered[0], 16 * tiles)
        spreads(0, range(tiles), True)
        steps = U * 10
        with dve.Fori(0, trips - 1) as i:
            step.enter(i, steps)
            for u in range(U):
                group(i, u)
            step.leave(trips - 1)
        for u in range(U):
            group(trips - 1, u, last=u == U - 1)

    def pe_program(pe):
        def turn(k, o):
            pe.wait_ge(one_hot_ready, k + 1)
            for t in range(tiles):
                last = nc.tensor.transpose(ps_t[:, t * P:(t + 1) * P], one_hot[o][:, t, :], m.ident[:, :])
            last.then_inc(turned, 1)

        def maxima(k, o):
            pe.wait_ge(one_hot_b_ready, k + 1)
            pe.wait_ge(spread_ready, k + 1)
            for t in range(tiles):
                last = nc.tensor.matmul(m.four[:, t * H * P:(t + 1) * H * P], one_hot_b[o][:, t, :],
                                        spread[:, t].rearrange("p h e -> p (h e)"), start=True, stop=True)
            last.then_inc(max_ready, 1)

        def group(i, u, last_group=False):
            k, o = i * U + u, u % 2
            pe.wait_ge(term_ready, k + 1)
            pe.wait_ge(one_hot_t_ready, k + 1)
            for t in range(tiles):
                last = nc.tensor.matmul(ps_e[:, t, :], one_hot_t[o][:, t, :], term, start=True, stop=True)
            last.then_inc(terms_at_edges, 1)
            if not last_group:
                turn(k + 1, 1 - o)
            pe.wait_ge(messages_ready, k + 1)
            for t in range(tiles):
                last = nc.tensor.matmul(ps_sum, one_hot[o][:, t, :], rows[u][:, t, 0:g.acc], start=t == 0, stop=t == tiles - 1)
            last.then_inc(summed, 1)
            if not last_group:
                maxima(k + 1, 1 - o)

        turn(0, 0)
        maxima(0, 0)
        with pe.Fori(0, trips - 1) as i:
            for u in range(U):
                group(i, u)
        for u in range(U):
            group(trips - 1, u, last_group=u == U - 1)

    return dict(pool=pool_program, act=act_program, dve=dve_program, pe=pe_program)


def least_v(dve, m, ps, least, v_ready, step):
    ends, own = m.small[:, 0:2 * H], m.ttab[:, 0:NB, 0:H]
    gathered = m.att[:, :, H:].rearrange("p b h -> p h b")
    step(dve.tensor_reduce(ends[:, 0:H], gathered, AX.X, ALU.min))
    step(dve.tensor_reduce(ends[:, H:], gathered, AX.X, ALU.max))
    dve.tensor_scalar(ends[:, H:], ends[:, H:], -1.0, None, ALU.mult).then_inc(least[0], 1)
    dve.wait_ge(least[1], 1)
    step(dve.tensor_reduce(m.small[0:2 * H, 8:9], ps[0:2 * H, 128:256], AX.X, ALU.min))
    dve.tensor_scalar(m.small[0:2 * H, 16:16 + 2 * H], m.ident[0:2 * H, 0:2 * H], m.small[0:2 * H, 8:9], None,
                      ALU.mult).then_inc(least[2], 1)
    dve.wait_ge(least[3], 1)
    step(dve.tensor_copy(m.low[:, :], ps[:, 256:256 + 2 * H]))
    low = m.low[:, 0:H].unsqueeze(1).broadcast_to([P, NB, H])
    step(dve.tensor_tensor(m.v[:, :, 0:H], m.att[:, :, H:], low, ALU.subtract))
    dve.tensor_scalar(m.v[:, :, H:], m.v[:, :, 0:H], SLOPE, None, ALU.mult).then_inc(v_ready, 1)
    step(dve.memset(m.ttab[:, :, :], 0.0))
    step(dve.tensor_tensor(own, m.att[:, :, 0:H], low, ALU.add))
    spread = m.small[:, 24:24 + H]
    step(dve.tensor_tensor(spread, m.low[:, 0:H], m.low[:, H:], ALU.add))
    step(dve.tensor_scalar(spread, spread, -1.0, None, ALU.mult))
    step(dve.tensor_reduce(m.small[:, 28:29], spread, AX.X, ALU.max))
    step(dve.tensor_scalar(m.near[:, :], m.small[0:1, 28:29], SPREAD, None, ALU.is_le))
    top, both, rest = m.mtab[:, 0:NB, :], m.both[:, :, :], m.att[:, :, :]
    step(dve.tensor_tensor(top, own, spread.unsqueeze(1).broadcast_to([P, NB, H]), ALU.add))
    step(dve.scalar_tensor_tensor(top, top, SLOPE, top, ALU.mult, ALU.max))
    step(dve.tensor_tensor(both[:, :, 0:H], own, top, ALU.subtract))
    step(dve.scalar_tensor_tensor(both[:, :, H:], own, SLOPE, top, ALU.mult, ALU.subtract))
    step(dve.memset(m.terms[:, :, :, :], 0.0))
    step(dve.tensor_copy(m.terms[:, 0:NB, 0, :], both))
    step(dve.tensor_tensor(rest, both, m.terms[:, 0:NB, 0, :], ALU.subtract))
    step(dve.tensor_copy(m.terms[:, 0:NB, 1, :], rest))
    step(dve.tensor_tensor(m.terms[:, 0:NB, 2, :], rest, m.terms[:, 0:NB, 1, :], ALU.subtract))
    dve.wait_ge(v_ready, 1)


def least_v_products(nc, pe, m, ps, least):
    pe.wait_ge(least[0], 1)
    nc.tensor.transpose(ps[0:2 * H, 128:256], m.small[:, 0:2 * H], m.ident[:, :]).then_inc(least[1], 1)
    pe.wait_ge(least[2], 1)
    nc.tensor.matmul(ps[:, 256:256 + 2 * H], m.ones[0:2 * H, :], m.small[0:2 * H, 16:16 + 2 * H], start=True,
                     stop=True).then_inc(least[3], 1)


def combine_and_experts(nc, m, io, sem):
    ST = 4
    FC = F // P
    w = region(m.weights, [("w1", NE * 2 * F), ("w2", NE * FC * D), ("table", NB * FFN.row)])
    prod = m.acc_f[:, :, :].rearrange("p b w -> p (b w)")[:, 0:NB * H * NE]
    s = region(m.slots, [(f"{n}{o}", D) for n in ("phi", "mixed", "near") for o in range(2)]
               + [(f"norm{o}", 2 * H) for o in range(2)]
               + [("mixed_t", D), ("x2n", D), ("x2t", D), ("den", H), ("mean", 1), ("var", 1), ("room", 1),
                  ("rstd", 1), ("wo", 2 * D), ("bo", D), ("w_gat", 2 * H * NE), ("att", 2 * H * NE), ("stage", 4 * FFN.run),
                  ("b1", NE * FC), ("b2", NE * D)]
               + [(f"hidden{o}", FC * ST * P) for o in range(2)] + [(f"y{o}", ST * D) for o in range(2)])
    wo, w_gat = s["wo"].rearrange("p (k n) -> p k n", k=2), s["w_gat"].rearrange("p (k n) -> p k n", k=2)
    acc = m.acc[:, :].rearrange("p (b w) -> p b w", w=GNN.acc)
    wide = m.wide[:, :].rearrange("p (b d) -> p b d", d=D)
    turned = m.wide[:, :].rearrange("p (b k n) -> p b k n", k=2, n=P)
    phi, mixed, near, norm = ([s[f"{n}{o}"] for o in range(2)] for n in ("phi", "mixed", "near", "norm"))
    table = w["table"].rearrange("p (b w) -> p b w", b=NB)
    stage = s["stage"].bitcast(I32).rearrange("p (k c) -> p k c", k=2)
    w1 = w["w1"].rearrange("p (e k f) -> p e k f", e=NE, k=2)
    w2 = w["w2"].rearrange("p (e c d) -> p e c d", e=NE, c=FC)
    hidden = [s[f"hidden{o}"].rearrange("p (c n) -> p c n", c=FC) for o in range(2)]
    y = [s[f"y{o}"].rearrange("p (t d) -> p t d", t=ST) for o in range(2)]
    bank = [m.four[:, i * 512:(i + 1) * 512] for i in range(4)] + [m.ps[i][:, :] for i in range(4)]
    ps_o = [bank[i][:, 0:2 * (P + H)].rearrange("p (j w) -> p j w", j=2) for i in range(2)]
    ps_t, ps_r, ps_x, ps_h, ps_s = bank[2][:, 0:D], [bank[4][:, 0:D], bank[5][:, 0:D]], bank[3][:, 0:D], bank[6][:, 0:H * NE], bank[7]
    ps_y = [bank[4 + i][:, 0:D] for i in range(4)]

    weights_in, phi_in, kv_ready, experts_in = sem("c_weights_in"), [sem("phi_in0"), sem("phi_in1")], sem("kv_ready"), sem("experts_in")
    queried, mixed_ready, mixed_turned, mixed_t_ready, mix_ready = (sem("c_" + x) for x in (
        "queried", "mixed_ready", "mixed_turned", "mixed_t_ready", "mix_ready"))
    var_ready, std_ready, x2n_ready, x2n_turned, x2t_ready, h_ready, h_read = (sem("c_" + x) for x in (
        "var_ready", "std_ready", "x2n_ready", "x2n_turned", "x2t_ready", "h_ready", "h_read"))
    least, v_ready, table_saved, dve_step, table_ready = [sem(f"ffn_least{i}") for i in range(4)], sem("ffn_v_ready"), sem(
        "table_saved"), sem("c_step"), sem("c_table_ready")
    staged, scattered = [sem(f"ffn_staged{i}") for i in range(2)], [sem(f"ffn_scattered{i}") for i in range(2)]
    made, gelu_done, y_ready, y_read = (sem("e_" + x) for x in ("made", "gelu_done", "y_ready", "y_read"))
    y_saved = [sem(f"e_y_saved{o}") for o in range(2)]
    trips = NB // ST
    assert trips * ST == NB - 1 and NB % 2

    def tiles(eng, first, tile):
        if first:
            tile(1, 1)
        with eng.Fori(first, NB // 2) as i:
            for o in range(2):
                tile(i * 2 + o, o)
        tile(NB - 1, 0)

    def stretches(eng, stretch):
        stretch(0, ST)
        with eng.Fori(1, trips) as j:
            stretch(j, ST)
        stretch(trips, 1)

    def rows_before(j, nt, e):
        return j * (NE * ST) + e * nt

    with nc.Block() as block:
        @block.sync
        def _(sp):
            def load_weights():
                sp.dma_start(wo, io["wo"].rearrange("(k p) n -> p k n", p=P)).then_inc(weights_in, 16)
                sp.dma_start(s["bo"], bcast(io["bo"], P)).then_inc(weights_in, 16)
                sp.dma_start(w_gat, io["W_gat"].rearrange("(k p) n -> p k n", p=P)).then_inc(weights_in, 16)
                for i, n in enumerate(("att_dst", "att_src")):
                    c = slice(i * H * NE, (i + 1) * H * NE)
                    sp.dma_start(s["att"][:, c], bcast(io[n].rearrange("h d -> (h d)"), P)).then_inc(weights_in, 16)
                for e in range(NE):
                    sp.dma_start(w1[:, e], io["W1"][e].rearrange("(k p) f -> p k f", p=P)).then_inc(experts_in, 16)
                    sp.dma_start(w2[:, e], io["W2"][e].rearrange("(c p) d -> p c d", p=P)).then_inc(experts_in, 16)
                sp.dma_start(s["b2"], bcast(io["b2"].rearrange("e d -> (e d)"), P)).then_inc(experts_in, 16)
                sp.dma_start(s["b1"], io["b1"]).then_inc(experts_in, 16)

            stage_edges(sp, FFN, m.places[:, 0, :], m.places[:, 1, :], stage, staged, scattered,
                        [(0, None), (1, load_weights)])
            sp.wait_ge(table_ready, 1)
            sp.dma_start(m.table[FFN].rearrange("(b p) w -> p b w", p=P), table).then_inc(table_saved, 16)
            sp.wait_ge(table_saved, 16)

        @block.gpsimd
        def _(pool):
            scatter_edges(pool, m, FFN, stage, staged, scattered)

        @block.scalar
        def _(act):
            def load_phi(i, o):
                act.dma_start(phi[o], m.phi_q[bass.ds(i * P, P), :]).then_inc(phi_in[o], 16)

            def front(i, o):
                act.wait_ge(mixed_turned, i + 1)
                act.copy(s["mixed_t"], ps_t).then_inc(mixed_t_ready, 1)

            def tile(i, o, ahead=2):
                if ahead:
                    front(i + 1, 1 - o)
                if ahead > 1:
                    load_phi(i + 2, o)
                act.wait_ge(var_ready, i + 1)
                act.activation(s["rstd"], s["var"], ACT.Sqrt).then_inc(std_ready, 1)
                act.wait_ge(x2n_turned, i + 1)
                act.copy(s["x2t"], ps_x).then_inc(x2t_ready, 1)
                act.wait_ge(x2t_ready, i + 1)
                alone(act)
                act.copy(wide[:, bass.ds(i, 1), :].rearrange("p o d -> p (o d)"), s["x2t"])
                act.wait_ge(h_ready, i + 1)
                alone(act)
                act.copy(m.h2[:, bass.ds(i, 1), :].rearrange("p o d -> p (o d)"), ps_h).then_inc(h_read, 1)

            load_phi(0, 0)
            load_phi(1, 1)
            front(0, 0)
            with act.Fori(0, NB // 2 - 1) as i:
                for o in range(2):
                    tile(i * 2 + o, o)
            tile(NB - 3, 0)
            tile(NB - 2, 1, ahead=1)
            tile(NB - 1, 0, ahead=0)

            act.sem_inc(gelu_done, FC)
            act.wait_ge(experts_in, 16 * 10)

            def stretch(j, nt):
                for e in range(NE):
                    at = j * NE + e
                    if not isinstance(j, int) or at >= 2:
                        act.wait_ge(y_read, rows_before(j, nt, e) - (nt if e else ST))
                    for c in range(FC):
                        act.wait_ge(made, at * FC + c + 1)
                        act.activation(hidden[e % 2][:, c, 0:nt * P], bank[c][:, 0:nt * P], ACT.Gelu,
                                       bias=s["b1"][:, e * FC + c:e * FC + c + 1]).then_inc(gelu_done, 1)
                    if e:
                        save(j, nt, e - 1)
                save(j, nt, NE - 1)

            def save(j, nt, e):
                act.wait_ge(y_read, rows_before(j, nt, e) + nt)
                act.dma_start(m.y[bass.ds(j * (ST * P), nt * P), e * D:(e + 1) * D].rearrange("(t p) d -> p t d", p=P),
                              y[e % 2][:, 0:nt, :]).then_inc(y_saved[e % 2], 16)

            stretches(act, stretch)
            for o in range(2):
                act.wait_ge(y_saved[o], 16 * (NE // 2) * (trips + 1))

        @block.vector
        def _(dve):
            step = Steps(dve, dve_step)
            for j in range(2):
                step(dve.tensor_tensor(m.kvm[:, j, 0:P], m.kv[:, j, 0:P], m.head_mask[:, :], ALU.mult))
                step(dve.tensor_scalar(m.kvm[:, j, P:], m.head_of[:, :], m.kv[:, j, P:], None, ALU.mult))
            dve.sem_inc(kv_ready, 1)
            dve.wait_ge(weights_in, 16 * 5)

            def front(i, o):
                b = bass.ds(i, 1)
                sums = acc[:, b, :].rearrange("p o (h w) -> p (o h) w", h=H)
                near4, n3 = near[o].rearrange("p (h d) -> p h d", h=H), norm[o].rearrange("p (j h) -> p j h", j=2)
                step(dve.tensor_scalar(s["den"], sums[:, :, DH], 1e-30, None, ALU.max))
                step(dve.reciprocal(s["den"], s["den"]))
                step(dve.tensor_tensor(near4, sums[:, :, 0:DH], s["den"].unsqueeze(2).broadcast_to([P, H, DH]), ALU.mult))
                dve.tensor_tensor(near[o], near[o], wide[:, b, :].rearrange("p o d -> p (o d)"), ALU.add)
                dve.wait_ge(queried, i + 1)
                step(dve.tensor_scalar(n3, ps_o[o][:, :, P:], 1e-6, None, ALU.add))
                step(dve.reciprocal(norm[o], norm[o]))
                for j in range(2):
                    ins = dve.tensor_tensor(mixed[o][:, j * P:(j + 1) * P].rearrange("p (h d) -> p h d", d=MD),
                                            ps_o[o][:, j, 0:P].rearrange("p (h d) -> p h d", d=MD),
                                            n3[:, j, :].unsqueeze(2).broadcast_to([P, H, MD]), ALU.mult)
                ins.then_inc(mixed_ready, 1)
                step(dve.tensor_tensor(near[o], near[o], s["bo"], ALU.add))

            def back(i, o):
                x2 = acc[:, bass.ds(i, 1), 0:D].rearrange("p o d -> p (o d)")
                dve.wait_ge(mix_ready, i + 1)
                step(dve.tensor_tensor(x2, near[o], ps_r[o], ALU.add))
                alone(dve)
                step(dve.bn_stats(m.bn[:, :], x2))
                mean_var(dve, step, m.bn[:, :].unsqueeze(1), s["mean"], s["var"], s["room"]).then_inc(var_ready, 1)
                dve.wait_ge(std_ready, i + 1)
                step(dve.reciprocal(s["rstd"], s["rstd"]))
                dve.tensor_scalar(s["x2n"], x2, s["mean"], s["rstd"], ALU.subtract, ALU.mult).then_inc(x2n_ready, 1)

            front(0, 0)
            with dve.Fori(0, NB // 2) as i:
                step.enter(i, 2 * (6 + 5))
                for o in range(2):
                    front(i * 2 + o + 1, 1 - o)
                    back(i * 2 + o, o)
                step.leave(NB // 2)
            back(NB - 1, 0)
            dve.wait_ge(h_read, NB)
            h2 = m.h2[:, :, :].rearrange("p b (h e) -> p b h e", h=H)
            for j in range(2):
                a = s["att"][:, j * H * NE:(j + 1) * H * NE].unsqueeze(1).broadcast_to([P, NB, H * NE])
                step(dve.tensor_tensor(prod.rearrange("p (b c) -> p b c", b=NB), m.h2[:, :, :], a, ALU.mult))
                step(dve.tensor_reduce(m.att[:, :, j * H:(j + 1) * H], prod.rearrange("p (b h e) -> p b h e", b=NB, h=H),
                                       AX.X, ALU.add))
            least_v(dve, m, ps_s, least, v_ready, step)
            step(dve.memset(w["table"], 1.0))
            for h in range(H):
                step(dve.tensor_copy(table[:, :, h * (FFN.wh + 1):h * (FFN.wh + 1) + FFN.wh], h2[:, :, h, :]))
            dve.tensor_copy(table[:, :, FFN.acc:], m.v[:, :, :]).then_inc(table_ready, 1)

            dve.wait_ge(experts_in, 16 * 10)

            def stretch(j, nt):
                for e in range(NE):
                    if not isinstance(j, int) or j * NE + e >= 2:
                        dve.wait_ge(y_saved[e % 2], (j * (NE // 2) + e // 2) * 16)
                    for t in range(nt):
                        dve.wait_ge(y_ready, rows_before(j, nt, e) + t + 1)
                        dve.tensor_tensor(y[e % 2][:, t, :], ps_y[t], s["b2"][:, e * D:(e + 1) * D], ALU.add).then_inc(y_read, 1)

            stretches(dve, stretch)

        @block.tensor
        def _(pe):
            pe.wait_ge(kv_ready, 1)
            pe.wait_ge(weights_in, 16 * 5)

            def front(i, o, loads):
                pe.wait_ge(phi_in[o], loads * 16)
                for j in range(2):
                    last = nc.tensor.matmul(ps_o[o][:, j, :], phi[o][:, j * P:(j + 1) * P], m.kvm[:, j, :], start=True, stop=True)
                last.then_inc(queried, 1)
                pe.wait_ge(mixed_ready, i + 1)
                for k in range(2):
                    last = nc.tensor.transpose(ps_t[:, k * P:(k + 1) * P], mixed[o][:, k * P:(k + 1) * P], m.ident[:, :])
                last.then_inc(mixed_turned, 1)
                pe.wait_ge(mixed_t_ready, i + 1)
                for k in range(2):
                    last = nc.tensor.matmul(ps_r[o], s["mixed_t"][:, k * P:(k + 1) * P], wo[:, k, :], start=k == 0, stop=k == 1)
                last.then_inc(mix_ready, 1)

            def back(i):
                pe.wait_ge(x2n_ready, i + 1)
                for k in range(2):
                    last = nc.tensor.transpose(ps_x[:, k * P:(k + 1) * P], s["x2n"][:, k * P:(k + 1) * P], m.ident[:, :])
                last.then_inc(x2n_turned, 1)
                pe.wait_ge(x2t_ready, i + 1)
                for k in range(2):
                    last = nc.tensor.matmul(ps_h, s["x2t"][:, k * P:(k + 1) * P], w_gat[:, k, :], start=k == 0, stop=k == 1)
                last.then_inc(h_ready, 1)

            front(0, 0, 1)
            with pe.Fori(0, NB // 2) as i:
                front(i * 2 + 1, 1, i + 1)
                back(i * 2)
                front(i * 2 + 2, 0, i + 2)
                back(i * 2 + 1)
            back(NB - 1)
            least_v_products(nc, pe, m, ps_s, least)

            pe.wait_ge(experts_in, 16 * 10)
            pe.wait_ge(v_ready, 1)

            def stretch(j, nt):
                def make(e):
                    for c in range(FC):
                        pe.wait_ge(gelu_done, (j * NE + e) * FC + c + 1)
                        for k in range(2):
                            last = nc.tensor.matmul(bank[c][:, 0:nt * P], w1[:, e, k, c * P:(c + 1) * P],
                                                    turned[:, bass.ds(j * ST, nt), k, :], start=k == 0, stop=k == 1)
                        last.then_inc(made, 1)

                def contract(e):
                    at = j * NE + e
                    pe.wait_ge(gelu_done, at * FC + 2 * FC)
                    for t in range(nt):
                        if not isinstance(j, int) or at:
                            pe.wait_ge(y_read, rows_before(j, nt, e) - (ST - 1 - t if nt == ST else 0))
                        for c in range(FC):
                            last = nc.tensor.matmul(ps_y[t], hidden[e % 2][:, c, t * P:(t + 1) * P], w2[:, e, c, :],
                                                    start=c == 0, stop=c == FC - 1)
                        last.then_inc(y_ready, 1)

                make(0)
                for e in range(1, NE):
                    make(e)
                    contract(e - 1)
                contract(NE - 1)

            stretches(pe, stretch)


def gate(nc, m, io, out, sem):
    K, FEW, SLOTS = H * NE, 4, 3
    trips = NB // FEW // SLOTS
    assert trips * SLOTS * FEW == NB - 1
    rows = [m.wide[:, o * FEW * NE * D:(o + 1) * FEW * NE * D].rearrange("p (t e d) -> p t e d", t=FEW, e=NE)
            for o in range(SLOTS)]
    acc = m.acc[:, :].rearrange("p (b w) -> p b w", w=GNN.acc)
    s = region(m.slots, [("agg", NB * K), ("sq", NB * K), ("den", NB * H), ("mean", NB), ("rstd", NB), ("scores", NB * NE),
                         ("beaten", NB * NE), ("one", NB), ("top", NB), ("e", NB * NE), ("b_gat", K), ("gamma", K), ("beta", K)])
    agg4 = s["agg"].rearrange("p (b h e) -> p b h e", b=NB, h=H)
    agg, sq = (s[n].rearrange("p (b k) -> p b k", b=NB) for n in ("agg", "sq"))
    scores, beaten, e = (s[n].rearrange("p (b e) -> p b e", b=NB) for n in ("scores", "beaten", "e"))
    params_in, var_ready, std_ready, dve_step = (sem("s_" + x) for x in ("params_in", "var_ready", "std_ready", "step"))
    gap_ready, exp_ready = sem("s_gap_ready"), sem("s_exp_ready")
    rows_in, added, gated = [sem(f"s_rows_in{o}") for o in range(SLOTS)], sem("s_added"), sem("s_gated")
    saved = sem("s_saved")

    def wide(ap):
        return ap.unsqueeze(1).broadcast_to([P, NB, K])

    def each(ap, n):
        return ap.unsqueeze(2).broadcast_to([P, NB, n])

    with nc.Block() as block:
        @block.sync
        def _(sp):
            for n, k in (("b_gat", "b_gat"), ("gamma", "ln_gamma"), ("beta", "ln_beta")):
                sp.dma_start(s[n], bcast(io[k], P)).then_inc(params_in, 16)

            def load(i, o):
                sp.dma_start(rows[o].rearrange("p t e d -> p t (e d)"),
                             m.y[bass.ds((i * SLOTS + o) * (FEW * P), FEW * P), :].rearrange("(t p) w -> p t w", p=P)
                             ).then_inc(rows_in[o], 16)

            for o in range(SLOTS):
                load(0, o)
            with sp.Fori(1, trips) as i:
                for o in range(SLOTS):
                    sp.wait_ge(gated, ((i - 1) * SLOTS + o + 1))
                    load(i, o)
            sp.wait_ge(gated, (trips - 1) * SLOTS + 1)
            sp.dma_start(rows[0][:, 0].rearrange("p e d -> p (e d)"), m.y[(NB - 1) * P:NB * P, :]).then_inc(rows_in[0], 16)

        @block.scalar
        def _(act):
            act.wait_ge(var_ready, 1)
            act.activation(s["rstd"], s["rstd"], ACT.Sqrt).then_inc(std_ready, 1)
            act.wait_ge(gap_ready, 1)
            act.activation(s["e"], s["e"], ACT.Exp).then_inc(exp_ready, 1)
            with act.Fori(0, NB // FEW) as i:
                act.wait_ge(gated, i + 1)
                act.dma_start(out[bass.ds(i * (FEW * P), FEW * P), :].rearrange("(t p) d -> p t d", p=P),
                              acc[:, bass.ds(i * FEW, FEW), 0:D]).then_inc(saved, 16)
            act.wait_ge(gated, NB // FEW + 1)
            act.dma_start(out[(NB - 1) * P:N, :], acc[0:LAST, NB - 1, 0:D]).then_inc(saved, 16)
            act.wait_ge(saved, 16 * (NB // FEW + 1))

        @block.vector
        def _(dve):
            step = Steps(dve, dve_step)
            sums = m.acc_f[:, 0:NB, :].rearrange("p b (h w) -> p b h w", h=H)
            den = s["den"].rearrange("p (b h) -> p b h", b=NB)
            step(dve.tensor_scalar(den, sums[:, :, :, FFN.wh], 1e-16, None, ALU.add))
            step(dve.reciprocal(s["den"], s["den"]))
            for h in range(H):
                step(dve.tensor_tensor(agg4[:, :, h, :], sums[:, :, h, 0:FFN.wh], each(den[:, :, h], NE), ALU.mult))
            dve.wait_ge(params_in, 48)
            step(dve.tensor_tensor(agg, agg, wide(s["b_gat"]), ALU.add))
            step(dve.tensor_reduce(s["mean"], agg, AX.X, ALU.add))
            step(dve.tensor_scalar(s["mean"], s["mean"], 1.0 / K, None, ALU.mult))
            step(dve.tensor_tensor(agg, agg, each(s["mean"], K), ALU.subtract))
            step(dve.tensor_tensor(sq, agg, agg, ALU.mult))
            step(dve.tensor_reduce(s["rstd"], sq, AX.X, ALU.add))
            dve.tensor_scalar(s["rstd"], s["rstd"], 1.0 / K, EPS, ALU.mult, ALU.add).then_inc(var_ready, 1)
            dve.wait_ge(std_ready, 1)
            step(dve.reciprocal(s["rstd"], s["rstd"]))
            step(dve.tensor_tensor(agg, agg, each(s["rstd"], K), ALU.mult))
            step(dve.tensor_tensor(agg, agg, wide(s["gamma"]), ALU.mult))
            step(dve.tensor_tensor(agg, agg, wide(s["beta"]), ALU.add))
            step(dve.tensor_reduce(scores, s["agg"].rearrange("p (b h e) -> p b e h", b=NB, h=H), AX.X, ALU.add))
            step(dve.tensor_scalar(s["scores"], s["scores"], 1.0 / H, None, ALU.mult))
            step(dve.memset(s["beaten"], 0.0))
            for a in range(NE):
                for b in range(NE):
                    if a != b:
                        step(dve.tensor_tensor(s["one"], scores[:, :, b], scores[:, :, a], ALU.is_ge if b < a else ALU.is_gt))
                        step(dve.tensor_tensor(beaten[:, :, a], beaten[:, :, a], s["one"], ALU.add))
            step(dve.tensor_reduce(s["top"], scores, AX.X, ALU.max))
            dve.tensor_tensor(e, scores, each(s["top"], NE), ALU.subtract).then_inc(gap_ready, 1)
            step(dve.tensor_scalar(s["beaten"], s["beaten"], 2.0, None, ALU.is_lt))
            dve.wait_ge(exp_ready, 1)
            step(dve.tensor_tensor(s["e"], s["e"], s["beaten"], ALU.mult))
            step(dve.tensor_reduce(s["one"], e, AX.X, ALU.add))
            step(dve.reciprocal(s["one"], s["one"]))
            step(dve.tensor_tensor(m.gates[:, :, :], e, each(s["one"], NE), ALU.mult))

            gates = m.gates[:, :, :].rearrange("p b e -> p (b e)")

            def few(k, o, arrivals, nt):
                dve.wait_ge(rows_in[o], arrivals * 16)
                for e in range(NE):
                    for t in range(nt):
                        if e:
                            dve.wait_ge(added, k * (NE - 1) * FEW + (e - 1) * nt + t + 1)
                        x2 = acc[:, bass.ds(k * FEW + t, 1), 0:D].rearrange("p o d -> p (o d)")
                        ins = dve.scalar_tensor_tensor(x2, rows[o][:, t, e, :], gates[:, bass.ds((k * FEW + t) * NE + e, 1)],
                                                       x2, ALU.mult, ALU.add)
                        if e < NE - 1:
                            ins.then_inc(added, 1)
                ins.then_inc(gated, 1)

            with dve.Fori(0, trips) as i:
                for o in range(SLOTS):
                    few(i * SLOTS + o, o, i + 1, FEW)
            few(NB // FEW, 0, trips + 1, 1)


_INS = [("x", "x"), ("src", "src"), ("dst", "dst"), ("L0_gnn_W", "W_t"), ("L0_gnn_b", "b"), ("L0_gnn_a_src", "a_src"),
        ("L0_gnn_a_dst", "a_dst"), ("L0_mix_wq", "wq"), ("L0_mix_bq", "bq"), ("L0_mix_wk", "wk"), ("L0_mix_bk", "bk"),
        ("L0_mix_wv", "wv"), ("L0_mix_bv", "bv"), ("L0_mix_wo", "wo"), ("L0_mix_bo", "bo"), ("L0_ffn_W_gat", "W_gat"),
        ("L0_ffn_att_src", "att_src"), ("L0_ffn_att_dst", "att_dst"), ("L0_ffn_b_gat", "b_gat"),
        ("L0_ffn_ln_gamma", "ln_gamma"), ("L0_ffn_ln_beta", "ln_beta"), ("L0_ffn_W1", "W1"), ("L0_ffn_b1", "b1"),
        ("L0_ffn_W2", "W2"), ("L0_ffn_b2", "b2"), ("L0_ffn_edge_index", "edge_index")]


def laid_out(inputs):
    import numpy as np
    got = {}
    for name, short in _INS:
        a = np.ascontiguousarray(inputs[name])
        if short == "W_t":
            a = np.ascontiguousarray(a.T)
        if short == "bq":
            a = np.ascontiguousarray(a.reshape(2, P).T).reshape(-1)
        if short == "b1":
            a = np.ascontiguousarray(a.reshape(NE * F // P, P).T)
        got[short] = a
    return got


def kernel(**inputs):
    import concourse.bacc as _bacc
    from concourse.bass_utils import run_bass_kernel_spmd as _run

    nc = _bacc.Bacc("TRN2", target_bir_lowering=False, num_devices=1)
    arrays, io = {}, {}
    for short, a in laid_out(inputs).items():
        arrays[f"in_{short}"] = a
        io[short] = nc.dram_tensor(f"in_{short}", a.shape, mybir.dt.from_np(a.dtype), kind="ExternalInput").ap()
    out = nc.dram_tensor("out", (N, D), F32, kind="ExternalOutput").ap()
    build(nc, io, out)
    r = _run(nc, [arrays], core_ids=[0])
    return r.results[0]["out"]
```
